# Optimizing a Trainium2 kernel written in Bass

```python
import numpy as np
import jax
import jax.numpy as jnp

def _softmax(x, axis=-1):
    return jax.nn.softmax(x, axis=axis)

def _gelu(x):
    return jax.nn.gelu(x, approximate=True)

def _silu(x):
    return jax.nn.silu(x)

def _sigmoid(x):
    return jax.nn.sigmoid(x)

def _layernorm(x, axis=-1, eps=1e-05):
    m = jnp.mean(x, axis=axis, keepdims=True)
    v = jnp.var(x, axis=axis, keepdims=True)
    return (x - m) / jnp.sqrt(v + eps)

def _scatter_add(tgt, idx, src, axis=0):
    return tgt.at[idx].add(src)

def _segment_sum(src, seg, n):
    return jax.ops.segment_sum(src, seg, n)
kernel_name = 'mk_gnn_ffn_d1_gnn_r8_4cca5f'

def setup_inputs(seed: int=0):
    np.random.seed(seed)
    _w = jnp.asarray

    def _rec_inputs():
        import jax
        import jax.numpy as jnp
        _gk = jax.random.key(seed)
        x = -0.0002117 + 1 * jax.random.normal(jax.random.fold_in(_gk, 1), (6250, 256), jnp.float32)
        src = jax.random.randint(jax.random.fold_in(_gk, 2), (100000,), 0, 6250, jnp.int32)
        dst = jax.random.randint(jax.random.fold_in(_gk, 3), (100000,), 0, 6250, jnp.int32)
        _o = jnp.argsort(dst, stable=True)
        src = src[_o]
        dst = dst[_o]
        edge_weight = jax.random.uniform(jax.random.fold_in(_gk, 12), (100000,), jnp.float32, 0.0, 1)
        return (x, src, dst, edge_weight)
    x, src, dst, edge_weight = _rec_inputs()

    def _L0_gnn_setup():
        import jax, jax.numpy as jnp
        import numpy as np
        BN_EPS = 1e-05
        IDX = np.array([[0, 1, 2, 3, 4, 5, 6, 7], [1, 0, 3, 2, 5, 4, 7, 6], [2, 3, 0, 1, 6, 7, 4, 5], [3, 2, 1, 0, 7, 6, 5, 4], [4, 5, 6, 7, 0, 1, 2, 3], [5, 4, 7, 6, 1, 0, 3, 2], [6, 7, 4, 5, 2, 3, 0, 1], [7, 6, 5, 4, 3, 2, 1, 0]], dtype=np.int32)
        SIGN = np.array([[1, 1, 1, 1, 1, 1, 1, 1], [1, -1, 1, -1, 1, -1, -1, 1], [1, -1, -1, 1, 1, 1, -1, -1], [1, 1, -1, -1, 1, -1, 1, -1], [1, -1, -1, -1, -1, 1, 1, 1], [1, 1, -1, 1, -1, -1, -1, 1], [1, 1, 1, -1, -1, 1, -1, -1], [1, -1, 1, 1, -1, -1, 1, -1]], dtype=np.float32)

        def make_octonion_mul(kernel):
            in8, out = kernel.shape
            out8 = out // 8
            a = kernel.reshape(in8, 8, out8).transpose(1, 0, 2)
            blocks = jnp.asarray(SIGN)[:, :, None, None] * a[jnp.asarray(IDX)]
            return jnp.transpose(blocks, (1, 2, 0, 3)).reshape(8 * in8, out)
        key = jax.random.key(seed)
        ks = jax.random.split(key, 5)
        N, E, D_IN, D_OUT = (12500, 400000, 256, 256)
        stdv = float(np.sqrt(6.0 / (D_IN // 8 + D_OUT)))
        return {'x': jax.random.normal(ks[0], (N, D_IN), dtype=jnp.float32), 'weight': jax.random.uniform(ks[1], (D_IN // 8, D_OUT), dtype=jnp.float32, minval=-stdv, maxval=stdv), 'gamma': jnp.ones((D_OUT,), dtype=jnp.float32), 'beta': jnp.zeros((D_OUT,), dtype=jnp.float32), 'edge_weight': jax.random.uniform(ks[2], (E,), dtype=jnp.float32), 'edge_src': jax.random.randint(ks[3], (E,), 0, N, dtype=jnp.int32), 'edge_dst': jax.random.randint(ks[4], (E,), 0, N, dtype=jnp.int32)}
    _L0_gnn_all = _L0_gnn_setup()
    _L0_gnn_in = {k: v for k, v in _L0_gnn_all.items() if k in ('weight', 'gamma', 'beta')}
    del _L0_gnn_all

    def _L0_ffn_setup():
        import jax, jax.numpy as jnp
        import numpy as np
        B, N, D = (16, 512, 256)
        NUM_EXPERTS, TOP_K, HEADS = (4, 2, 4)
        N_EDGES = 131072
        LN_EPS = 1e-05

        def _layernorm(x, g, b):
            mu = x.mean(-1, keepdims=True)
            var = ((x - mu) ** 2).mean(-1, keepdims=True)
            return (x - mu) * jax.lax.rsqrt(var + LN_EPS) * g + b

        def _forward(x, edge_index, W_gat, att_src, att_dst, b_gat, ln_gamma, ln_beta, W1, b1, W2, b2):
            Bc, Nc, Dc = x.shape
            M = Bc * Nc
            x_flat = x.reshape(M, Dc)
            h = (x_flat @ W_gat).reshape(M, HEADS, NUM_EXPERTS)
            loops = jnp.arange(M, dtype=edge_index.dtype)
            src = jnp.concatenate([edge_index[0], loops])
            dst = jnp.concatenate([edge_index[1], loops])
            a_src = (h * att_src).sum(-1)
            a_dst = (h * att_dst).sum(-1)
            e = jax.nn.leaky_relu(a_src[src] + a_dst[dst], negative_slope=0.2)
            e_max = jax.ops.segment_max(e, dst, num_segments=M)
            ee = jnp.exp(e - e_max[dst])
            denom = jax.ops.segment_sum(ee, dst, num_segments=M)
            alpha = ee / (denom[dst] + 1e-16)
            msg = h[src] * alpha[:, :, None]
            agg = jax.ops.segment_sum(msg, dst, num_segments=M).reshape(M, HEADS * NUM_EXPERTS) + b_gat
            scores = _layernorm(agg, ln_gamma, ln_beta).reshape(M, HEADS, NUM_EXPERTS).mean(1)
            scores = scores.reshape(Bc, Nc, NUM_EXPERTS)
            topk_s, topk_i = jax.lax.top_k(scores, TOP_K)
            w = jax.nn.softmax(topk_s, axis=-1)
            out = jnp.zeros_like(x)
            for ei in range(NUM_EXPERTS):
                g = jnp.where(topk_i == ei, w, 0.0).sum(-1)
                hh = jax.nn.gelu(x @ W1[ei] + b1[ei], approximate=False)
                out = out + g[..., None] * (hh @ W2[ei] + b2[ei])
            return out
        key = jax.random.key(seed)
        ks = jax.random.split(key, 8)
        s = 0.05
        return {'x': jax.random.normal(ks[0], (B, N, D), jnp.float32), 'W_gat': jax.random.normal(ks[1], (D, HEADS * NUM_EXPERTS), jnp.float32) * s, 'att_src': jax.random.normal(ks[2], (HEADS, NUM_EXPERTS), jnp.float32) * s, 'att_dst': jax.random.normal(ks[3], (HEADS, NUM_EXPERTS), jnp.float32) * s, 'b_gat': jnp.zeros((HEADS * NUM_EXPERTS,), jnp.float32), 'ln_gamma': jnp.ones((HEADS * NUM_EXPERTS,), jnp.float32), 'ln_beta': jnp.zeros((HEADS * NUM_EXPERTS,), jnp.float32), 'W1': jax.random.normal(ks[4], (NUM_EXPERTS, D, 2 * D), jnp.float32) * s, 'b1': jnp.zeros((NUM_EXPERTS, 2 * D), jnp.float32), 'W2': jax.random.normal(ks[5], (NUM_EXPERTS, 2 * D, D), jnp.float32) * s, 'b2': jnp.zeros((NUM_EXPERTS, D), jnp.float32), 'edge_index': jax.random.randint(ks[6], (2, N_EDGES), 0, B * N, jnp.int32)}
    _L0_ffn_all = _L0_ffn_setup()
    _L0_ffn_in = {k: v for k, v in _L0_ffn_all.items() if k in ('W_gat', 'att_src', 'att_dst', 'b_gat', 'ln_gamma', 'ln_beta', 'W1', 'b1', 'W2', 'b2', 'edge_index')}
    del _L0_ffn_all
    return {'x': x, 'src': src, 'dst': dst, 'edge_weight': edge_weight, 'L0_gnn_weight': _L0_gnn_in['weight'], 'L0_gnn_gamma': _L0_gnn_in['gamma'], 'L0_gnn_beta': _L0_gnn_in['beta'], 'L0_ffn_W_gat': _L0_ffn_in['W_gat'], 'L0_ffn_att_src': _L0_ffn_in['att_src'], 'L0_ffn_att_dst': _L0_ffn_in['att_dst'], 'L0_ffn_b_gat': _L0_ffn_in['b_gat'], 'L0_ffn_ln_gamma': _L0_ffn_in['ln_gamma'], 'L0_ffn_ln_beta': _L0_ffn_in['ln_beta'], 'L0_ffn_W1': _L0_ffn_in['W1'], 'L0_ffn_b1': _L0_ffn_in['b1'], 'L0_ffn_W2': _L0_ffn_in['W2'], 'L0_ffn_b2': _L0_ffn_in['b2'], 'L0_ffn_edge_index': _L0_ffn_in['edge_index']}

def reference(x, src, dst, edge_weight, L0_gnn_weight, L0_gnn_gamma, L0_gnn_beta, L0_ffn_W_gat, L0_ffn_att_src, L0_ffn_att_dst, L0_ffn_b_gat, L0_ffn_ln_gamma, L0_ffn_ln_beta, L0_ffn_W1, L0_ffn_b1, L0_ffn_W2, L0_ffn_b2, L0_ffn_edge_index):
    import jax
    import jax.numpy as jnp

    def _L0_gnn_ref(x, weight, gamma, beta, edge_weight, edge_src, edge_dst):
        import jax, jax.numpy as jnp
        import numpy as np
        BN_EPS = 1e-05
        IDX = np.array([[0, 1, 2, 3, 4, 5, 6, 7], [1, 0, 3, 2, 5, 4, 7, 6], [2, 3, 0, 1, 6, 7, 4, 5], [3, 2, 1, 0, 7, 6, 5, 4], [4, 5, 6, 7, 0, 1, 2, 3], [5, 4, 7, 6, 1, 0, 3, 2], [6, 7, 4, 5, 2, 3, 0, 1], [7, 6, 5, 4, 3, 2, 1, 0]], dtype=np.int32)
        SIGN = np.array([[1, 1, 1, 1, 1, 1, 1, 1], [1, -1, 1, -1, 1, -1, -1, 1], [1, -1, -1, 1, 1, 1, -1, -1], [1, 1, -1, -1, 1, -1, 1, -1], [1, -1, -1, -1, -1, 1, 1, 1], [1, 1, -1, 1, -1, -1, -1, 1], [1, 1, 1, -1, -1, 1, -1, -1], [1, -1, 1, 1, -1, -1, 1, -1]], dtype=np.float32)

        def make_octonion_mul(kernel):
            in8, out = kernel.shape
            out8 = out // 8
            a = kernel.reshape(in8, 8, out8).transpose(1, 0, 2)
            blocks = jnp.asarray(SIGN)[:, :, None, None] * a[jnp.asarray(IDX)]
            return jnp.transpose(blocks, (1, 2, 0, 3)).reshape(8 * in8, out)
        N = x.shape[0]
        hamilton = make_octonion_mul(weight)
        support = x @ hamilton
        msgs = edge_weight[:, None] * support[edge_src]
        out = jax.ops.segment_sum(msgs, edge_dst, num_segments=N)
        mean = jnp.mean(out, axis=0)
        var = jnp.var(out, axis=0)
        out = (out - mean) * jax.lax.rsqrt(var + BN_EPS) * gamma + beta
        return jnp.tanh(out)

    def _L0_ffn_ref(x, W_gat, att_src, att_dst, b_gat, ln_gamma, ln_beta, W1, b1, W2, b2, edge_index):
        import jax, jax.numpy as jnp
        import numpy as np
        B, N, D = (16, 512, 256)
        NUM_EXPERTS, TOP_K, HEADS = (4, 2, 4)
        N_EDGES = 131072
        LN_EPS = 1e-05

        def _layernorm(x, g, b):
            mu = x.mean(-1, keepdims=True)
            var = ((x - mu) ** 2).mean(-1, keepdims=True)
            return (x - mu) * jax.lax.rsqrt(var + LN_EPS) * g + b

        def _forward(x, edge_index, W_gat, att_src, att_dst, b_gat, ln_gamma, ln_beta, W1, b1, W2, b2):
            Bc, Nc, Dc = x.shape
            M = Bc * Nc
            x_flat = x.reshape(M, Dc)
            h = (x_flat @ W_gat).reshape(M, HEADS, NUM_EXPERTS)
            loops = jnp.arange(M, dtype=edge_index.dtype)
            src = jnp.concatenate([edge_index[0], loops])
            dst = jnp.concatenate([edge_index[1], loops])
            a_src = (h * att_src).sum(-1)
            a_dst = (h * att_dst).sum(-1)
            e = jax.nn.leaky_relu(a_src[src] + a_dst[dst], negative_slope=0.2)
            e_max = jax.ops.segment_max(e, dst, num_segments=M)
            ee = jnp.exp(e - e_max[dst])
            denom = jax.ops.segment_sum(ee, dst, num_segments=M)
            alpha = ee / (denom[dst] + 1e-16)
            msg = h[src] * alpha[:, :, None]
            agg = jax.ops.segment_sum(msg, dst, num_segments=M).reshape(M, HEADS * NUM_EXPERTS) + b_gat
            scores = _layernorm(agg, ln_gamma, ln_beta).reshape(M, HEADS, NUM_EXPERTS).mean(1)
            scores = scores.reshape(Bc, Nc, NUM_EXPERTS)
            topk_s, topk_i = jax.lax.top_k(scores, TOP_K)
            w = jax.nn.softmax(topk_s, axis=-1)
            out = jnp.zeros_like(x)
            for ei in range(NUM_EXPERTS):
                g = jnp.where(topk_i == ei, w, 0.0).sum(-1)
                hh = jax.nn.gelu(x @ W1[ei] + b1[ei], approximate=False)
                out = out + g[..., None] * (hh @ W2[ei] + b2[ei])
            return out
        return _forward(x, edge_index, W_gat, att_src, att_dst, b_gat, ln_gamma, ln_beta, W1, b1, W2, b2)
    x = x + _L0_gnn_ref(_layernorm(x, axis=-1), L0_gnn_weight, L0_gnn_gamma, L0_gnn_beta, edge_weight, src, dst)
    x = x + _L0_ffn_ref(_layernorm(x, axis=-1)[None], L0_ffn_W_gat, L0_ffn_att_src, L0_ffn_att_dst, L0_ffn_b_gat, L0_ffn_ln_gamma, L0_ffn_ln_beta, L0_ffn_W1, L0_ffn_b1, L0_ffn_W2, L0_ffn_b2, L0_ffn_edge_index)[0]
    return x

_drawn_inputs = setup_inputs


def setup_inputs(seed=0):
    import zlib

    import numpy as np

    out = dict(_drawn_inputs(seed))
    spreads = {'L0_gnn_gamma': (1.0, 0.2),
     'L0_gnn_beta': (0.0, 0.1),
     'L0_ffn_b_gat': (0.0, 0.1),
     'L0_ffn_ln_gamma': (1.0, 0.2),
     'L0_ffn_ln_beta': (0.0, 0.1),
     'L0_ffn_b1': (0.0, 0.1),
     'L0_ffn_b2': (0.0, 0.1)}
    factors = {}
    for name, (base, spread) in spreads.items():
        noise = np.random.default_rng([zlib.crc32(name.encode()), seed]).standard_normal(out[name].shape)
        drawn = base * np.exp(spread * noise) if base else spread * noise
        out[name] = jnp.asarray(drawn.astype(out[name].dtype))
    for name, factor in factors.items():
        out[name] = (out[name] * factor).astype(out[name].dtype)
    return out
```

```python
import concourse.bass as bass
import concourse.mybir as mybir
from contextlib import ExitStack, contextmanager

P = 128
IDX = [[0, 1, 2, 3, 4, 5, 6, 7], [1, 0, 3, 2, 5, 4, 7, 6], [2, 3, 0, 1, 6, 7, 4, 5], [3, 2, 1, 0, 7, 6, 5, 4],
       [4, 5, 6, 7, 0, 1, 2, 3], [5, 4, 7, 6, 1, 0, 3, 2], [6, 7, 4, 5, 2, 3, 0, 1], [7, 6, 5, 4, 3, 2, 1, 0]]
SIGN = [[1, 1, 1, 1, 1, 1, 1, 1], [1, -1, 1, -1, 1, -1, -1, 1], [1, -1, -1, 1, 1, 1, -1, -1],
        [1, 1, -1, -1, 1, -1, 1, -1], [1, -1, -1, -1, -1, 1, 1, 1], [1, 1, -1, 1, -1, -1, -1, 1],
        [1, 1, 1, -1, -1, 1, -1, -1], [1, -1, 1, 1, -1, -1, 1, -1]]
BIG = 1e30
EPS = 1e-5


class Chain:

    def __init__(self, eng, sem):
        self.eng, self.sem, self.base, self.n, self.turn = eng, sem, 0, 0, None

    def value(self):
        return self.base + self.n if self.turn is None else self.turn + (self.base + self.n)

    def __call__(self, ins):
        self.mark(ins)
        self.wait()

    def mark(self, ins):
        ins.then_inc(self.sem, 1)
        self.n += 1

    def wait(self):
        self.eng.wait_ge(self.sem, self.value())

    @contextmanager
    def loop(self, first, end, per):
        self.base, self.n = self.base + self.n - first * per, 0
        with self.eng.Fori(first, end) as i:
            self.turn = i * per
            yield i
            assert self.n == per, (self.n, per)
        self.base, self.n, self.turn = self.base + end * per, 0, None


def gnn_moe(nc, x, src, dst, edge_weight, gnn_w, gnn_gamma, gnn_beta, w_gat, att_src, att_dst, b_gat,
            ln_gamma, ln_beta, w1, b1, w2, b2, edge_index, out):
    f32, bf16, i32, u32 = mybir.dt.float32, mybir.dt.bfloat16, mybir.dt.int32, mybir.dt.uint32
    ALU, ACT, AX = mybir.AluOpType, mybir.ActivationFunctionType, mybir.AxisListType

    N, D = x.shape
    NT = -(-N // P)
    NP = NT * P
    LAST = N - (NT - 1) * P
    E1 = src.shape[0]
    FULL = E1 // P
    REST = E1 - FULL * P
    ROWB = -(-(FULL + 1 + NT + 1) // P)
    STEPS = FULL + 1 + NT
    HS = 13
    TURNS = 32
    assert TURNS * 2 * HS >= STEPS and (TURNS + 1) * 2 * HS <= ROWB * P
    E2 = edge_index.shape[1]
    RUN = E2 // P
    GT = 4
    HT = 16
    RT = RUN // (2 * HT)
    assert RT == TURNS and RUN % (2 * HT) == 0
    CH = 2 * HT
    NE, FF = w1.shape[0], w1.shape[2]
    H = w_gat.shape[1] // NE
    HE = H * NE
    KD = D // P
    MF = FF // P
    TB = NP // TURNS
    TH = TB // 2
    assert TB * TURNS == NP and TH <= P
    W = HE + 2 * H
    LF = H + HE
    SINK = E2

    def dram(name, shape, dt=f32):
        return nc.dram_tensor(name, shape, dt).ap()

    x1_d = dram("x1_d", [NP, D])
    rows_d = dram("rows_d", [ROWB * P, 3 * P])
    win_d = dram("win_d", [ROWB * P], i32)
    node_d = dram("node_d", [NP, W])
    x2_d = dram("x2_d", [NP, D])
    sorted_d = dram("sorted_d", [E2, 2])
    adst_d = dram("adst_d", [E2 + NP, H])
    sums_d = dram("sums_d", [E2 + 1, W])
    y_d = dram("y_d", [NP, NE, D])

    ctx = ExitStack()
    with ctx:
        def sb(name, shape, dt=f32):
            return ctx.enter_context(nc.sbuf_tensor(name, shape, dt))

        def sem(name):
            return ctx.enter_context(nc.semaphore(name))

        regA = sb("regA", [P, NT * D])
        xa = regA[:, :].rearrange("p (n d) -> p n d", n=NT)
        gnn = regA[:, :].rearrange("p (k n) -> p k n", k=KD)
        regB = sb("regB", [P, NT * D])
        acc = regB[:, :].rearrange("p (k n) -> p k n", k=KD)
        x3T = acc
        regC = sb("regC", [P, 2 * HS * (D + P)])
        rows = regC[:, 0:2 * HS * D].rearrange("p (a s d) -> p a s d", a=2, s=HS)
        onehot = regC[:, 2 * HS * D:2 * HS * (D + P)].rearrange("p (a s d) -> p a s d", a=2, s=HS)
        w1s = regC[:, 0:NE * KD * FF].rearrange("p (e k f) -> p e k f", e=NE, k=KD)
        w2s = regC[:, NE * KD * FF:NE * KD * FF + NE * MF * D].rearrange("p (e k f) -> p e k f", e=NE, k=MF)
        iokb = regC[:, 0:ROWB * P].bitcast(i32)
        ham4 = regC[:, ROWB * P:ROWB * P + D]
        st1 = regC[:, 2 * ROWB * P:2 * ROWB * P + NT * 6].rearrange("p (n s) -> p n s", n=NT)
        EX = NE * (KD * FF + MF * D)
        b2s = regC[0:1, EX:EX + NE * D].rearrange("p (e d) -> p e d", e=NE)
        RD = 3 * ROWB * P
        erow = regB[:, 0:RD].rearrange("p (c q e) -> p c q e", c=ROWB, q=3)
        eint = regB[:, RD:2 * RD].bitcast(i32).rearrange("p (c q e) -> p c q e", c=ROWB, q=3)
        strow = regB[:, 2 * RD:3 * RD].rearrange("p (c q e) -> p c q e", c=ROWB, q=3)
        before = regB[:, 3 * RD:3 * RD + ROWB * ROWB * P // 2].bitcast(bf16).rearrange("p (c k) -> p c k", c=ROWB)
        adraw = regA[:, 0:H * RUN].rearrange("p (t h) -> p t h", h=H)
        adst = regA[:, H * RUN:2 * H * RUN].rearrange("p (h t) -> p h t", h=H)
        at = 2 * H * RUN
        yo = regA[:, at:at + 2 * NE * D].rearrange("p (a e d) -> p a e d", a=2, e=NE)
        at += 2 * NE * D
        lc = regA[:, at:at + 2 * CH * W].rearrange("p (a t w) -> p a t w", a=2, t=CH)
        at += 2 * CH * W
        hc = regA[:, at:at + W * CH].rearrange("p (w t) -> p w t", w=W)
        assert at + W * CH <= NT * D
        regE = sb("regE", [P, 4 * ROWB * P + 16])
        stcol = regE[:, 0:RD].rearrange("p (q k) -> p q k", q=3)
        step_src = regE[:, RD:RD + ROWB * P].bitcast(u32)
        xin = regE[:, 0:2 * D].rearrange("p (a d) -> p a d", a=2)
        x2o = regE[:, 2 * D:4 * D].rearrange("p (a d) -> p a d", a=2)
        x3 = regE[:, 4 * D:6 * D].rearrange("p (a d) -> p a d", a=2)
        olt = regE[:, 6 * D:6 * D + 2 * GT * P].rearrange("p (a b c) -> p a b c", a=2, b=GT)
        at = 6 * D + 2 * GT * P
        run4 = regE[:, at:at + GT * GT * NT].rearrange("p (a b c) -> p a b c", a=GT, b=GT)
        at += GT * GT * NT
        ub = regE[:, at:at + GT * P // 2].bitcast(bf16).rearrange("p (a b) -> p a b", a=GT)
        assert at + GT * P // 2 <= 4 * ROWB * P + 16
        crow = regE[0:LF, 0:8 * (P + 1)].rearrange("p (a b) -> p a b", a=8)
        kint = sb("kint", [P, RUN], i32)
        sint = sb("sint", [P, RUN], i32)
        pay = sb("pay", [P, RUN + CH, 2])
        lo = sb("lo", [P, RUN + HT], bf16)
        hi = sb("hi", [P, RUN + HT], bf16)
        ol = sb("ol", [P, 2, HT, P], bf16)
        ohf = sb("ohf", [P, 2 * HT * NT], bf16)
        oh = ohf[:, :].rearrange("p (a b c) -> p a b c", a=2, b=HT)
        olf = ol[:, :, :, :].rearrange("p a b c -> p (a b c)").bitcast(f32)
        hh = olf[:, 0:MF * TB].rearrange("p (m t) -> p m t", m=MF)
        at = MF * TB
        sc, sc2, ww, rr = [olf[:, at + i * H * CH:at + (i + 1) * H * CH].rearrange("p (h t) -> p h t", h=H) for i in range(4)]
        at += 4 * H * CH
        mb = olf[:, at:at + H * (CH + 1)].rearrange("p (h t) -> p h t", h=H)
        nm = ohf[:, :].bitcast(f32)[:, 0:HE * CH].rearrange("p (f t) -> p f t", f=HE)
        neg = kint[:, :].bitcast(f32)
        keep = sint[:, :].bitcast(f32)
        iot = sb("iot", [P, P], i32)
        iof = sb("iof", [P, P])
        iob = sb("iob", [P, P], bf16)
        pidx = sb("pidx", [P, ROWB], i32)
        pidf = sb("pidf", [P, ROWB])
        ident = sb("ident", [P, P])
        identb = sb("identb", [P, P], bf16)
        above = sb("above", [P, P])
        ones = sb("ones", [P, P])
        onesb = sb("onesb", [P, 1], bf16)
        ZC = 148
        ZR = (E2 + NP) * H // P // ZC
        assert ZC * ZR * P == (E2 + NP) * H
        zero = sb("zero", [P, ZC])
        eps = sb("eps", [P, 1])
        sinkrow = sb("sinkrow", [1, W])
        mv1 = sb("mv1", [P, NT, 2])
        sd1 = sb("sd1", [P, NT])
        rs1 = sb("rs1", [P, NT])
        nb1 = sb("nb1", [P, NT])
        gam = sb("gam", [P, KD])
        bet = sb("bet", [P, KD])
        CB = -(-NP // 512)
        stb = sb("stb", [P, KD, CB, 6])
        mvb = sb("mvb", [P, KD, 2])
        sdb = sb("sdb", [P, KD])
        scb = sb("scb", [P, KD])
        bib = sb("bib", [P, KD])
        lwin = sb("lwin", [P, ROWB], i32)
        lv = sb("lv", [P, ROWB])
        ikf = sb("ikf", [P, ROWB])
        jkf = sb("jkf", [P, ROWB])
        iku = sb("iku", [P, ROWB], u32)
        jki = sb("jki", [P, ROWB], i32)
        wins = sb("wins", [1, 2 * TURNS, 16], i32)
        idxr = sb("idxr", [P, 2, 16], u32)
        cnt = sb("cnt", [P, NT])
        basef = sb("basef", [P, NT])
        tots = sb("tots", [P, NT])
        totx = sb("totx", [P, NT + 1])
        gm = sb("gm", [P, GT, NT])
        posr = sb("posr", [P, 2, HT], u32)
        payr = sb("payr", [P, 2, HT, 2])
        tt = sb("tt", [P, KD, P])
        xt = sb("xt", [P, KD, P])
        stn = sb("stn", [P, 6])
        mvn = sb("mvn", [P, 2])
        sdn = sb("sdn", [P, 1])
        rsn = sb("rsn", [P, 1])
        nbn = sb("nbn", [P, 1])
        wg = sb("wg", [P, KD, W])
        attb = sb("attb", [P, 2, HE])
        wt = sb("wt", [P, HE])
        tab = sb("tab", [P, NT, W])
        sidx = sb("sidx", [P, NT], u32)
        eidx = sb("eidx", [P, NT], u32)
        t49 = sb("t49", [P, 4, NT])
        b1s = sb("b1s", [P, NE, MF])
        gatp = sb("gatp", [P, 3, HE])
        key0 = sb("key0", [P, 1])
        keyp = sb("keyp", [P, 1])
        key0u = sb("key0u", [P, 1], u32)
        arow = sb("arow", [P, W])
        grow = sb("grow", [P, 2, HT, W])
        gidx = sb("gidx", [P, 2, HT], u32)
        ham = grow[:, :, :, :].rearrange("p a b c -> p (a b c)")[:, 0:KD * D].rearrange("p (k d) -> p k d", k=KD)
        last = sb("last", [P, W])
        cin = sb("cin", [P, 4, LF])
        cout = sb("cout", [P, 2, LF])
        same = lo[:, 0:RUN]
        nfirst = sb("nfirst", [P, 1])
        fidx = sb("fidx", [P, 1], u32)
        cf = sb("cf", [P, 4])
        frow = sb("frow", [P, W])
        fx = sb("fx", [P, 4, LF])
        esum = pay[:, :, :].rearrange("p t w -> p (t w)")[:, 0:NT * W].rearrange("p (n w) -> p n w", n=NT)

        fin = [regA[:, i * NT * HE:(i + 1) * NT * HE] for i in range(6)]
        f4 = [regA[:, 6 * NT * HE + i * NT * H:6 * NT * HE + (i + 1) * NT * H] for i in range(16)]
        assert 6 * NT * HE + 16 * NT * H <= NT * D
        YR = 8
        yin = regB[:, 0:YR * NE * D].rearrange("p (b e d) -> p b e d", b=YR, e=NE)
        xin2 = regB[:, YR * NE * D:YR * (NE + 1) * D].rearrange("p (b d) -> p b d", b=YR)

        bank = [ctx.enter_context(nc.psum_tensor(f"bank{i}", [P, 512], f32)) for i in range(8)]

        def slot(s):
            return bank[s % 7][:, 0:D]

        SB = HS - 7

        s_fill = sem("s_fill")
        s_x = sem("s_x")
        s_edge = sem("s_edge")
        s_gat = sem("s_gat")
        s_par = sem("s_par")
        s_cst = sem("s_cst")
        s_cstv = sem("s_cstv")
        s_sd1, s_rs1, s_x1, s_x1d = sem("s_sd1"), sem("s_rs1"), sem("s_x1"), sem("s_x1d")
        s_rows, s_rowsd, s_bef, s_ik, s_iku, s_strow, s_dl, s_tr, s_win, s_wind = [
            sem(n) for n in ("s_rows", "s_rowsd", "s_bef", "s_ik", "s_iku", "s_strow", "s_dl", "s_tr", "s_win", "s_wind")]
        s_v = sem("s_v")
        s_idx, s_oh, s_hist, s_sel, s_step, s_acc = [sem(n) for n in ("s_idx", "s_oh", "s_hist", "s_sel", "s_step", "s_acc")]
        s_row = [sem("s_row0"), sem("s_row1")]
        s_zero, s_adz = sem("s_zero"), sem("s_adz")
        s_cnt, s_pre, s_t0 = sem("s_cnt"), sem("s_pre"), sem("s_t0")
        s_bo, s_bn, s_bc, s_sdb, s_bnr, s_tanh = [sem(n) for n in ("s_bo", "s_bn", "s_bc", "s_sdb", "s_bnr", "s_tanh")]
        s_ol, s_r, s_t, s_trp, s_olt, s_eq, s_u, s_g, s_gm, s_pos = [
            sem(n) for n in ("s_ol", "s_r", "s_t", "s_trp", "s_olt", "s_eq", "s_u", "s_g", "s_gm", "s_pos")]
        s_scat = [sem("s_scat0"), sem("s_scat1")]
        s_xin = [sem("s_xin0"), sem("s_xin1")]
        s_x2d = [sem("s_x2d0"), sem("s_x2d1")]
        s_px, s_mvn, s_sdn, s_rsn, s_x2, s_x3, s_x3t, s_x3c, s_tabp, s_tab = [
            sem(n) for n in ("s_px", "s_mvn", "s_sdn", "s_rsn", "s_x2", "s_x3", "s_x3t", "s_x3c", "s_tabp", "s_tab")]
        s_wexp, s_noded, s_seidx, s_ads, s_srt, s_keys, s_k0, s_arow, s_adr = [
            sem(n) for n in ("s_wexp", "s_noded", "s_seidx", "s_ads", "s_srt", "s_keys", "s_k0", "s_arow", "s_adr")]
        s_gidx = sem("s_gidx")
        s_grow = [sem("s_grow0"), sem("s_grow1")]
        s_sc, s_ww, s_lc = sem("s_sc"), sem("s_ww"), sem("s_lc")
        s_lcd = [sem("s_lcd0"), sem("s_lcd1")]
        s_up, s_hh, s_dn, s_yo = sem("s_up"), sem("s_hh"), sem("s_dn"), sem("s_yo")
        s_yd = [sem("s_yd0"), sem("s_yd1")]
        s_cin, s_ctr, s_ce, s_cx, s_cb, s_cbt, s_fidx, s_frow, s_fe, s_fx, s_fst, s_fixed, s_esum = [
            sem(n) for n in ("s_cin", "s_ctr", "s_ce", "s_cx", "s_cb", "s_cbt", "s_fidx", "s_frow", "s_fe", "s_fx",
                             "s_fst", "s_fixed", "s_esum")]
        s_tt, s_begun, s_begun_v = sem("s_tt"), sem("s_begun"), sem("s_begun_v")
        s_ma, s_mx, s_sqv, s_sqa = sem("s_ma"), sem("s_mx"), sem("s_sqv"), sem("s_sqa")
        s_yl = [sem(f"s_yl{i}") for i in range(YR)]
        s_cmb = sem("s_cmb")
        s_out = [sem(f"s_out{i}") for i in range(YR)]

        def each(ap, n):
            return ap.unsqueeze(2).to_broadcast([ap.shape[0], ap.shape[1], n])

        def every(ap, n):
            return ap.unsqueeze(1).to_broadcast([ap.shape[0], n, ap.shape[1]])

        block = ctx.enter_context(nc.Block())

        @block.sync
        def _(sp):
            sp.sem_inc(s_hist, 2)
            sp.sem_inc(s_hh, MF)
            sp.sem_inc(s_yo, 2)
            sp.sem_inc(s_acc, SB)
            sp.sem_inc(s_g, 3)
            sp.sem_inc(s_t, 1)
            sp.sem_inc(s_u, 1)
            sp.sem_inc(s_gm, 1)
            sp.sem_inc(s_px, 2)
            sp.sem_inc(s_x3, 1)
            for s in s_x2d + s_lcd + s_yd:
                sp.sem_inc(s, 16)
            sp.wait_ge(s_fill, 1)
            with nc.allow_non_contiguous_dma(reason="short parameter vectors"):
                sp.dma_start(xa[:, 0:NT - 1, :], x[0:(NT - 1) * P, :].rearrange("(n p) d -> p n d", p=P)).then_inc(s_x, 16)
                sp.dma_start(xa[0:LAST, NT - 1, :], x[(NT - 1) * P:N, :]).then_inc(s_x, 16)
                for q, a in ((0, src), (1, dst)):
                    fb = (ROWB - 1) * P
                    sp.dma_start(eint[:, 0:ROWB - 1, q, :], a[0:fb * P].rearrange("(c p e) -> p c e", p=P, e=P)).then_inc(s_edge, 16)
                    sp.dma_start(eint[0:FULL - fb, ROWB - 1, q, :], a[fb * P:FULL * P].rearrange("(p e) -> p e", e=P)).then_inc(s_edge, 16)
                    sp.dma_start(eint[FULL - fb:FULL - fb + 1, ROWB - 1, q, 0:REST], a[FULL * P:E1].rearrange("(a e) -> a e", a=1)).then_inc(s_edge, 16)
                sp.dma_start(erow[:, 0:ROWB - 1, 2, :], edge_weight[0:fb * P].rearrange("(c p e) -> p c e", p=P, e=P)).then_inc(s_edge, 16)
                sp.dma_start(erow[0:FULL - fb, ROWB - 1, 2, :], edge_weight[fb * P:FULL * P].rearrange("(p e) -> p e", e=P)).then_inc(s_edge, 16)
                sp.dma_start(erow[FULL - fb:FULL - fb + 1, ROWB - 1, 2, 0:REST], edge_weight[FULL * P:E1].rearrange("(a e) -> a e", a=1)).then_inc(s_edge, 16)
                sp.dma_start(kint[:, :], edge_index[1, :].rearrange("(p t) -> p t", p=P)).then_inc(s_gat, 16)
                sp.dma_start(sint[:, :], edge_index[0, :].rearrange("(p t) -> p t", p=P)).then_inc(s_gat, 16)
                for g in range(4):
                    sp.dma_start(ham4[32 * g:32 * g + 32, :], gnn_w[:, :]).then_inc(s_par, 16)
                sp.dma_start(gam[:, :], gnn_gamma.rearrange("(m p) -> p m", p=P)).then_inc(s_par, 16)
                sp.dma_start(bet[:, :], gnn_beta.rearrange("(m p) -> p m", p=P)).then_inc(s_par, 16)
                sp.dma_start(wg[:, :, 0:HE], w_gat.rearrange("(k p) f -> p k f", p=P)).then_inc(s_par, 16)
                for q, a in ((0, att_src), (1, att_dst)):
                    sp.dma_start(attb[:, q, :], a.rearrange("h e -> (h e)").partition_broadcast(P)).then_inc(s_par, 16)
                for q, a in ((0, b_gat), (1, ln_gamma), (2, ln_beta)):
                    sp.dma_start(gatp[:, q, :], a.partition_broadcast(P)).then_inc(s_par, 16)
                for e in range(NE):
                    sp.dma_start(b1s[:, e, :], b1[e, :].rearrange("(m p) -> p m", p=P)).then_inc(s_par, 16)
            sp.wait_ge(s_zero, 2)
            sp.dma_start(adst_d.rearrange("(p q t) h -> p q (t h)", p=P, q=ZR), every(zero[:, :], ZR)).then_inc(s_adz, 16)
            sp.dma_start(sums_d[SINK:SINK + 1, :], sinkrow[:, :]).then_inc(s_adz, 16)
            sp.wait_ge(s_rows, 1)
            sp.dma_start(rows_d.rearrange("(c p) w -> p c w", p=P), erow[:, :, :, :].rearrange("p c q e -> p c (q e)")).then_inc(s_rowsd, 16)
            sp.wait_ge(s_x1, 1)
            sp.dma_start(x1_d.rearrange("(n p) d -> p n d", p=P), xa).then_inc(s_x1d, 16)
            sp.wait_ge(s_win, 1)
            with nc.allow_non_contiguous_dma(reason="896 window numbers"):
                sp.dma_start(win_d.rearrange("(c p) -> p c", p=P), jki[:, :]).then_inc(s_wind, 16)
            sp.wait_ge(s_wind, 16)
            sp.dma_start(wins[:, :, 0:HS], win_d[0:2 * TURNS * HS].rearrange("(o a s) -> o a s", o=1, s=HS)).then_inc(s_wind, 16)

            sp.wait_ge(s_step, 2 * HS * TURNS)
            for e in range(NE):
                sp.dma_start(w1s[:, e, :, :], w1[e].rearrange("(k p) f -> p k f", p=P)).then_inc(s_wexp, 16)
                sp.dma_start(w2s[:, e, :, :], w2[e].rearrange("(k p) f -> p k f", p=P)).then_inc(s_wexp, 16)

            sp.dma_start(b2s, b2.rearrange("(a e) d -> a e d", a=1)).then_inc(s_wexp, 16)

            def load_x(n, hf, rows_n=P):
                sp.wait_ge(s_px, n + 1)
                sp.dma_start(xin[0:rows_n, hf, :], x[bass.ds(n * P, rows_n), :]).then_inc(s_xin[hf], 16)

            def store_x2(n, hf):
                sp.wait_ge(s_x2, n + 1)
                sp.dma_start(x2_d[bass.ds(n * P, P), :], x2o[:, hf, :]).then_inc(s_x2d[hf], 16)

            with sp.Fori(0, (NT - 1) // 2) as i:
                load_x(i * 2, 0)
                load_x(i * 2 + 1, 1)
                store_x2(i * 2, 0)
                store_x2(i * 2 + 1, 1)
            load_x(NT - 1, 0, LAST)
            store_x2(NT - 1, 0)
            sp.wait_ge(s_tab, NT)
            sp.dma_start(node_d.rearrange("(n p) w -> p n w", p=P), tab[:, :, :]).then_inc(s_noded, 16)
            for hf in range(2):
                sp.wait_ge(s_scat[hf], 16 * HT * RT)
            sp.dma_start(pay[:, 0:RUN, :], sorted_d.rearrange("(p t) w -> p t w", p=P)).then_inc(s_srt, 16)
            with nc.allow_non_contiguous_dma(reason="one key of each partition"):
                sp.dma_start(keyp[1:P, :], sorted_d.rearrange("(p t) w -> p t w", p=P)[0:P - 1, RUN - 1, 0:1]).then_inc(s_srt, 16)
            sp.wait_ge(s_ads, 16 * NT)
            sp.dma_start(adraw, adst_d[0:E2, :].rearrange("(p t) h -> p t h", p=P)).then_inc(s_adr, 16)

            with sp.Fori(0, TURNS // 2) as i:
                for hf in range(2):
                    t = i * 2 + hf
                    sp.wait_ge(s_lc, t + 1)
                    sp.dma_start(sums_d[0:E2, :].rearrange("(p t) w -> p t w", p=P)[:, bass.ds(t * CH, CH), :],
                                 lc[:, hf, :, :]).then_inc(s_lcd[hf], 16)
                    for a in range(2):
                        sp.wait_ge(s_yo, t * (2 * NE) + (2 * NE + 1 + a))
                        sp.dma_start(y_d[bass.ds(t * TB + a * TH, TH), :, :], yo[0:TH, a, :, :]).then_inc(s_yd[a], 16)
            sp.wait_ge(s_yd[0], 16 * (TURNS + 1))
            sp.wait_ge(s_yd[1], 16 * (TURNS + 1))
            sp.wait_ge(s_x2d[0], 16 * (NT // 2 + 2))
            sp.wait_ge(s_x2d[1], 16 * (NT // 2 + 1))
            for n in range(NT):
                b, m = n % YR, (P if n < NT - 1 else LAST)
                if n >= YR:
                    sp.wait_ge(s_cmb, n - YR + 1)
                    sp.wait_ge(s_out[b], 16 * (n // YR))
                sp.dma_start(yin[0:m, b, :, :], y_d[n * P:n * P + m, :, :]).then_inc(s_yl[b], 16)
                sp.dma_start(xin2[0:m, b, :], x2_d[n * P:n * P + m, :]).then_inc(s_yl[b], 16)
                if n >= YR - 1:
                    k = n - YR + 1
                    sp.wait_ge(s_cmb, k + 1)
                    sp.dma_start(out[k * P:k * P + P, :], xin2[:, k % YR, :]).then_inc(s_out[k % YR], 16)
            for k in range(NT - YR + 1, NT):
                m = P if k < NT - 1 else LAST
                sp.wait_ge(s_cmb, k + 1)
                sp.dma_start(out[k * P:k * P + m, :], xin2[0:m, k % YR, :]).then_inc(s_out[k % YR], 16)
            for b in range(YR):
                sp.wait_ge(s_out[b], 16 * len(range(b, NT, YR)))

        @block.gpsimd
        def _(pool):
            pool.iota(iot[:, :], pattern=[[1, P]], base=0, channel_multiplier=0)
            pool.iota(iokb[:, :], pattern=[[1, ROWB * P]], base=0, channel_multiplier=0)
            pool.iota(pidx[:, :], pattern=[[P, ROWB]], base=0, channel_multiplier=1)
            pool.memset(ident[:, :], 0.0)
            pool.memset(above[:, :], 1.0)
            pool.memset(ones[:, :], 1.0).then_inc(s_cst, 1)
            pool.wait_ge(s_cst, 1)
            pool.affine_select(out=ident[:, :], in_=ident[:, :], compare_op=ALU.not_equal, fill=1.0, base=0,
                               pattern=[[-1, P]], channel_multiplier=1)
            pool.affine_select(out=above[:, :], in_=above[:, :], compare_op=ALU.is_gt, fill=0.0, base=0,
                               pattern=[[1, P]], channel_multiplier=-1).then_inc(s_cst, 1)
            pool.wait_ge(s_iku, 1)
            pool.wait_ge(s_rowsd, 16)
            for c in range(ROWB):
                pool.indirect_dma_start(strow[:, c, :, :].rearrange("p q e -> p (q e)"), None, rows_d,
                                        bass.IndirectOffsetOnAxis(ap=iku[:, c:c + 1], axis=0)).then_inc(s_strow, 16)
            pool.wait_ge(s_x1d, 16)
            with pool.Fori(0, TURNS) as i:
                for hf in range(2):
                    pool.wait_ge(s_idx, i * 2 + (hf + 1))
                    pool.sem_inc(s_begun, 1)
                    for s in range(HS):
                        pool.indirect_dma_start(rows[:, hf, s, :], None, x1_d,
                                                bass.IndirectOffsetOnAxis(ap=idxr[:, hf, s:s + 1], axis=0)
                                                ).then_inc(s_row[hf], 16)
            with pool.Fori(0, RT) as i:
                for hf in range(2):
                    for g in range(HT // GT):
                        pool.wait_ge(s_pos, i * (2 * HT // GT) + (hf * (HT // GT) + g + 1))
                        pool.sem_inc(s_begun, 1)
                        for t in range(g * GT, (g + 1) * GT):
                            pool.indirect_dma_start(sorted_d, bass.IndirectOffsetOnAxis(ap=posr[:, hf, t:t + 1], axis=0),
                                                    payr[:, hf, t, :], None).then_inc(s_scat[hf], 16)
            pool.wait_ge(s_tab, NT)
            pool.wait_ge(s_seidx, 1)
            pool.wait_ge(s_adz, 16 * 2)
            for n in range(NT):
                pool.indirect_dma_start(adst_d, bass.IndirectOffsetOnAxis(ap=sidx[:, n:n + 1], axis=0),
                                        tab[:, n, HE + H:W], None).then_inc(s_ads, 16)
            pool.wait_ge(s_k0, 1)
            pool.wait_ge(s_noded, 16)
            pool.indirect_dma_start(arow[:, :], None, node_d, bass.IndirectOffsetOnAxis(ap=key0u[:, :], axis=0)).then_inc(s_arow, 16)
            with pool.Fori(0, RT) as i:
                for hf in range(2):
                    pool.wait_ge(s_gidx, i * 2 + (hf + 1))
                    pool.sem_inc(s_begun, 1)
                    for t in range(HT):
                        pool.indirect_dma_start(grow[:, hf, t, :], None, node_d,
                                                bass.IndirectOffsetOnAxis(ap=gidx[:, hf, t:t + 1], axis=0)
                                                ).then_inc(s_grow[hf], 16)
            pool.wait_ge(s_fidx, 1)
            for s in s_lcd:
                pool.wait_ge(s, 16 * (TURNS // 2 + 1))
            pool.indirect_dma_start(frow[:, :], None, sums_d, bass.IndirectOffsetOnAxis(ap=fidx[:, :], axis=0)).then_inc(s_frow, 16)
            pool.wait_ge(s_fst, 1)
            pool.indirect_dma_start(sums_d, bass.IndirectOffsetOnAxis(ap=fidx[:, :], axis=0), arow[:, :], None).then_inc(s_fixed, 16)
            pool.wait_ge(s_fixed, 16)
            for n in range(NT):
                pool.indirect_dma_start(esum[:, n, :], None, sums_d, bass.IndirectOffsetOnAxis(ap=eidx[:, n:n + 1], axis=0)
                                        ).then_inc(s_esum, 16)

        @block.scalar
        def _(act):
            act.wait_ge(s_cstv, 1)
            act.wait_ge(s_sd1, 1)
            act.activation(sd1[:, :], mv1[:, :, 1], ACT.Sqrt, bias=eps[:, :], scale=1.0).then_inc(s_sd1, 1)
            act.wait_ge(s_rs1, 1)
            for n in range(NT):
                ins = act.activation(xa[:, n, :], xa[:, n, :], ACT.Identity, bias=nb1[:, n:n + 1], scale=rs1[:, n:n + 1])
            ins.then_inc(s_x1, 1)
            for b in range(CB):
                w = min(512, NP - b * 512)
                act.wait_ge(s_bo, b + 1)
                for m in range(KD):
                    ins = act.activation(gnn[:, m, b * 512:b * 512 + w], bank[m + 2 * (b % 2)][:, 0:w], ACT.Copy)
                ins.then_inc(s_bc, 1)
            act.wait_ge(s_sdb, 1)
            act.activation(sdb[:, :], mvb[:, :, 1], ACT.Sqrt, bias=eps[:, :], scale=1.0).then_inc(s_sdb, 1)
            act.wait_ge(s_bnr, 1)
            act.wait_ge(s_bc, CB)
            for m in range(KD):
                ins = act.activation(gnn[:, m, :], gnn[:, m, :], ACT.Tanh, bias=bib[:, m:m + 1], scale=scb[:, m:m + 1])
            ins.then_inc(s_tanh, 1)

            def olt_copy(g, par, tp):
                act.wait_ge(s_trp, g + 1)
                act.wait_ge(s_g, g + 2)
                act.activation(olt[:, par, :, :].rearrange("p a b -> p (a b)"), bank[par][:, :].bitcast(bf16)[:, 0:GT * P],
                               ACT.Copy).then_inc(s_olt, 1)

            def rank(G, gi):
                act.wait_ge(s_r, G + 1)
                act.wait_ge(s_g, G + 1)
                act.activation(run4[:, gi, :, :].rearrange("p a b -> p (a b)"), bank[3][:, 0:GT * NT], ACT.Copy).then_inc(s_t, 1)
                olt_copy(G + 1, (gi + 1) % 2, None)

            def next_tanh(n):
                act.activation(tt[:, :, :], gnn[:, :, bass.ds(n * P, P)], ACT.Copy).then_inc(s_tt, 1)

            def node(n, hf, gi, turn, ahead=True):
                if gi == 0:
                    act.wait_ge(s_mvn, n + 1)
                    act.activation(sdn[:, :], mvn[:, 1:2], ACT.Sqrt, bias=eps[:, :], scale=1.0).then_inc(s_sdn, 1)
                if gi == 1:
                    act.wait_ge(s_rsn, n + 1)
                    act.wait_ge(s_x2d[hf], (turn + 1) * 16)
                    act.activation(x2o[:, hf, :], bank[5][:, 0:D], ACT.Copy).then_inc(s_x2, 1)
                    act.activation(x3[:, hf, :], bank[5][:, 0:D], ACT.Identity, bias=nbn[:, :], scale=rsn[:, :]).then_inc(s_x3, 1)
                if gi == 2:
                    act.wait_ge(s_x3t, n + 1)
                    act.activation(xt[:, :, :], bank[6][:, 0:D].rearrange("p (k n) -> p k n", k=KD), ACT.Copy)
                    act.activation(x3T[:, :, bass.ds(n * P, P)], bank[6][:, 0:D].rearrange("p (k n) -> p k n", k=KD),
                                   ACT.Copy).then_inc(s_x3c, 1)
                if gi == 3:
                    act.wait_ge(s_tabp, n + 1)
                    act.activation(tab[:, bass.ds(n, 1), :].rearrange("p a w -> p (a w)"), bank[7][:, 0:W], ACT.Copy).then_inc(s_tab, 1)
                    if ahead:
                        next_tanh(n + 1)

            act.wait_ge(s_tanh, 1)
            next_tanh(0)
            olt_copy(0, 0, None)
            NG = HT // GT
            with act.Fori(0, (NT - 1) // 2) as i:
                for hf in range(2):
                    for gi in range(NG):
                        rank(i * (2 * NG) + (hf * NG + gi), gi)
                        node(i * 2 + hf, hf, gi, i)
            for gi in range(NG):
                node(NT - 1, 0, gi, (NT - 1) // 2, ahead=False)
            with act.Fori((NT - 1) // 2, RT) as i:
                for hf in range(2):
                    for gi in range(NG):
                        rank(i * (2 * NG) + (hf * NG + gi), gi)

            with act.Fori(0, TURNS) as i:
                for e in range(NE):
                    for m in range(MF):
                        k = e * MF + m
                        act.wait_ge(s_up, i * (NE * MF) + (k + 1))
                        act.activation(hh[:, m, :], bank[m][:, 0:TB], ACT.Gelu, bias=b1s[:, e, m:m + 1], scale=1.0).then_inc(s_hh, 1)
                    for a in range(2):
                        act.wait_ge(s_dn, i * (2 * NE) + (2 * e + a + 1))
                        if e == 0:
                            act.wait_ge(s_yd[a], (i + 1) * 16)
                        act.activation(yo[0:TH, a, e, :], bank[4 + a][0:TH, 0:D], ACT.Copy).then_inc(s_yo, 1)
                act.wait_ge(s_sc, i + 1)
                act.activation(rr[:, :, :], sc2[:, :, :], ACT.Exp)
                act.activation(ww[:, :, :], sc[:, :, :], ACT.Exp).then_inc(s_ww, 1)

            act.wait_ge(s_ce, 1)
            act.activation(crow[:, 4, 0:P], crow[:, 4, 0:P], ACT.Exp)
            act.activation(crow[:, 5, 0:P], crow[:, 5, 0:P], ACT.Exp).then_inc(s_cx, 1)
            act.wait_ge(s_fe, 1)
            act.activation(fx[:, 1:3, :], fx[:, 1:3, :], ACT.Exp).then_inc(s_fx, 1)
            act.wait_ge(s_ma, 1)
            act.activation(f4[2], f4[2], ACT.Exp)
            act.activation(f4[3], f4[3], ACT.Exp).then_inc(s_mx, 1)
            act.wait_ge(s_sqv, 1)
            act.activation(t49[:, 0, :], t49[:, 0, :], ACT.Sqrt, bias=eps[:, :], scale=1.0).then_inc(s_sqa, 1)
            act.wait_ge(s_ma, 2)
            act.activation(f4[2], f4[2], ACT.Exp).then_inc(s_mx, 1)

        @block.vector
        def _(dve):
            v = Chain(dve, s_v)
            fb = ROWB - 1
            dve.memset(xa[:, NT - 1, :], 0.0)
            dve.memset(eint[:, fb, 0, :], 0)
            dve.memset(eint[:, fb, 1, :], N - 1)
            dve.memset(erow[:, fb, 2, :], 0.0).then_inc(s_fill, 1)
            dve.memset(zero[:, :], 0.0).then_inc(s_zero, 1)
            dve.memset(eps[:, :], EPS)
            dve.memset(onesb[:, :], 1.0).then_inc(s_cstv, 1)
            dve.memset(lo[:, RUN:RUN + HT], 0.0)
            dve.memset(hi[:, RUN:RUN + HT], 0.0)
            dve.memset(keyp[0:1, :], -1.0)
            dve.memset(pay[:, RUN:RUN + CH, :], 0.0)
            dve.memset(sinkrow[:, H:W], 0.0)
            dve.memset(sinkrow[:, 0:H], -BIG).then_inc(s_zero, 1)
            dve.wait_ge(s_cst, 2)
            dve.tensor_copy(iof[:, :], iot[:, :])
            dve.tensor_copy(iob[:, :], iot[:, :])
            dve.tensor_copy(pidf[:, :], pidx[:, :])
            v(dve.tensor_copy(identb[:, :], ident[:, :]))
            dve.wait_ge(s_edge, 16 * 9)
            v.mark(dve.tensor_scalar(erow[:, :, 0, :], eint[:, :, 0, :], float(N - 1), 0.0, ALU.min, ALU.max))
            dve.tensor_copy(erow[:, :, 1, :], eint[:, :, 1, :]).then_inc(s_rows, 1)
            v(dve.tensor_single_scalar(lwin[:, :], eint[:, :, 1, P - 1], 7, ALU.arith_shift_right))
            v(dve.tensor_scalar(lv[:, :], lwin[:, :], 0.0, float(NT - 1), ALU.max, ALU.min))
            v(dve.scalar_tensor_tensor(lv[:, :], lv[:, :], 1.0, pidf[:, :], ALU.add, ALU.add))
            for c in range(ROWB):
                ins = dve.tensor_scalar(before[:, c, :], iokb[:, :], lv[:, c:c + 1], None, ALU.is_ge)
            ins.then_inc(s_bef, 1)
            dve.wait_ge(s_x, 32)
            for n in range(NT):
                ins = dve.bn_stats(st1[:, n, :], xa[:, n, :])
            v(ins)
            for n in range(NT):
                ins = dve.bn_aggr(mv1[:, n, :], st1[:, n, :])
            ins.then_inc(s_sd1, 1)
            dve.wait_ge(s_sd1, 2)
            v(dve.reciprocal(rs1[:, :], sd1[:, :]))
            dve.scalar_tensor_tensor(nb1[:, :], mv1[:, :, 0], -1.0, rs1[:, :], ALU.mult, ALU.mult).then_inc(s_rs1, 1)
            dve.wait_ge(s_ik, 1)
            v(dve.tensor_copy(ikf[:, :], bank[0][:, 0:ROWB]))
            dve.tensor_copy(iku[:, :], ikf[:, :]).then_inc(s_iku, 1)
            v(dve.tensor_tensor(jkf[:, :], pidf[:, :], ikf[:, :], ALU.subtract))
            v(dve.tensor_scalar(jkf[:, :], jkf[:, :], float(NT - 1), float(P), ALU.min, ALU.mult))
            dve.tensor_copy(jki[:, :], jkf[:, :]).then_inc(s_win, 1)
            dve.wait_ge(s_strow, 16 * ROWB)
            for c in range(ROWB):
                ins = dve.tensor_scalar(strow[:, c, 1, :], strow[:, c, 1, :], jkf[:, c:c + 1], None, ALU.subtract)
            ins.then_inc(s_dl, 1)
            for q in range(3):
                dve.wait_ge(s_tr, q + 1)
                v.mark(dve.tensor_copy(stcol[:, q, 0:4 * P], bank[1 + 2 * q][:, :]))
                v.mark(dve.tensor_copy(stcol[:, q, 4 * P:ROWB * P], bank[2 + 2 * q][:, 0:(ROWB - 4) * P]))
            v.wait()
            v(dve.tensor_copy(step_src, stcol[:, 0, :]))
            dve.wait_ge(s_gat, 32)
            v.mark(dve.tensor_scalar(pay[:, 0:RUN, 1], sint[:, :], float(N - 1), 0.0, ALU.min, ALU.max))
            v(dve.tensor_scalar(pay[:, 0:RUN, 0], kint[:, :], 0.0, 2.0**33, ALU.is_lt, ALU.mult))
            v(dve.tensor_tensor(pay[:, 0:RUN, 0], pay[:, 0:RUN, 0], kint[:, :], ALU.add))
            v(dve.tensor_scalar(pay[:, 0:RUN, 0], pay[:, 0:RUN, 0], float(N), None, ALU.min))
            v(dve.tensor_copy(kint[:, :], pay[:, 0:RUN, 0]))
            v(dve.tensor_single_scalar(sint[:, :], kint[:, :], P - 1, ALU.bitwise_and))
            v(dve.tensor_copy(lo[:, 0:RUN], sint[:, :]))
            v(dve.tensor_single_scalar(sint[:, :], kint[:, :], 7, ALU.arith_shift_right))
            v(dve.tensor_copy(hi[:, 0:RUN], sint[:, :]))
            dve.wait_ge(s_par, 16 * 16)
            S8 = D // 8
            for q in range(8):
                r = slice(32 * (q % 4), 32 * (q % 4) + 32)
                for p in range(8):
                    j = IDX[p][q]
                    dve.tensor_scalar(ham[r, q // 4, p * S8:(p + 1) * S8], ham4[r, j * S8:(j + 1) * S8],
                                      float(SIGN[p][q]), None, ALU.mult)
            for k in range(KD):
                for q in range(2):
                    v(dve.tensor_tensor(wt[:, :], wg[:, k, 0:HE], attb[:, q, :], ALU.mult))
                    v(dve.tensor_reduce(wg[:, k, HE + q * H:HE + (q + 1) * H], wt[:, :].rearrange("p (h e) -> p h e", h=H),
                                        AX.X, ALU.add))
            v(dve.memset(regB[:, :], 0.0))
            for hf in range(2):
                dve.tensor_copy(idxr[:, hf, 0:HS], step_src[:, hf * HS:(hf + 1) * HS]).then_inc(s_idx, 1)
            regs = [dve.alloc_register(f"win{s}") for s in range(HS)]
            dve.wait_ge(s_wind, 32)
            with dve.Fori(0, TURNS) as i:
                for hf in range(2):
                    dve.wait_ge(s_hist, i * 2 + (hf + 1))
                    at = i * CH + hf * HT
                    dve.tensor_tensor(ol[:, hf, :, :], every(iob[:, :], HT), each(lo[:, bass.ds(at, HT)], P), ALU.is_equal)
                    dve.tensor_tensor(oh[:, hf, :, :], every(iob[:, 0:NT], HT), each(hi[:, bass.ds(at, HT)], NT),
                                      ALU.is_equal).then_inc(s_oh, 1)
                    for s in range(HS):
                        k = i * (2 * HS) + (hf * HS + s)
                        ins = dve.tensor_scalar(onehot[:, hf, s, :], iof[:, :], stcol[:, 1, bass.ds(k, 1)],
                                                stcol[:, 2, bass.ds(k, 1)], ALU.is_equal, ALU.mult)
                    ins.then_inc(s_sel, 1)
                for hf in range(2):
                    dve.load(regs, wins[0:1, bass.ds(i * 2 + hf, 1), 0:HS])
                    for s in range(HS):
                        k = i * (2 * HS) + (hf * HS + s)
                        w = dve.snap(regs[s], min_val=0, max_val=(NT - 1) * P)
                        dve.wait_ge(s_step, k + 1)
                        dve.wait_ge(s_acc, k + SB)
                        dve.tensor_tensor(acc[:, :, bass.ds(w, P)], acc[:, :, bass.ds(w, P)],
                                          slot(s).rearrange("p (k n) -> p k n", k=KD), ALU.add).then_inc(s_acc, 1)
                    dve.tensor_copy(idxr[:, hf, 0:HS], step_src[:, bass.ds((i + 1) * (2 * HS) + hf * HS, HS)]).then_inc(s_idx, 1)
            dve.wait_ge(s_hist, 2 * TURNS + 2)
            dve.tensor_copy(cnt[:, :], bank[7][:, 0:NT]).then_inc(s_cnt, 1)
            dve.memset(totx[:, 0:1], 0.0)
            dve.wait_ge(s_pre, 1)
            v(dve.tensor_copy(tots[:, :], bank[6][:, 64:64 + NT]))
            v(dve.tensor_tensor_scan(totx[:, 1:NT + 1], ones[:, 0:NT], tots[:, :], 0.0, ALU.mult, ALU.add))
            v(dve.tensor_tensor(basef[:, :], bank[6][:, 0:NT], totx[:, 0:NT], ALU.add))
            dve.tensor_copy(run4[:, GT - 1, GT - 1, :], basef[:, :]).then_inc(s_t0, 1)

            def onehots(half, hf):
                dve.tensor_tensor(ol[:, hf, :, :], every(iob[:, :], HT), each(lo[:, bass.ds(half * HT, HT)], P), ALU.is_equal)
                dve.tensor_tensor(oh[:, hf, :, :], every(iob[:, 0:NT], HT), each(hi[:, bass.ds(half * HT, HT)], NT),
                                  ALU.is_equal).then_inc(s_ol, 1)

            onehots(0, 0)
            for b in range(CB):
                w = min(512, N - b * 512)
                dve.wait_ge(s_bc, b + 1)
                for m in range(KD):
                    ins = dve.bn_stats(stb[:, m, b, :], gnn[:, m, b * 512:b * 512 + w])
                ins.then_inc(s_bn, 1)
            dve.wait_ge(s_bn, CB)
            for m in range(KD):
                ins = dve.bn_aggr(mvb[:, m, :], stb[:, m, :, :])
            ins.then_inc(s_sdb, 1)
            dve.wait_ge(s_sdb, 2)
            v(dve.reciprocal(sdb[:, :], sdb[:, :]))
            v(dve.tensor_tensor(scb[:, :], sdb[:, :], gam[:, :], ALU.mult))
            v(dve.tensor_tensor(bib[:, :], mvb[:, :, 0], scb[:, :], ALU.mult))
            dve.tensor_tensor(bib[:, :], bet[:, :], bib[:, :], ALU.subtract).then_inc(s_bnr, 1)

            NG = HT // GT

            def rank(i, hf, gi):
                G = i * (2 * NG) + (hf * NG + gi)
                if gi == 0:
                    if not isinstance(i, int):
                        dve.wait_ge(s_scat[hf], i * (16 * HT))
                    dve.tensor_copy(payr[:, hf, :, :], pay[:, bass.ds(i * CH + hf * HT, HT), :])
                    onehots(i * 2 + (hf + 1), 1 - hf)
                dve.wait_ge(s_eq, G + 1)
                dve.tensor_tensor(ub[:, :, :], bank[2][:, :].rearrange("p (a b) -> p a b", a=GT), every(above[:, :], GT),
                                  ALU.mult).then_inc(s_u, 1)
                dve.wait_ge(s_g, G + 4)
                g0 = gi * GT
                dve.tensor_tensor(gm[:, :, :], bank[4][:, 0:GT * NT].rearrange("p (a b) -> p a b", a=GT),
                                  oh[:, hf, g0:g0 + GT, :], ALU.mult).then_inc(s_gm, 1)
                dve.wait_ge(s_gm, G + 2)
                with nc.allow_low_precision(reason="whole numbers below 2**24, summed in float32"):
                    dve.tensor_reduce(posr[:, hf, g0:g0 + GT], gm[:, :, :], AX.X, ALU.add).then_inc(s_pos, 1)

            def node(n, gi):
                if gi == 0:
                    dve.wait_ge(s_px, n + 3)
                    v(dve.bn_stats(stn[:, :], bank[5][:, 0:D]))
                    dve.sem_inc(s_begun_v, 1)
                    dve.bn_aggr(mvn[:, :], stn[:, :]).then_inc(s_mvn, 1)
                if gi == 1:
                    dve.wait_ge(s_sdn, n + 1)
                    v(dve.reciprocal(rsn[:, :], sdn[:, :]))
                    dve.scalar_tensor_tensor(nbn[:, :], mvn[:, 0:1], -1.0, rsn[:, :], ALU.mult, ALU.mult).then_inc(s_rsn, 1)

            def ranks_and_nodes(i):
                for hf in range(2):
                    for gi in range(NG):
                        if gi == 1:
                            node(i * 2 + hf, gi)
                        rank(i, hf, gi)
                        if gi == 0:
                            node(i * 2 + hf, gi)

            ranks_and_nodes(0)
            with v.loop(1, (NT - 1) // 2, 4) as i:
                ranks_and_nodes(i)
            node(NT - 1, 0)
            node(NT - 1, 1)
            v(dve.tensor_scalar(t49[:, 0, :], cnt[:, :], 0.0, None, ALU.is_equal))
            v(dve.tensor_scalar(t49[:, 1, :], pidf[:, 0:1].to_broadcast([P, NT]), float(E2), None, ALU.add))
            v(dve.tensor_scalar(t49[:, 2, :], iof[:, 0:NT], float(P), None, ALU.mult))
            v(dve.tensor_tensor(t49[:, 1, :], t49[:, 1, :], t49[:, 2, :], ALU.add))
            v(dve.tensor_tensor(t49[:, 1, :], t49[:, 1, :], basef[:, :], ALU.subtract))
            v(dve.tensor_tensor(t49[:, 1, :], t49[:, 1, :], t49[:, 0, :], ALU.mult))
            v(dve.tensor_tensor(sidx[:, :], t49[:, 1, :], basef[:, :], ALU.add))
            v(dve.tensor_tensor(t49[:, 1, :], basef[:, :], cnt[:, :], ALU.add))
            v(dve.tensor_scalar(t49[:, 1, :], t49[:, 1, :], -1.0, None, ALU.add))
            v(dve.tensor_scalar(t49[:, 2, :], t49[:, 1, :], -1.0, float(SINK), ALU.mult, ALU.add))
            v(dve.tensor_tensor(t49[:, 2, :], t49[:, 2, :], t49[:, 0, :], ALU.mult))
            dve.tensor_tensor(eidx[:, :], t49[:, 1, :], t49[:, 2, :], ALU.add).then_inc(s_seidx, 1)
            with dve.Fori((NT - 1) // 2, RT) as i:
                for hf in range(2):
                    for gi in range(NG):
                        rank(i, hf, gi)

            dve.wait_ge(s_srt, 32)
            v(dve.tensor_copy(key0[:, :], pay[:, 0, 0:1]))
            dve.tensor_copy(key0u[:, :], key0[:, :]).then_inc(s_k0, 1)
            v.mark(dve.tensor_tensor(keep[:, 1:RUN], pay[:, 1:RUN, 0], pay[:, 0:RUN - 1, 0], ALU.is_equal))
            v(dve.tensor_tensor(keep[:, 0:1], key0[:, :], keyp[:, :], ALU.is_equal))
            v.mark(dve.tensor_scalar(neg[:, :], keep[:, :], -1.0, BIG, ALU.add, ALU.mult))
            v(dve.tensor_scalar(same[:, :], pay[:, 0:RUN, 0], key0[:, :], None, ALU.is_equal))
            for hf in range(2):
                dve.tensor_copy(gidx[:, hf, :], pay[:, hf * HT:(hf + 1) * HT, 1]).then_inc(s_gidx, 1)
            v(dve.tensor_reduce(nfirst[:, :], same[:, :], AX.X, ALU.add))
            v(dve.tensor_scalar(cf[:, 0:1], pidf[:, 0:1], float(RUN), -1.0, ALU.mult, ALU.add))
            dve.tensor_tensor(fidx[:, :], cf[:, 0:1], nfirst[:, :], ALU.add).then_inc(s_fidx, 1)
            dve.wait_ge(s_arow, 16)
            dve.wait_ge(s_adr, 16)
            for h in range(H):
                v.mark(dve.tensor_tensor_scan(adst[:, h, :], keep[:, :], adraw[:, :, h], arow[:, HE + H + h:HE + H + h + 1],
                                              ALU.mult, ALU.add))
            v.mark(dve.memset(last[:, 0:H], -BIG))
            v(dve.memset(last[:, H:W], 0.0))

            def chunk(i, j):
                t = i * 2 + j
                for hf in range(2):
                    dve.wait_ge(s_grow[hf], (t + 1) * (16 * HT))
                    v.mark(dve.tensor_copy(hc[:, :, hf * HT:(hf + 1) * HT], grow[:, hf, :, :].rearrange("p t w -> p w t")))
                v.wait()
                for hf in range(2):
                    dve.tensor_copy(gidx[:, hf, :], pay[:, bass.ds((t + 1) * CH + hf * HT, HT), 1]).then_inc(s_gidx, 1)
                tc = bass.ds(t * CH, CH)
                v(dve.tensor_tensor(sc[:, :, :], hc[:, HE:HE + H, :], adst[:, :, tc], ALU.add))
                v(dve.scalar_tensor_tensor(sc[:, :, :], sc[:, :, :], 0.2, sc[:, :, :], ALU.mult, ALU.max))
                v(dve.tensor_copy(mb[:, :, 0], last[:, 0:H]))
                for h in range(H):
                    v.mark(dve.tensor_tensor_scan(mb[:, h, 1:CH + 1], neg[:, tc], sc[:, h, :], last[:, h:h + 1], ALU.add, ALU.max))
                v.wait()
                v(dve.tensor_tensor(sc2[:, :, :], mb[:, :, 0:CH], every(neg[:, tc], H), ALU.add))
                v.mark(dve.tensor_tensor(sc2[:, :, :], sc2[:, :, :], mb[:, :, 1:CH + 1], ALU.subtract))
                v(dve.tensor_tensor(sc[:, :, :], sc[:, :, :], mb[:, :, 1:CH + 1], ALU.subtract))
                dve.sem_inc(s_sc, 1)
                dve.wait_ge(s_ww, t + 1)
                dve.wait_ge(s_lcd[j], (i + 1) * 16)
                v(dve.tensor_tensor(nm[:, :, :].rearrange("p (h e) t -> p h e t", h=H),
                                    hc[:, 0:HE, :].rearrange("p (h e) t -> p h e t", h=H),
                                    ww[:, :, :].unsqueeze(2).to_broadcast([P, H, NE, CH]), ALU.mult))
                for h in range(H):
                    v.mark(dve.tensor_tensor_scan(lc[:, j, :, H + h], rr[:, h, :], ww[:, h, :], last[:, H + h:H + h + 1],
                                                  ALU.mult, ALU.add))
                for f in range(HE):
                    v.mark(dve.tensor_tensor_scan(lc[:, j, :, 2 * H + f], rr[:, f // NE, :], nm[:, f, :],
                                                  last[:, 2 * H + f:2 * H + f + 1], ALU.mult, ALU.add))
                v(dve.tensor_copy(lc[:, j, :, 0:H], mb[:, :, 1:CH + 1].rearrange("p h t -> p t h")))
                v.mark(dve.tensor_copy(last[:, :], lc[:, j, CH - 1, :]))
                dve.wait_ge(s_v, v.value())
                dve.sem_inc(s_lc, 1)
            per = 2 * (2 + 1 + 1 + 1 + H + 1 + 1 + 1 + 1 + H + HE + 1 + 1)
            with v.loop(0, TURNS // 2, per) as i:
                chunk(i, 0)
                chunk(i, 1)

            v.mark(dve.tensor_copy(cin[:, 0, 0:H], last[:, 0:H]))
            v.mark(dve.tensor_copy(cin[:, 0, H:LF].rearrange("p (h e) -> p h e", h=H), each(last[:, 0:H], NE)))
            v.mark(dve.tensor_copy(cin[:, 1, :], last[:, H:W]))
            v(dve.tensor_scalar(cf[:, 2:3], nfirst[:, :], float(RUN), None, ALU.is_equal))
            v(dve.tensor_tensor(cf[:, 2:3], cf[:, 2:3], keep[:, 0:1], ALU.mult))
            v(dve.tensor_scalar(cf[:, 2:3], cf[:, 2:3], -1.0, BIG, ALU.add, ALU.mult))
            v.mark(dve.tensor_copy(cin[:, 2, :], cf[:, 2:3].to_broadcast([P, LF])))
            dve.tensor_copy(cin[:, 3, :], neg[:, 0:1].to_broadcast([P, LF])).then_inc(s_cin, 1)
            dve.wait_ge(s_ctr, 1)
            v.mark(dve.tensor_copy(crow[:, 0:4, 0:P], bank[0][0:LF, :].rearrange("p (a b) -> p a b", a=4)))
            v.mark(dve.memset(crow[:, 6, 0:1], -BIG))
            v(dve.memset(crow[:, 7, 0:1], 0.0))
            v(dve.tensor_tensor_scan(crow[:, 6, 1:P + 1], crow[:, 2, 0:P], crow[:, 0, 0:P], -BIG, ALU.add, ALU.max))
            v(dve.tensor_tensor(crow[:, 4, 0:P], crow[:, 6, 0:P], crow[:, 2, 0:P], ALU.add))
            v.mark(dve.tensor_tensor(crow[:, 4, 0:P], crow[:, 4, 0:P], crow[:, 6, 1:P + 1], ALU.subtract))
            v(dve.tensor_tensor(crow[:, 5, 0:P], crow[:, 0, 0:P], crow[:, 6, 1:P + 1], ALU.subtract))
            dve.sem_inc(s_ce, 1)
            dve.wait_ge(s_cx, 1)
            v(dve.tensor_tensor(crow[:, 1, 0:P], crow[:, 1, 0:P], crow[:, 5, 0:P], ALU.mult))
            v(dve.tensor_tensor_scan(crow[:, 7, 1:P + 1], crow[:, 4, 0:P], crow[:, 1, 0:P], 0.0, ALU.mult, ALU.add))
            dve.tensor_tensor(crow[:, 0, 0:P], crow[:, 6, 0:P], crow[:, 3, 0:P], ALU.add).then_inc(s_cb, 1)
            dve.wait_ge(s_cbt, 1)
            v(dve.tensor_copy(cout[:, :, :], bank[1][:, 0:2 * LF].rearrange("p (a b) -> p a b", a=2)))
            dve.wait_ge(s_frow, 16)
            v.mark(dve.tensor_copy(fx[:, 1, 0:H], frow[:, 0:H]))
            v(dve.tensor_copy(fx[:, 1, H:LF].rearrange("p (h e) -> p h e", h=H), each(frow[:, 0:H], NE)))
            v(dve.tensor_tensor(fx[:, 0, :], fx[:, 1, :], cout[:, 0, :], ALU.max))
            v.mark(dve.tensor_tensor(fx[:, 1, :], fx[:, 1, :], fx[:, 0, :], ALU.subtract))
            v(dve.tensor_tensor(fx[:, 2, :], cout[:, 0, :], fx[:, 0, :], ALU.subtract))
            dve.sem_inc(s_fe, 1)
            dve.wait_ge(s_fx, 1)
            v.mark(dve.tensor_tensor(fx[:, 1, :], fx[:, 1, :], frow[:, H:W], ALU.mult))
            v(dve.tensor_tensor(fx[:, 2, :], fx[:, 2, :], cout[:, 1, :], ALU.mult))
            v.mark(dve.tensor_tensor(arow[:, H:W], fx[:, 1, :], fx[:, 2, :], ALU.add))
            dve.tensor_copy(arow[:, 0:H], fx[:, 0, 0:H]).then_inc(s_fst, 1)

            def h3(ap):
                return ap.rearrange("p (n h) -> p n h", h=H)

            def he(ap):
                return ap.rearrange("p (n f) -> p n f", f=HE)

            def bc(ap):
                return each(ap, NE)

            v(dve.tensor_tensor(h3(f4[0]), tab[:, :, HE:HE + H], tab[:, :, HE + H:W], ALU.add))
            v(dve.scalar_tensor_tensor(f4[0], f4[0], 0.2, f4[0], ALU.mult, ALU.max))
            dve.wait_ge(s_esum, 16 * NT)
            v(dve.tensor_tensor(h3(f4[1]), esum[:, :, 0:H], h3(f4[0]), ALU.max))
            v.mark(dve.tensor_tensor(h3(f4[2]), esum[:, :, 0:H], h3(f4[1]), ALU.subtract))
            v(dve.tensor_tensor(f4[3], f4[0], f4[1], ALU.subtract))
            dve.sem_inc(s_ma, 1)
            dve.wait_ge(s_mx, 1)
            v(dve.tensor_tensor(h3(f4[4]), esum[:, :, H:2 * H], h3(f4[2]), ALU.mult))
            v(dve.tensor_tensor(f4[4], f4[4], f4[3], ALU.add))
            v(dve.tensor_scalar(f4[4], f4[4], 1e-16, None, ALU.add))
            v(dve.reciprocal(f4[4], f4[4]))
            v.mark(dve.tensor_copy(he(fin[0]), esum[:, :, 2 * H:W]))
            v(dve.tensor_copy(he(fin[1]), tab[:, :, 0:HE]))

            def g3(ap):
                return ap.rearrange("p (g e) -> p g e", e=NE)

            v.mark(dve.tensor_tensor(g3(fin[0]), g3(fin[0]), bc(f4[2]), ALU.mult))
            v(dve.tensor_tensor(g3(fin[1]), g3(fin[1]), bc(f4[3]), ALU.mult))
            v(dve.tensor_tensor(fin[0], fin[0], fin[1], ALU.add))
            v(dve.tensor_tensor(g3(fin[0]), g3(fin[0]), bc(f4[4]), ALU.mult))
            v(dve.tensor_tensor(he(fin[0]), he(fin[0]), every(gatp[:, 0, :], NT), ALU.add))
            v(dve.tensor_reduce(t49[:, 1, :], he(fin[0]), AX.X, ALU.add))
            v(dve.tensor_scalar(t49[:, 1, :], t49[:, 1, :], 1.0 / HE, None, ALU.mult))
            v(dve.tensor_tensor(he(fin[0]), he(fin[0]), each(t49[:, 1, :], HE), ALU.subtract))
            v(dve.tensor_tensor(fin[1], fin[0], fin[0], ALU.mult))
            v(dve.tensor_reduce(t49[:, 0, :], he(fin[1]), AX.X, ALU.add))
            v(dve.tensor_scalar(t49[:, 0, :], t49[:, 0, :], 1.0 / HE, None, ALU.mult))
            dve.sem_inc(s_sqv, 1)
            dve.wait_ge(s_sqa, 1)
            v(dve.reciprocal(t49[:, 0, :], t49[:, 0, :]))
            v(dve.tensor_tensor(he(fin[0]), he(fin[0]), each(t49[:, 0, :], HE), ALU.mult))
            v(dve.tensor_tensor(he(fin[0]), he(fin[0]), every(gatp[:, 1, :], NT), ALU.mult))
            v(dve.tensor_tensor(he(fin[0]), he(fin[0]), every(gatp[:, 2, :], NT), ALU.add))
            v(dve.tensor_reduce(f4[0], fin[0].rearrange("p (n h e) -> p n e h", h=H, e=NE), AX.X, ALU.add))
            v(dve.tensor_scalar(f4[0], f4[0], 1.0 / H, None, ALU.mult))
            sco = f4[0].rearrange("p (n e) -> p n e", e=NE)
            rk = f4[1].rearrange("p (n e) -> p n e", e=NE)
            v(dve.memset(f4[1], 0.0))
            for a in range(NE):
                for b in range(a + 1, NE):
                    v(dve.tensor_tensor(t49[:, 2, :], sco[:, :, b], sco[:, :, a], ALU.is_gt))
                    v.mark(dve.tensor_tensor(rk[:, :, a], rk[:, :, a], t49[:, 2, :], ALU.add))
                    v(dve.tensor_scalar(t49[:, 3, :], t49[:, 2, :], -1.0, 1.0, ALU.mult, ALU.add))
                    v(dve.tensor_tensor(rk[:, :, b], rk[:, :, b], t49[:, 3, :], ALU.add))
            v(dve.tensor_reduce(t49[:, 2, :], sco, AX.X, ALU.max))
            v(dve.tensor_tensor(f4[2].rearrange("p (n e) -> p n e", e=NE), sco, each(t49[:, 2, :], NE), ALU.subtract))
            dve.sem_inc(s_ma, 1)
            dve.wait_ge(s_mx, 2)
            v(dve.tensor_scalar(f4[1], f4[1], 1.5, None, ALU.is_lt))
            v(dve.tensor_tensor(f4[1], f4[1], f4[2], ALU.mult))
            v(dve.tensor_reduce(t49[:, 2, :], rk, AX.X, ALU.add))
            v(dve.reciprocal(t49[:, 2, :], t49[:, 2, :]))
            v(dve.tensor_tensor(rk, rk, each(t49[:, 2, :], NE), ALU.mult))
            for n in range(NT):
                b, m = n % YR, (P if n < NT - 1 else LAST)
                dve.wait_ge(s_yl[b], 32 * (n // YR + 1))
                for e in range(NE):
                    ins = dve.scalar_tensor_tensor(xin2[0:m, b, :], yin[0:m, b, e, :], rk[0:m, n, e:e + 1], xin2[0:m, b, :],
                                                   ALU.mult, ALU.add)
                    if e < NE - 1:
                        v(ins)
                ins.then_inc(s_cmb, 1)

        @block.tensor
        def _(pe):
            pe.wait_ge(s_bef, 1)
            pe.wait_ge(s_cstv, 1)
            for k in range(ROWB):
                for c in range(ROWB):
                    ins = pe.matmul(bank[0][:, k:k + 1], before[:, c, k * P:(k + 1) * P], onesb[:, :], start=c == 0, stop=c == ROWB - 1)
            ins.then_inc(s_ik, 1)
            pe.wait_ge(s_dl, 1)
            pe.wait_ge(s_cst, 2)
            for q in range(3):
                for c in range(ROWB):
                    ins = pe.transpose(bank[1 + 2 * q + c // 4][:, (c % 4) * P:(c % 4 + 1) * P], strow[:, c, q, :], ident[:, :])
                ins.then_inc(s_tr, 1)
            pe.wait_ge(s_zero, 1)
            pe.matmul(bank[7][:, 0:NT], zero[:, 0:P], zero[:, 0:NT], start=True, stop=False, skip_group_check=True)
            with pe.Fori(0, TURNS) as i:
                for hf in range(2):
                    pe.wait_ge(s_oh, i * 2 + (hf + 1))
                    for t in range(HT):
                        ins = pe.matmul(bank[7][:, 0:NT], ol[:, hf, t, :], oh[:, hf, t, :], start=False, stop=False, skip_group_check=True)
                    ins.then_inc(s_hist, 1)
                    pe.wait_ge(s_row[hf], (i + 1) * (16 * HS))
                    pe.wait_ge(s_sel, i * 2 + (hf + 1))
                    for s in range(HS):
                        pe.wait_ge(s_acc, i * (2 * HS) + (hf * HS + s + 1))
                        for m in range(KD):
                            ins = pe.matmul(slot(s)[:, m * P:(m + 1) * P], rows[:, hf, s, m * P:(m + 1) * P],
                                            onehot[:, hf, s, :], start=True, stop=True)
                        ins.then_inc(s_step, 1)
            pe.wait_ge(s_cnt, 1)
            pe.wait_ge(s_acc, 2 * HS * TURNS + SB)
            pe.matmul(bank[6][:, 0:NT], above[:, :], cnt[:, :], start=True, stop=True)
            pe.matmul(bank[6][:, 64:64 + NT], ones[:, :], cnt[:, :], start=True, stop=True).then_inc(s_pre, 1)
            for b in range(CB):
                w = min(512, NP - b * 512)
                if b >= 2:
                    pe.wait_ge(s_bc, b - 1)
                for m in range(KD):
                    for k in range(KD):
                        ins = pe.matmul(bank[m + 2 * (b % 2)][:, 0:w], ham[:, k, m * P:(m + 1) * P], acc[:, k, b * 512:b * 512 + w],
                                        start=k == 0, stop=k == KD - 1)
                ins.then_inc(s_bo, 1)
            pe.wait_ge(s_bc, CB)

            NG = HT // GT

            def transposes(hf, gi, par):
                for t in range(GT):
                    ins = pe.transpose(bank[par][:, :].bitcast(bf16)[:, t * P:(t + 1) * P], ol[:, hf, gi * GT + t, :], identb[:, :])
                ins.then_inc(s_trp, 1)

            def rank(i, hf, gi):
                G = i * (2 * NG) + (hf * NG + gi)
                g0 = gi * GT
                prev = run4[:, (gi - 1) % GT, GT - 1, :]
                pe.wait_ge(s_t, G + 1)
                pe.matmul(bank[3][:, 0:GT * NT], ident[:, :], every(prev, GT), start=True, stop=False, skip_group_check=True)
                for t in range(GT):
                    ins = pe.matmul(bank[3][:, t * NT:GT * NT], ol[:, hf, g0 + t, :], every(oh[:, hf, g0 + t, :], GT - t),
                                    start=False, stop=t == GT - 1, skip_group_check=True)
                ins.then_inc(s_r, 1)
                pe.wait_ge(s_olt, G + 1)
                pe.wait_ge(s_u, G + 1)
                for t in range(GT):
                    ins = pe.matmul(bank[2][:, t * P:(t + 1) * P], olt[:, gi % 2, t, :], olt[:, gi % 2, t, :], start=True, stop=True)
                ins.then_inc(s_eq, 1)
                if gi == NG - 1:
                    pe.wait_ge(s_ol, i * 2 + (hf + 2))
                transposes(hf if gi < NG - 1 else 1 - hf, (gi + 1) % NG, (gi + 1) % 2)
                pe.wait_ge(s_u, G + 2)
                pe.wait_ge(s_t, G + 2)
                pe.wait_ge(s_gm, G + 1)
                for t in range(GT):
                    tb = prev if t == 0 else run4[:, gi, t - 1, :]
                    pe.matmul(bank[4][:, t * NT:(t + 1) * NT], olt[:, gi % 2, t, :], tb, start=True, stop=False, skip_group_check=True)
                    ins = pe.matmul(bank[4][:, t * NT:(t + 1) * NT], ub[:, t, :], oh[:, hf, g0 + t, :], start=False, stop=True,
                                    skip_group_check=True)
                ins.then_inc(s_g, 1)

            def node(n, hf, gi, turn):
                if gi == 0:
                    pe.wait_ge(s_xin[hf], (turn + 1) * 16)
                    pe.wait_ge(s_tt, n + 1)
                    pe.wait_ge(s_x3, n + 1)
                    pe.matmul(bank[5][:, 0:D], ident[:, :], xin[:, hf, :], start=True, stop=False, skip_group_check=True)
                    for m in range(KD):
                        ins = pe.matmul(bank[5][:, m * P:(m + 1) * P], tt[:, m, :], ident[:, :], start=False,
                                        stop=m == KD - 1, skip_group_check=True)
                    ins.then_inc(s_px, 1)
                if gi == 2:
                    pe.wait_ge(s_x3, n + 2)
                    for m in range(KD):
                        ins = pe.transpose(bank[6][:, m * P:(m + 1) * P], x3[:, hf, m * P:(m + 1) * P], ident[:, :])
                    ins.then_inc(s_x3t, 1)
                if gi == 3:
                    pe.wait_ge(s_x3c, n + 1)
                    for k in range(KD):
                        ins = pe.matmul(bank[7][:, 0:W], xt[:, k, :], wg[:, k, :], start=k == 0, stop=k == KD - 1)
                    ins.then_inc(s_tabp, 1)

            pe.wait_ge(s_t0, 1)
            pe.wait_ge(s_ol, 1)
            pe.wait_ge(s_tanh, 1)
            transposes(0, 0, 0)
            with pe.Fori(0, (NT - 1) // 2) as i:
                for hf in range(2):
                    for gi in range(NG):
                        node(i * 2 + hf, hf, gi, i)
                        rank(i, hf, gi)
            for gi in range(NG):
                node(NT - 1, 0, gi, (NT - 1) // 2)
            with pe.Fori((NT - 1) // 2, RT) as i:
                for hf in range(2):
                    for gi in range(NG):
                        rank(i, hf, gi)

            pe.wait_ge(s_wexp, 16 * (2 * NE + 1))
            pe.wait_ge(s_olt, RT * 2 * NG + 1)
            pe.wait_ge(s_gm, RT * 2 * NG + 1)
            pe.wait_ge(s_x3c, NT)
            with pe.Fori(0, TURNS) as i:
                for e in range(NE):
                    for m in range(MF):
                        k0 = i * (NE * MF) + (e * MF + m)
                        pe.wait_ge(s_hh, k0 + 1)
                        for k in range(KD):
                            ins = pe.matmul(bank[m][:, 0:TB], w1s[:, e, k, m * P:(m + 1) * P], x3T[:, k, bass.ds(i * TB, TB)],
                                            start=k == 0, stop=k == KD - 1)
                        ins.then_inc(s_up, 1)
                    pe.wait_ge(s_hh, i * (NE * MF) + ((e + 2) * MF))
                    for a in range(2):
                        pe.wait_ge(s_yo, i * (2 * NE) + (2 * e + a + 1))
                        for k in range(MF):
                            pe.matmul(bank[4 + a][0:TH, 0:D], hh[:, k, a * TH:(a + 1) * TH], w2s[:, e, k, :], start=k == 0, stop=False)
                        ins = pe.matmul(bank[4 + a][0:TH, 0:D], ones[0:1, 0:TH], b2s[0:1, e, :], start=False, stop=True)
                        ins.then_inc(s_dn, 1)
            pe.wait_ge(s_cin, 1)
            for q in range(4):
                ins = pe.transpose(bank[0][0:LF, q * P:(q + 1) * P], cin[:, q, :], ident[:, :])
            ins.then_inc(s_ctr, 1)
            pe.wait_ge(s_cb, 1)
            pe.transpose(bank[1][:, 0:LF], crow[:, 0, 0:P], ident[0:LF, 0:LF])
            pe.transpose(bank[1][:, LF:2 * LF], crow[:, 7, 0:P], ident[0:LF, 0:LF]).then_inc(s_cbt, 1)


_INS = ["x", "src", "dst", "edge_weight", "L0_gnn_weight", "L0_gnn_gamma", "L0_gnn_beta", "L0_ffn_W_gat",
        "L0_ffn_att_src", "L0_ffn_att_dst", "L0_ffn_b_gat", "L0_ffn_ln_gamma", "L0_ffn_ln_beta", "L0_ffn_W1",
        "L0_ffn_b1", "L0_ffn_W2", "L0_ffn_b2", "L0_ffn_edge_index"]


def kernel(**inputs):
    import numpy as _np
    import concourse.bacc as _bacc
    from concourse import mybir as _mybir
    from concourse.bass_utils import run_bass_kernel_spmd as _run

    nc = _bacc.Bacc("TRN2", target_bir_lowering=False, num_devices=1)
    arrays, args = {}, []
    for name in _INS:
        a = _np.ascontiguousarray(inputs[name])
        arrays[f"in_{name}_dram"] = a
        args.append(nc.dram_tensor(f"in_{name}_dram", a.shape, _mybir.dt.from_np(a.dtype), kind="ExternalInput").ap())
    shape = inputs["x"].shape
    args.append(nc.dram_tensor("out_0_dram", shape, _mybir.dt.float32, kind="ExternalOutput").ap())
    gnn_moe(nc, *args)
    r = _run(nc, [arrays], core_ids=[0])
    return r.results[0]["out_0_dram"]
```

```python
import concourse.bass as bass
import concourse.mybir as mybir
from contextlib import ExitStack, contextmanager

P = 128
IDX = [[0, 1, 2, 3, 4, 5, 6, 7], [1, 0, 3, 2, 5, 4, 7, 6], [2, 3, 0, 1, 6, 7, 4, 5], [3, 2, 1, 0, 7, 6, 5, 4],
       [4, 5, 6, 7, 0, 1, 2, 3], [5, 4, 7, 6, 1, 0, 3, 2], [6, 7, 4, 5, 2, 3, 0, 1], [7, 6, 5, 4, 3, 2, 1, 0]]
SIGN = [[1, 1, 1, 1, 1, 1, 1, 1], [1, -1, 1, -1, 1, -1, -1, 1], [1, -1, -1, 1, 1, 1, -1, -1],
        [1, 1, -1, -1, 1, -1, 1, -1], [1, -1, -1, -1, -1, 1, 1, 1], [1, 1, -1, 1, -1, -1, -1, 1],
        [1, 1, 1, -1, -1, 1, -1, -1], [1, -1, 1, 1, -1, -1, 1, -1]]
BIG = 1e30
EPS = 1e-5


class Chain:

    def __init__(self, eng, sem):
        self.eng, self.sem, self.base, self.n, self.turn = eng, sem, 0, 0, None

    def value(self):
        return self.base + self.n if self.turn is None else self.turn + (self.base + self.n)

    def __call__(self, ins):
        self.mark(ins)
        self.wait()

    def mark(self, ins):
        ins.then_inc(self.sem, 1)
        self.n += 1

    def wait(self):
        self.eng.wait_ge(self.sem, self.value())

    @contextmanager
    def loop(self, first, end, per):
        self.base, self.n = self.base + self.n - first * per, 0
        with self.eng.Fori(first, end) as i:
            self.turn = i * per
            yield i
            assert self.n == per, (self.n, per)
        self.base, self.n, self.turn = self.base + end * per, 0, None


def gnn_moe(nc, x, src, dst, edge_weight, gnn_w, gnn_gamma, gnn_beta, w_gat, att_src, att_dst, b_gat,
            ln_gamma, ln_beta, w1, b1, w2, b2, edge_index, out):
    f32, bf16, i32, u32 = mybir.dt.float32, mybir.dt.bfloat16, mybir.dt.int32, mybir.dt.uint32
    ALU, ACT, AX = mybir.AluOpType, mybir.ActivationFunctionType, mybir.AxisListType

    N, D = x.shape
    NT = -(-N // P)
    NP = NT * P
    LAST = N - (NT - 1) * P
    E1 = src.shape[0]
    FULL = E1 // P
    REST = E1 - FULL * P
    ROWB = -(-(FULL + 1 + NT + 1) // P)
    STEPS = FULL + 1 + NT
    HS = 13
    TURNS = 32
    assert TURNS * 2 * HS >= STEPS and (TURNS + 1) * 2 * HS <= ROWB * P
    E2 = edge_index.shape[1]
    RUN = E2 // P
    GT = 4
    HT = 16
    RT = RUN // (2 * HT)
    assert RT == TURNS and RUN % (2 * HT) == 0
    CH = 2 * HT
    NE, FF = w1.shape[0], w1.shape[2]
    H = w_gat.shape[1] // NE
    HE = H * NE
    KD = D // P
    MF = FF // P
    TB = 2 * P
    FT = NP // TB
    assert FT * TB + P == NP and FT < TURNS and FT % 2 == 0
    LOADS = 7
    LN = NT // LOADS
    CT = 3
    LAG = 2
    N0 = CT + 2
    N1 = N0 + (NT - 1) // 2
    W = HE + 2 * H
    LF = H + HE
    SINK = E2

    def dram(name, shape, dt=f32):
        return nc.dram_tensor(name, shape, dt).ap()

    x1_d = dram("x1_d", [NP, D])
    rows_d = dram("rows_d", [ROWB * P, 3 * P])
    win_d = dram("win_d", [ROWB * P], i32)
    node_d = dram("node_d", [NP, W])
    x2_d = dram("x2_d", [NP, D])
    sorted_d = dram("sorted_d", [E2, 2])
    adst_d = dram("adst_d", [E2 + NP, H])
    sums_d = dram("sums_d", [E2 + 1, W])
    y_d = dram("y_d", [NP, NE, D])
    lastkey_d = dram("lastkey_d", [P, 1])

    ctx = ExitStack()
    with ctx:
        def sb(name, shape, dt=f32):
            return ctx.enter_context(nc.sbuf_tensor(name, shape, dt))

        def sem(name):
            return ctx.enter_context(nc.semaphore(name))

        regA = sb("regA", [P, NT * D])
        xa = regA[:, :].rearrange("p (n d) -> p n d", n=NT)
        gnn = regA[:, :].rearrange("p (k n) -> p k n", k=KD)
        regB = sb("regB", [P, NT * D])
        acc = regB[:, :].rearrange("p (k n) -> p k n", k=KD)
        x3T = acc
        regC = sb("regC", [P, 2 * HS * (D + P)])
        rows = regC[:, 0:2 * HS * D].rearrange("p (a s d) -> p a s d", a=2, s=HS)
        onehot = regC[:, 2 * HS * D:2 * HS * (D + P)].rearrange("p (a s d) -> p a s d", a=2, s=HS)
        w1s = regC[:, 0:NE * KD * FF].rearrange("p (e k f) -> p e k f", e=NE, k=KD)
        w2s = regC[:, NE * KD * FF:NE * KD * FF + NE * MF * D].rearrange("p (e k f) -> p e k f", e=NE, k=MF)
        iokb = regC[:, 0:ROWB * P].bitcast(i32)
        ham4 = regC[:, ROWB * P:ROWB * P + D]
        st1 = regC[:, 2 * ROWB * P:2 * ROWB * P + NT * 6].rearrange("p (n s) -> p n s", n=NT)
        EX = NE * (KD * FF + MF * D)
        EXB = EX + NE * D
        oltb = regC[:, EXB:EXB + GT * P].bitcast(bf16).rearrange("p (a b c) -> p a b c", a=2, b=GT)
        assert EXB + GT * P <= 2 * HS * (D + P)
        b2s = regC[0:1, EX:EX + NE * D].rearrange("p (e d) -> p e d", e=NE)
        RD = 3 * ROWB * P
        erow = regB[:, 0:RD].rearrange("p (c q e) -> p c q e", c=ROWB, q=3)
        eint = regB[:, RD:2 * RD].bitcast(i32).rearrange("p (c q e) -> p c q e", c=ROWB, q=3)
        strow = regB[:, 2 * RD:3 * RD].rearrange("p (c q e) -> p c q e", c=ROWB, q=3)
        before = regB[:, 3 * RD:3 * RD + ROWB * ROWB * P // 2].bitcast(bf16).rearrange("p (c k) -> p c k", c=ROWB)
        adraw = regA[:, 0:H * RUN].rearrange("p (t h) -> p t h", h=H)
        adst = regA[:, H * RUN:2 * H * RUN].rearrange("p (h t) -> p h t", h=H)
        at = 2 * H * RUN
        yo = regA[:, at:at + 2 * NE * D].rearrange("p (a e d) -> p a e d", a=2, e=NE)
        at += 2 * NE * D
        lc = regA[:, at:at + 2 * CH * W].rearrange("p (a t w) -> p a t w", a=2, t=CH)
        at += 2 * CH * W
        hc = regA[:, at:at + W * CH].rearrange("p (w t) -> p w t", w=W)
        assert at + W * CH <= NT * D
        regE = sb("regE", [P, 4 * ROWB * P + 16])
        stcol = regE[:, 0:RD].rearrange("p (q k) -> p q k", q=3)
        step_src = regE[:, RD:RD + ROWB * P].bitcast(u32)
        xin = regE[:, 0:2 * D].rearrange("p (a d) -> p a d", a=2)
        x2o = regE[:, 2 * D:4 * D].rearrange("p (a d) -> p a d", a=2)
        x3 = regE[:, 4 * D:6 * D].rearrange("p (a d) -> p a d", a=2)
        olt = regE[:, 6 * D:6 * D + 2 * GT * P].rearrange("p (a b c) -> p a b c", a=2, b=GT)
        at = 6 * D + 2 * GT * P
        run4 = regE[:, at:at + GT * GT * NT].rearrange("p (a b c) -> p a b c", a=GT, b=GT)
        at += GT * GT * NT
        ub = regE[:, at:at + GT * P // 2].bitcast(bf16).rearrange("p (a b) -> p a b", a=GT)
        assert at + GT * P // 2 <= 4 * ROWB * P + 16
        icol = regE[:, 0:RUN].bitcast(i32)
        hold = regE[:, RUN:2 * RUN]
        crow = regE[0:LF, 2 * RUN:2 * RUN + 8 * (P + 1)].rearrange("p (a b) -> p a b", a=8)
        kint = sb("kint", [P, RUN], i32)
        sint = sb("sint", [P, RUN], i32)
        pay = sb("pay", [P, RUN + CH, 2])
        lo = sb("lo", [P, RUN + HT], bf16)
        hi = sb("hi", [P, RUN + HT], bf16)
        ol = sb("ol", [P, 2, HT, P], bf16)
        ohf = sb("ohf", [P, 2 * HT * NT], bf16)
        oh = ohf[:, :].rearrange("p (a b c) -> p a b c", a=2, b=HT)
        olf = ol[:, :, :, :].rearrange("p a b c -> p (a b c)").bitcast(f32)
        hh = olf[:, 0:MF * TB].rearrange("p (m t) -> p m t", m=MF)
        at = MF * TB
        sc, sc2, ww, rr = [olf[:, at + i * H * CH:at + (i + 1) * H * CH].rearrange("p (h t) -> p h t", h=H) for i in range(4)]
        at += 4 * H * CH
        mb = olf[:, at:at + H * (CH + 1)].rearrange("p (h t) -> p h t", h=H)
        nm = ohf[:, :].bitcast(f32)[:, 0:HE * CH].rearrange("p (f t) -> p f t", f=HE)
        neg = kint[:, :].bitcast(f32)
        keep = sint[:, :].bitcast(f32)
        iot = sb("iot", [P, P], i32)
        iof = sb("iof", [P, P])
        iob = sb("iob", [P, P], bf16)
        pidx = sb("pidx", [P, ROWB], i32)
        pidf = sb("pidf", [P, ROWB])
        ident = sb("ident", [P, P])
        identb = sb("identb", [P, P], bf16)
        above = sb("above", [P, P])
        ones = sb("ones", [P, P])
        onesb = sb("onesb", [P, 1], bf16)
        ZC = 148
        ZR = (E2 + NP) * H // P // ZC
        assert ZC * ZR * P == (E2 + NP) * H
        zero = sb("zero", [P, ZC])
        eps = sb("eps", [P, 1])
        sinkrow = sb("sinkrow", [1, W])
        mv1 = sb("mv1", [P, NT, 2])
        sd1 = sb("sd1", [P, NT])
        rs1 = sb("rs1", [P, NT])
        nb1 = sb("nb1", [P, NT])
        gam = sb("gam", [P, KD])
        bet = sb("bet", [P, KD])
        CB = -(-NP // 512)
        stb = sb("stb", [P, KD, CB, 6])
        mvb = sb("mvb", [P, KD, 2])
        sdb = sb("sdb", [P, KD])
        scb = sb("scb", [P, KD])
        bib = sb("bib", [P, KD])
        lwin = sb("lwin", [P, ROWB], i32)
        lv = sb("lv", [P, ROWB])
        ikf = sb("ikf", [P, ROWB])
        jkf = sb("jkf", [P, ROWB])
        iku = sb("iku", [P, ROWB], u32)
        jki = sb("jki", [P, ROWB], i32)
        wins = sb("wins", [1, 2 * TURNS, 16], i32)
        idxr = sb("idxr", [P, 2, 16], u32)
        cnt = sb("cnt", [P, NT])
        basef = sb("basef", [P, NT])
        tots = sb("tots", [P, NT])
        totx = sb("totx", [P, NT + 1])
        gm = sb("gm", [P, GT, NT])
        posr = sb("posr", [P, 2, HT], u32)
        payr = sb("payr", [P, 2, HT, 2])
        tt = sb("tt", [P, KD, P])
        xt = sb("xt", [P, KD, P])
        stn = sb("stn", [P, 6])
        mvn = sb("mvn", [P, 2])
        sdn = sb("sdn", [P, 1])
        rsn = sb("rsn", [P, 1])
        nbn = sb("nbn", [P, 1])
        wg = sb("wg", [P, KD, W])
        attb = sb("attb", [P, 2, HE])
        wt = sb("wt", [P, HE])
        tab = sb("tab", [P, NT, W])
        vcol = sb("vcol", [P, 1])
        runp = sb("runp", [P, 4])
        runi = sb("runi", [P, 1], i32)
        posf = sb("posf", [P, GT])
        posq = sb("posq", [P, GT], i32)
        q49 = sb("q49", [P, NT], i32)
        lastk = sb("lastk", [P, 1])
        sidx = sb("sidx", [P, NT], u32)
        eidx = sb("eidx", [P, NT], u32)
        t49 = sb("t49", [P, 4, NT])
        b1s = sb("b1s", [P, NE, MF])
        gatp = sb("gatp", [P, 3, HE])
        key0 = sb("key0", [P, 1])
        keyp = sb("keyp", [P, 1])
        key0u = sb("key0u", [P, 1], u32)
        arow = sb("arow", [P, W])
        grow = sb("grow", [P, 2, HT, W])
        gidx = sb("gidx", [P, 2, HT], u32)
        ham = grow[:, :, :, :].rearrange("p a b c -> p (a b c)")[:, 0:KD * D].rearrange("p (k d) -> p k d", k=KD)
        last = sb("last", [P, W])
        cin = sb("cin", [P, 4, LF])
        cout = sb("cout", [P, 2, LF])
        same = lo[:, 0:RUN]
        nfirst = sb("nfirst", [P, 1])
        fidx = sb("fidx", [P, 1], u32)
        cf = sb("cf", [P, 4])
        frow = sb("frow", [P, W])
        fx = sb("fx", [P, 4, LF])
        esum = pay[:, :, :].rearrange("p t w -> p (t w)")[:, 0:NT * W].rearrange("p (n w) -> p n w", n=NT)

        fin = [regA[:, i * NT * HE:(i + 1) * NT * HE] for i in range(6)]
        f4 = [regA[:, 6 * NT * HE + i * NT * H:6 * NT * HE + (i + 1) * NT * H] for i in range(16)]
        assert 6 * NT * HE + 16 * NT * H <= NT * D
        YB = NT * D // ((NE + 1) * D)
        YR = YB + 2 * HS * (D + P) // ((NE + 1) * D)

        def ring(b):
            reg, k = (regB, b) if b < YB else (regC, b - YB)
            return reg[:, k * (NE + 1) * D:(k + 1) * (NE + 1) * D].rearrange("p (e d) -> p e d", e=NE + 1)


        bank = [ctx.enter_context(nc.psum_tensor(f"bank{i}", [P, 512], f32)) for i in range(8)]

        def slot(s):
            return bank[s % 7][:, 0:D]

        SB = HS - 7

        s_fill = sem("s_fill")
        s_x = [sem(f"s_xpart{i}") for i in range(LOADS)]
        s_edge = sem("s_edge")
        s_gat = sem("s_gat")
        s_par = sem("s_par")
        s_cst = sem("s_cst")
        s_cstv = sem("s_cstv")
        s_mv1, s_sd1, s_rs1, s_x1, s_x1d = sem("s_mv1"), sem("s_sd1"), sem("s_rs1"), sem("s_x1"), sem("s_x1d")
        s_rows, s_rowsd, s_bef, s_ik, s_iku, s_strow, s_dl, s_tr, s_win, s_wind = [
            sem(n) for n in ("s_rows", "s_rowsd", "s_bef", "s_ik", "s_iku", "s_strow", "s_dl", "s_tr", "s_win", "s_wind")]
        s_v = sem("s_v")
        s_idx, s_oh, s_hist, s_sel, s_step, s_acc = [sem(n) for n in ("s_idx", "s_oh", "s_hist", "s_sel", "s_step", "s_acc")]
        s_row = [sem("s_row0"), sem("s_row1")]
        s_zero, s_adz = sem("s_zero"), sem("s_adz")
        s_cnt, s_pre, s_t0 = sem("s_cnt"), sem("s_pre"), sem("s_t0")
        s_icol, s_lastk, s_lastd = sem("s_icol"), sem("s_lastk"), sem("s_lastd")
        s_bo, s_bn, s_bc, s_sdb, s_bnr, s_tanh = [sem(n) for n in ("s_bo", "s_bn", "s_bc", "s_sdb", "s_bnr", "s_tanh")]
        s_ol, s_r, s_t, s_trp, s_olt, s_eq, s_u, s_g, s_gm, s_pos = [
            sem(n) for n in ("s_ol", "s_r", "s_t", "s_trp", "s_olt", "s_eq", "s_u", "s_g", "s_gm", "s_pos")]
        s_scat = [sem("s_scat0"), sem("s_scat1")]
        s_xin = [sem("s_xin0"), sem("s_xin1")]
        s_x2d = [sem("s_x2d0"), sem("s_x2d1")]
        s_px, s_mvn, s_sdn, s_rsn, s_x2, s_x3, s_x3t, s_x3c, s_tabp, s_tab = [
            sem(n) for n in ("s_px", "s_mvn", "s_sdn", "s_rsn", "s_x2", "s_x3", "s_x3t", "s_x3c", "s_tabp", "s_tab")]
        s_wexp, s_noded, s_seidx, s_ads, s_srt, s_keys, s_k0, s_arow, s_adr = [
            sem(n) for n in ("s_wexp", "s_noded", "s_seidx", "s_ads", "s_srt", "s_keys", "s_k0", "s_arow", "s_adr")]
        s_gidx = sem("s_gidx")
        s_grow = [sem("s_grow0"), sem("s_grow1")]
        s_sc, s_ww, s_lc = sem("s_sc"), sem("s_ww"), sem("s_lc")
        s_lcd = [sem("s_lcd0"), sem("s_lcd1")]
        s_up, s_hh, s_dn, s_yo = sem("s_up"), sem("s_hh"), sem("s_dn"), sem("s_yo")
        s_yd = [sem("s_yd0"), sem("s_yd1")]
        s_cin, s_ctr, s_ce, s_cx, s_cb, s_cbt, s_fidx, s_frow, s_fe, s_fx, s_fst, s_fixed, s_esum = [
            sem(n) for n in ("s_cin", "s_ctr", "s_ce", "s_cx", "s_cb", "s_cbt", "s_fidx", "s_frow", "s_fe", "s_fx",
                             "s_fst", "s_fixed", "s_esum")]
        s_tt, s_begun, s_begun_v = [sem(n) for n in ("s_tt", "s_begun", "s_begun_v")]
        s_ma, s_mx, s_sqv, s_sqa = sem("s_ma"), sem("s_mx"), sem("s_sqv"), sem("s_sqa")
        s_yl = [sem(f"s_yl{i}") for i in range(YR)]
        s_cmb = sem("s_cmb")
        s_out = [sem(f"s_out{i}") for i in range(YR)]

        def each(ap, n):
            return ap.unsqueeze(2).to_broadcast([ap.shape[0], ap.shape[1], n])

        def every(ap, n):
            return ap.unsqueeze(1).to_broadcast([ap.shape[0], n, ap.shape[1]])

        block = ctx.enter_context(nc.Block())

        @block.sync
        def _(sp):
            sp.sem_inc(s_hist, 2)
            sp.sem_inc(s_hh, MF)
            sp.sem_inc(s_yo, 2)
            sp.sem_inc(s_acc, SB)
            sp.sem_inc(s_g, 3)
            sp.sem_inc(s_t, 1)
            sp.sem_inc(s_u, 1)
            sp.sem_inc(s_gm, 1)
            sp.sem_inc(s_px, 2)
            sp.sem_inc(s_x3, 1)
            sp.sem_inc(s_bc, 1)
            for s in s_x2d + s_lcd + s_yd:
                sp.sem_inc(s, 16)
            sp.wait_ge(s_fill, 1)
            with nc.allow_non_contiguous_dma(reason="short parameter vectors"):
                for q, a in ((0, src), (1, dst)):
                    fb = (ROWB - 1) * P
                    sp.dma_start(eint[:, 0:ROWB - 1, q, :], a[0:fb * P].rearrange("(c p e) -> p c e", p=P, e=P)).then_inc(s_edge, 16)
                    sp.dma_start(eint[0:FULL - fb, ROWB - 1, q, :], a[fb * P:FULL * P].rearrange("(p e) -> p e", e=P)).then_inc(s_edge, 16)
                    sp.dma_start(eint[FULL - fb:FULL - fb + 1, ROWB - 1, q, 0:REST], a[FULL * P:E1].rearrange("(a e) -> a e", a=1)).then_inc(s_edge, 16)
                sp.dma_start(erow[:, 0:ROWB - 1, 2, :], edge_weight[0:fb * P].rearrange("(c p e) -> p c e", p=P, e=P)).then_inc(s_edge, 16)
                sp.dma_start(erow[0:FULL - fb, ROWB - 1, 2, :], edge_weight[fb * P:FULL * P].rearrange("(p e) -> p e", e=P)).then_inc(s_edge, 16)
                sp.dma_start(erow[FULL - fb:FULL - fb + 1, ROWB - 1, 2, 0:REST], edge_weight[FULL * P:E1].rearrange("(a e) -> a e", a=1)).then_inc(s_edge, 16)
                for c in range(LOADS):
                    n0, n1 = c * LN, min((c + 1) * LN, NT - 1)
                    sp.dma_start(xa[:, n0:n1, :], x[n0 * P:n1 * P, :].rearrange("(n p) d -> p n d", p=P)).then_inc(s_x[c], 16)
                sp.dma_start(xa[0:LAST, NT - 1, :], x[(NT - 1) * P:N, :]).then_inc(s_x[LOADS - 1], 16)
                sp.dma_start(kint[:, :], edge_index[1, :].rearrange("(p t) -> p t", p=P)).then_inc(s_gat, 16)
                sp.dma_start(sint[:, :], edge_index[0, :].rearrange("(p t) -> p t", p=P)).then_inc(s_gat, 16)
                for g in range(4):
                    sp.dma_start(ham4[32 * g:32 * g + 32, :], gnn_w[:, :]).then_inc(s_par, 16)
                sp.dma_start(gam[:, :], gnn_gamma.rearrange("(m p) -> p m", p=P)).then_inc(s_par, 16)
                sp.dma_start(bet[:, :], gnn_beta.rearrange("(m p) -> p m", p=P)).then_inc(s_par, 16)
                sp.dma_start(wg[:, :, 0:HE], w_gat.rearrange("(k p) f -> p k f", p=P)).then_inc(s_par, 16)
                for q, a in ((0, att_src), (1, att_dst)):
                    sp.dma_start(attb[:, q, :], a.rearrange("h e -> (h e)").partition_broadcast(P)).then_inc(s_par, 16)
                for q, a in ((0, b_gat), (1, ln_gamma), (2, ln_beta)):
                    sp.dma_start(gatp[:, q, :], a.partition_broadcast(P)).then_inc(s_par, 16)
                for e in range(NE):
                    sp.dma_start(b1s[:, e, :], b1[e, :].rearrange("(m p) -> p m", p=P)).then_inc(s_par, 16)
            sp.wait_ge(s_rows, 1)
            sp.dma_start(rows_d.rearrange("(c p) w -> p c w", p=P), erow[:, :, :, :].rearrange("p c q e -> p c (q e)")).then_inc(s_rowsd, 16)
            for c in range(LOADS):
                sp.wait_ge(s_x1, c + 1)
                sp.dma_start(x1_d[c * LN * P:(c + 1) * LN * P, :].rearrange("(n p) d -> p n d", p=P),
                             xa[:, c * LN:(c + 1) * LN, :]).then_inc(s_x1d, 16)
            sp.wait_ge(s_win, 1)
            with nc.allow_non_contiguous_dma(reason="896 window numbers"):
                sp.dma_start(win_d.rearrange("(c p) -> p c", p=P), jki[:, :]).then_inc(s_wind, 16)
            sp.wait_ge(s_wind, 16)
            sp.dma_start(wins[:, :, 0:HS], win_d[0:2 * TURNS * HS].rearrange("(o a s) -> o a s", o=1, s=HS)).then_inc(s_wind, 16)

            sp.wait_ge(s_zero, 2)
            sp.dma_start(adst_d.rearrange("(p q t) h -> p q (t h)", p=P, q=ZR), every(zero[:, :], ZR)).then_inc(s_adz, 16)
            sp.dma_start(sorted_d.rearrange("(p q t) w -> p q (t w)", p=P, q=HT), every(zero[:, 0:P], HT)).then_inc(s_adz, 16)
            sp.dma_start(sums_d[SINK:SINK + 1, :], sinkrow[:, :]).then_inc(s_adz, 16)

            sp.wait_ge(s_step, 2 * HS * TURNS)
            sp.wait_ge(s_sel, 2 * TURNS + 2)
            for e in range(NE):
                sp.dma_start(w1s[:, e, :, :], w1[e].rearrange("(k p) f -> p k f", p=P)).then_inc(s_wexp, 16)
                sp.dma_start(w2s[:, e, :, :], w2[e].rearrange("(k p) f -> p k f", p=P)).then_inc(s_wexp, 16)

            sp.dma_start(b2s, b2.rearrange("(a e) d -> a e d", a=1)).then_inc(s_wexp, 16)

            def load_x(n, hf, rows_n=P):
                sp.wait_ge(s_px, n + 1)
                sp.dma_start(xin[0:rows_n, hf, :], x[bass.ds(n * P, rows_n), :]).then_inc(s_xin[hf], 16)

            def store_x2(n, hf):
                sp.wait_ge(s_x2, n + 1)
                sp.dma_start(x2_d[bass.ds(n * P, P), :], x2o[:, hf, :]).then_inc(s_x2d[hf], 16)

            with sp.Fori(0, (NT - 1) // 2) as i:
                load_x(i * 2, 0)
                load_x(i * 2 + 1, 1)
                store_x2(i * 2, 0)
                store_x2(i * 2 + 1, 1)
            load_x(NT - 1, 0, LAST)
            store_x2(NT - 1, 0)
            sp.wait_ge(s_tab, NT)
            sp.dma_start(node_d.rearrange("(n p) w -> p n w", p=P), tab[:, :, :]).then_inc(s_noded, 16)
            for hf in range(2):
                sp.wait_ge(s_scat[hf], 16 * HT * RT)
            sp.dma_start(pay[:, 0:RUN, :], sorted_d.rearrange("(p t) w -> p t w", p=P)).then_inc(s_srt, 16)
            with nc.allow_non_contiguous_dma(reason="one key of each partition"):
                sp.wait_ge(s_lastk, 1)
                sp.dma_start(lastkey_d, lastk[:, :]).then_inc(s_lastd, 16)
                sp.wait_ge(s_lastd, 16)
                sp.dma_start(keyp[1:P, :], lastkey_d[0:P - 1, :]).then_inc(s_lastd, 16)
            def store_y(t):
                for a in range(2):
                    sp.wait_ge(s_yo, t * (2 * NE) + (2 * NE + 1 + a))
                    sp.dma_start(y_d[bass.ds(t * TB + a * P, P), :, :], yo[:, a, :, :]).then_inc(s_yd[a], 16)

            for t in range(LAG):
                store_y(t)
            sp.wait_ge(s_ads, 16 * NT)
            sp.dma_start(adraw, adst_d[0:E2, :].rearrange("(p t) h -> p t h", p=P)).then_inc(s_adr, 16)

            def store_sums(t, hf):
                sp.wait_ge(s_lc, t + 1)
                sp.dma_start(sums_d[0:E2, :].rearrange("(p t) w -> p t w", p=P)[:, bass.ds(t * CH, CH), :],
                             lc[:, hf, :, :]).then_inc(s_lcd[hf], 16)

            AHEAD = 4
            for t in range(LAG, AHEAD):
                store_y(t)
                store_sums(t - LAG, (t - LAG) % 2)
            with sp.Fori(AHEAD // 2, FT // 2) as i:
                for hf in range(2):
                    store_y(i * 2 + hf)
                    store_sums(i * 2 + (hf - LAG), (hf - LAG) % 2)
            sp.wait_ge(s_yo, (2 * FT + 1) * NE + 2)
            sp.dma_start(y_d[FT * TB:FT * TB + P, :, :], yo[:, 0, :, :]).then_inc(s_yd[0], 16)
            for t in range(FT - LAG, TURNS):
                store_sums(t, t % 2)
            sp.wait_ge(s_yd[0], 16 * (FT + 2))
            sp.wait_ge(s_yd[1], 16 * (FT + 1))
            sp.wait_ge(s_x2d[0], 16 * (NT // 2 + 2))
            sp.wait_ge(s_x2d[1], 16 * (NT // 2 + 1))
            def store_out(k):
                m = P if k < NT - 1 else LAST
                sp.wait_ge(s_cmb, k + 1)
                sp.dma_start(out[k * P:k * P + m, :], ring(k % YR)[0:m, NE, :]).then_inc(s_out[k % YR], 16)

            LEAD = 4
            stored = 0
            for n in range(NT):
                b, m = n % YR, (P if n < NT - 1 else LAST)
                if n >= YR:
                    while stored < n - YR + LEAD:
                        store_out(stored)
                        stored += 1
                    sp.wait_ge(s_out[b], 16 * (n // YR))
                sp.dma_start(ring(b)[0:m, 0:NE, :], y_d[n * P:n * P + m, :, :]).then_inc(s_yl[b], 16)
                sp.dma_start(ring(b)[0:m, NE, :], x2_d[n * P:n * P + m, :]).then_inc(s_yl[b], 16)
            for k in range(stored, NT):
                store_out(k)
            for b in range(YR):
                sp.wait_ge(s_out[b], 16 * len(range(b, NT, YR)))

        @block.gpsimd
        def _(pool):
            pool.iota(iot[:, :], pattern=[[1, P]], base=0, channel_multiplier=0)
            pool.iota(iokb[:, :], pattern=[[1, ROWB * P]], base=0, channel_multiplier=0)
            pool.iota(pidx[:, :], pattern=[[P, ROWB]], base=0, channel_multiplier=1)
            pool.memset(ident[:, :], 0.0)
            pool.memset(above[:, :], 1.0)
            pool.memset(ones[:, :], 1.0).then_inc(s_cst, 1)
            pool.wait_ge(s_cst, 1)
            pool.affine_select(out=ident[:, :], in_=ident[:, :], compare_op=ALU.not_equal, fill=1.0, base=0,
                               pattern=[[-1, P]], channel_multiplier=1)
            pool.affine_select(out=above[:, :], in_=above[:, :], compare_op=ALU.is_gt, fill=0.0, base=0,
                               pattern=[[1, P]], channel_multiplier=-1).then_inc(s_cst, 1)
            pool.wait_ge(s_iku, 1)
            pool.wait_ge(s_rowsd, 16)
            for c in range(ROWB):
                pool.indirect_dma_start(strow[:, c, :, :].rearrange("p q e -> p (q e)"), None, rows_d,
                                        bass.IndirectOffsetOnAxis(ap=iku[:, c:c + 1], axis=0)).then_inc(s_strow, 16)
            pool.wait_ge(s_x1d, 16 * LOADS)
            with pool.Fori(0, TURNS) as i:
                for hf in range(2):
                    pool.wait_ge(s_idx, i * 2 + (hf + 1))
                    pool.sem_inc(s_begun, 1)
                    for s in range(HS):
                        pool.indirect_dma_start(rows[:, hf, s, :], None, x1_d,
                                                bass.IndirectOffsetOnAxis(ap=idxr[:, hf, s:s + 1], axis=0)
                                                ).then_inc(s_row[hf], 16)
            pool.wait_ge(s_adz, 16 * 3)
            with pool.Fori(0, RT) as i:
                for hf in range(2):
                    for g in range(HT // GT):
                        pool.wait_ge(s_pos, i * (2 * HT // GT) + (hf * (HT // GT) + g + 1))
                        pool.sem_inc(s_begun, 1)
                        for t in range(g * GT, (g + 1) * GT):
                            pool.indirect_dma_start(sorted_d, bass.IndirectOffsetOnAxis(ap=posr[:, hf, t:t + 1], axis=0),
                                                    payr[:, hf, t, :], None, bounds_check=E2 - 1,
                                                    oob_is_err=False).then_inc(s_scat[hf], 16)
            pool.wait_ge(s_tab, NT)
            pool.wait_ge(s_seidx, 1)
            pool.wait_ge(s_x2d[0], 16 * (NT // 2 + 2))
            pool.wait_ge(s_x2d[1], 16 * (NT // 2 + 1))
            pool.iota(icol, pattern=[[1, RUN]], base=0, channel_multiplier=0).then_inc(s_icol, 1)
            for n in range(NT):
                pool.indirect_dma_start(adst_d, bass.IndirectOffsetOnAxis(ap=sidx[:, n:n + 1], axis=0),
                                        tab[:, n, HE + H:W], None).then_inc(s_ads, 16)
            pool.wait_ge(s_k0, 1)
            pool.wait_ge(s_noded, 16)
            pool.indirect_dma_start(arow[:, :], None, node_d, bass.IndirectOffsetOnAxis(ap=key0u[:, :], axis=0)).then_inc(s_arow, 16)
            run = pool.value_load(runi[0:1, 0:1], min_val=1, max_val=RUN)
            with pool.Fori(0, RT) as i:
                for hf in range(2):
                    pool.wait_ge(s_gidx, i * 2 + (hf + 1))
                    pool.sem_inc(s_begun, 1)
                    with pool.If(run > i * CH + hf * HT):
                        for t in range(HT):
                            pool.indirect_dma_start(grow[:, hf, t, :], None, node_d,
                                                    bass.IndirectOffsetOnAxis(ap=gidx[:, hf, t:t + 1], axis=0)
                                                    ).then_inc(s_grow[hf], 16)
            pool.wait_ge(s_fidx, 1)
            for s in s_lcd:
                pool.wait_ge(s, 16 * (TURNS // 2 + 1))
            pool.indirect_dma_start(frow[:, :], None, sums_d, bass.IndirectOffsetOnAxis(ap=fidx[:, :], axis=0)).then_inc(s_frow, 16)
            pool.wait_ge(s_fst, 1)
            pool.indirect_dma_start(sums_d, bass.IndirectOffsetOnAxis(ap=fidx[:, :], axis=0), arow[:, :], None).then_inc(s_fixed, 16)
            pool.wait_ge(s_fixed, 16)
            for n in range(NT):
                pool.indirect_dma_start(esum[:, n, :], None, sums_d, bass.IndirectOffsetOnAxis(ap=eidx[:, n:n + 1], axis=0)
                                        ).then_inc(s_esum, 16)

        @block.scalar
        def _(act):
            act.wait_ge(s_cstv, 1)
            for c in range(LOADS + 1):
                if c < LOADS:
                    part = slice(c * LN, (c + 1) * LN)
                    act.wait_ge(s_mv1, c + 1)
                    act.activation(sd1[:, part], mv1[:, part, 1], ACT.Sqrt, bias=eps[:, :], scale=1.0).then_inc(s_sd1, 1)
                if c:
                    act.wait_ge(s_rs1, c)
                    for n in range((c - 1) * LN, c * LN):
                        ins = act.activation(xa[:, n, :], xa[:, n, :], ACT.Identity, bias=nb1[:, n:n + 1], scale=rs1[:, n:n + 1])
                    ins.then_inc(s_x1, 1)
            def olt_copy(g, par, tp):
                act.wait_ge(s_trp, g + 1)
                act.wait_ge(s_g, g + 2)
                one = bank[par][:, :].bitcast(bf16)[:, 0:GT * P]
                act.activation(oltb[:, par, :, :].rearrange("p a b -> p (a b)"), one, ACT.Copy)
                act.activation(olt[:, par, :, :].rearrange("p a b -> p (a b)"), one, ACT.Copy).then_inc(s_olt, 1)

            def rank(G, gi):
                act.wait_ge(s_r, G + 1)
                act.wait_ge(s_g, G + 1)
                act.activation(run4[:, gi, :, :].rearrange("p a b -> p (a b)"), bank[3][:, 0:GT * NT], ACT.Copy).then_inc(s_t, 1)
                olt_copy(G + 1, (gi + 1) % 2, None)

            def next_tanh(n):
                act.activation(tt[:, :, :], gnn[:, :, bass.ds(n * P, P)], ACT.Copy).then_inc(s_tt, 1)

            def node(n, hf, gi, turn, ahead=True):
                if gi == 0 and not (isinstance(n, int) and n == 0):
                    act.wait_ge(s_tabp, n)
                    act.activation(tab[:, bass.ds(n - 1, 1), :].rearrange("p a w -> p (a w)"), bank[7][:, 0:W], ACT.Copy).then_inc(s_tab, 1)
                if gi == 1:
                    act.wait_ge(s_mvn, n + 1)
                    act.activation(sdn[:, :], mvn[:, 1:2], ACT.Sqrt, bias=eps[:, :], scale=1.0).then_inc(s_sdn, 1)
                    act.wait_ge(s_x2d[hf], (turn + 1) * 16)
                    act.activation(x2o[:, hf, :], bank[5][:, 0:D], ACT.Copy).then_inc(s_x2, 1)
                    if ahead:
                        next_tanh(n + 1)
                if gi == 3:
                    act.wait_ge(s_x3t, n + 1)
                    act.activation(xt[:, :, :], bank[6][:, 0:D].rearrange("p (k n) -> p k n", k=KD), ACT.Copy)
                    act.activation(x3T[:, :, bass.ds(n * P, P)], bank[6][:, 0:D].rearrange("p (k n) -> p k n", k=KD),
                                   ACT.Copy).then_inc(s_x3c, 1)

            def gnn_block(b, w=512):
                act.wait_ge(s_bo, b + 1)
                for m in range(KD):
                    ins = act.activation(gnn[:, m, bass.ds(b * 512, w)], bank[5 + m][:, 0:w], ACT.Copy)
                ins.then_inc(s_bc, 1)

            def turn(i, extra):
                for hf in range(2):
                    for gi in range(NG):
                        if extra == "gnn" and gi % 2:
                            gnn_block(i * 4 + (2 * hf + gi // 2))
                        if extra == "bn" and hf == 0 and gi == 1:
                            gnn_block(CB - 1, NP - (CB - 1) * 512)
                        rank(i * (2 * NG) + (hf * NG + gi), gi)
                        if extra == "bn" and hf == 1 and gi == 0:
                            act.wait_ge(s_sdb, 1)
                            act.activation(sdb[:, :], mvb[:, :, 1], ACT.Sqrt, bias=eps[:, :], scale=1.0).then_inc(s_sdb, 1)
                        if extra == "tanh":
                            k = hf * NG + gi
                            act.wait_ge(s_bnr, 1)
                            for m in range(KD):
                                part = gnn[:, m, k * (NP // 8):(k + 1) * (NP // 8)]
                                act.activation(part, part, ACT.Tanh, bias=bib[:, m:m + 1], scale=scb[:, m:m + 1]).then_inc(s_tanh, 1)
                        if extra == "nodes":
                            node(i * 2 + (hf - 2 * N0), hf, gi, i - N0)
                        if extra == "last" and hf == 0:
                            node(NT - 1, hf, gi, i - N0, ahead=False)
                        if extra == "last" and hf == 1 and gi == 0:
                            node(NT, hf, gi, i - N0)

            NG = HT // GT
            olt_copy(0, 0, None)
            turn(0, "gnn")
            with act.Fori(1, CT) as i:
                turn(i, "gnn")
            turn(CT, "bn")
            turn(CT + 1, "tanh")
            act.wait_ge(s_tanh, 8 * KD)
            next_tanh(0)
            turn(N0, "nodes")
            with act.Fori(N0 + 1, N1) as i:
                turn(i, "nodes")
            turn(N1, "last")
            with act.Fori(N1 + 1, RT) as i:
                turn(i, "")

            def gelu(i, e, m, T):
                act.wait_ge(s_up, i * (NE * MF) + (e * MF + m + 1))
                act.activation(hh[:, m, 0:T], bank[m][:, 0:T], ACT.Gelu, bias=b1s[:, e, m:m + 1], scale=1.0).then_inc(s_hh, 1)

            def outputs(i, e, halves=2):
                for a in range(halves):
                    act.wait_ge(s_dn, i * (2 * NE) + (halves * e + a + 1))
                    if e == 0:
                        act.wait_ge(s_yd[a], (i + 1) * 16)
                    act.activation(yo[:, a, e, :], bank[4 + a][:, 0:D], ACT.Copy).then_inc(s_yo, 1)

            def experts(i, halves=2):
                T = halves * P
                for e in range(NE):
                    first = isinstance(i, int) and i == 0 and e == 0
                    if not first:
                        act.wait_ge(s_dn, i * (2 * NE) + halves * e)
                    gelu(i, e, 0, T)
                    gelu(i, e, 1, T)
                    if e:
                        outputs(i, e - 1, halves)
                    elif not first:
                        outputs(i - 1, NE - 1)
                    gelu(i, e, 2, T)
                    gelu(i, e, 3, T)

            def exponentials(i):
                act.wait_ge(s_sc, i + 1)
                act.activation(rr[:, :, :], sc2[:, :, :], ACT.Exp)
                act.activation(ww[:, :, :], sc[:, :, :], ACT.Exp).then_inc(s_ww, 1)

            for i in range(LAG):
                experts(i)
            with act.Fori(LAG, FT) as i:
                experts(i)
                exponentials(i - LAG)
            experts(FT, 1)
            outputs(FT, NE - 1, 1)
            for i in range(FT - LAG, TURNS):
                act.wait_ge(s_ww, i)
                exponentials(i)

            act.wait_ge(s_ce, 1)
            act.activation(crow[:, 4, 0:P], crow[:, 4, 0:P], ACT.Exp)
            act.activation(crow[:, 5, 0:P], crow[:, 5, 0:P], ACT.Exp).then_inc(s_cx, 1)
            act.wait_ge(s_fe, 1)
            act.activation(fx[:, 1:3, :], fx[:, 1:3, :], ACT.Exp).then_inc(s_fx, 1)
            act.wait_ge(s_ma, 1)
            act.activation(f4[2], f4[2], ACT.Exp)
            act.activation(f4[3], f4[3], ACT.Exp).then_inc(s_mx, 1)
            act.wait_ge(s_sqv, 1)
            act.activation(t49[:, 0, :], t49[:, 0, :], ACT.Sqrt, bias=eps[:, :], scale=1.0).then_inc(s_sqa, 1)
            act.wait_ge(s_ma, 2)
            act.activation(f4[2], f4[2], ACT.Exp).then_inc(s_mx, 1)

        @block.vector
        def _(dve):
            v = Chain(dve, s_v)
            fb = ROWB - 1
            dve.memset(xa[:, NT - 1, :], 0.0)
            dve.memset(eint[:, fb, 0, :], 0)
            dve.memset(eint[:, fb, 1, :], N - 1)
            dve.memset(erow[:, fb, 2, :], 0.0).then_inc(s_fill, 1)
            dve.memset(zero[:, :], 0.0).then_inc(s_zero, 1)
            dve.memset(eps[:, :], EPS)
            dve.memset(onesb[:, :], 1.0).then_inc(s_cstv, 1)
            dve.memset(lo[:, RUN:RUN + HT], 0.0)
            dve.memset(hi[:, RUN:RUN + HT], 0.0)
            dve.memset(keyp[0:1, :], -1.0)
            dve.memset(pay[:, RUN:RUN + CH, :], 0.0)
            dve.memset(sinkrow[:, H:W], 0.0)
            dve.memset(sinkrow[:, 0:H], -BIG).then_inc(s_zero, 1)
            dve.wait_ge(s_cst, 2)
            dve.tensor_copy(iof[:, :], iot[:, :])
            dve.tensor_copy(iob[:, :], iot[:, :])
            dve.tensor_copy(pidf[:, :], pidx[:, :])
            v(dve.tensor_copy(identb[:, :], ident[:, :]))
            dve.wait_ge(s_edge, 16 * 9)
            v.mark(dve.tensor_scalar(erow[:, :, 0, :], eint[:, :, 0, :], float(N - 1), 0.0, ALU.min, ALU.max))
            dve.tensor_copy(erow[:, :, 1, :], eint[:, :, 1, :]).then_inc(s_rows, 1)
            v(dve.tensor_single_scalar(lwin[:, :], eint[:, :, 1, P - 1], 7, ALU.arith_shift_right))
            v(dve.tensor_scalar(lv[:, :], lwin[:, :], 0.0, float(NT - 1), ALU.max, ALU.min))
            v(dve.scalar_tensor_tensor(lv[:, :], lv[:, :], 1.0, pidf[:, :], ALU.add, ALU.add))
            for c in range(ROWB):
                ins = dve.tensor_scalar(before[:, c, :], iokb[:, :], lv[:, c:c + 1], None, ALU.is_ge)
            ins.then_inc(s_bef, 1)
            def stats(c):
                dve.wait_ge(s_x[c], 16 if c < LOADS - 1 else 32)
                for n in range(c * LN, (c + 1) * LN):
                    ins = dve.bn_stats(st1[:, n, :], xa[:, n, :])
                v(ins)
                for n in range(c * LN, (c + 1) * LN):
                    ins = dve.bn_aggr(mv1[:, n, :], st1[:, n, :])
                ins.then_inc(s_mv1, 1)

            def norms(c):
                part = slice(c * LN, (c + 1) * LN)
                dve.wait_ge(s_sd1, c + 1)
                v(dve.reciprocal(rs1[:, part], sd1[:, part]))
                dve.scalar_tensor_tensor(nb1[:, part], mv1[:, part, 0], -1.0, rs1[:, part], ALU.mult, ALU.mult).then_inc(s_rs1, 1)

            WALK = 3
            for c in range(WALK):
                stats(c)
                if c:
                    norms(c - 1)
            dve.wait_ge(s_ik, 1)
            v(dve.tensor_copy(ikf[:, :], bank[0][:, 0:ROWB]))
            dve.tensor_copy(iku[:, :], ikf[:, :]).then_inc(s_iku, 1)
            v(dve.tensor_tensor(jkf[:, :], pidf[:, :], ikf[:, :], ALU.subtract))
            v(dve.tensor_scalar(jkf[:, :], jkf[:, :], float(NT - 1), float(P), ALU.min, ALU.mult))
            dve.tensor_copy(jki[:, :], jkf[:, :]).then_inc(s_win, 1)
            for c in range(WALK, LOADS):
                stats(c)
                norms(c - 1)
            norms(LOADS - 1)
            dve.wait_ge(s_strow, 16 * ROWB)
            for c in range(ROWB):
                ins = dve.tensor_scalar(strow[:, c, 1, :], strow[:, c, 1, :], jkf[:, c:c + 1], None, ALU.subtract)
            ins.then_inc(s_dl, 1)
            for q in range(3):
                dve.wait_ge(s_tr, q + 1)
                v.mark(dve.tensor_copy(stcol[:, q, 0:4 * P], bank[1 + 2 * q][:, :]))
                v.mark(dve.tensor_copy(stcol[:, q, 4 * P:ROWB * P], bank[2 + 2 * q][:, 0:(ROWB - 4) * P]))
            v.wait()
            v(dve.tensor_copy(step_src, stcol[:, 0, :]))
            dve.wait_ge(s_gat, 32)
            v.mark(dve.tensor_scalar(pay[:, 0:RUN, 1], sint[:, :], float(N - 1), 0.0, ALU.min, ALU.max))
            v(dve.tensor_scalar(pay[:, 0:RUN, 0], kint[:, :], 0.0, 2.0**33, ALU.is_lt, ALU.mult))
            v(dve.tensor_tensor(pay[:, 0:RUN, 0], pay[:, 0:RUN, 0], kint[:, :], ALU.add))
            v(dve.tensor_scalar(pay[:, 0:RUN, 0], pay[:, 0:RUN, 0], float(N), None, ALU.min))
            v(dve.tensor_copy(kint[:, :], pay[:, 0:RUN, 0]))
            v(dve.tensor_single_scalar(sint[:, :], kint[:, :], P - 1, ALU.bitwise_and))
            v(dve.tensor_copy(lo[:, 0:RUN], sint[:, :]))
            v(dve.tensor_single_scalar(sint[:, :], kint[:, :], 7, ALU.arith_shift_right))
            v(dve.tensor_copy(hi[:, 0:RUN], sint[:, :]))
            dve.wait_ge(s_par, 16 * 16)
            dve.memset(grow[:, :, :, :].rearrange("p a b c -> p (a b c)")[:, KD * D:], 0.0)
            S8 = D // 8
            for q in range(8):
                r = slice(32 * (q % 4), 32 * (q % 4) + 32)
                for p in range(8):
                    j = IDX[p][q]
                    dve.tensor_scalar(ham[r, q // 4, p * S8:(p + 1) * S8], ham4[r, j * S8:(j + 1) * S8],
                                      float(SIGN[p][q]), None, ALU.mult)
            for k in range(KD):
                for q in range(2):
                    v(dve.tensor_tensor(wt[:, :], wg[:, k, 0:HE], attb[:, q, :], ALU.mult))
                    v(dve.tensor_reduce(wg[:, k, HE + q * H:HE + (q + 1) * H], wt[:, :].rearrange("p (h e) -> p h e", h=H),
                                        AX.X, ALU.add))
            v(dve.memset(regB[:, :], 0.0))
            def weighted(k, hf, s):
                return dve.tensor_scalar(onehot[:, hf, s, :], iof[:, :], stcol[:, 1, bass.ds(k, 1)],
                                         stcol[:, 2, bass.ds(k, 1)], ALU.is_equal, ALU.mult)

            for hf in range(2):
                dve.tensor_copy(idxr[:, hf, 0:HS], step_src[:, hf * HS:(hf + 1) * HS]).then_inc(s_idx, 1)
            for hf in range(2):
                for s in range(HS):
                    ins = weighted(hf * HS + s, hf, s)
                ins.then_inc(s_sel, 1)
            regs = [dve.alloc_register(f"win{s}") for s in range(HS)]
            dve.wait_ge(s_wind, 32)
            with dve.Fori(0, TURNS) as i:
                for hf in range(2):
                    dve.wait_ge(s_hist, i * 2 + (hf + 1))
                    at = i * CH + hf * HT
                    dve.tensor_tensor(ol[:, hf, :, :], every(iob[:, :], HT), each(lo[:, bass.ds(at, HT)], P), ALU.is_equal)
                    dve.tensor_tensor(oh[:, hf, :, :], every(iob[:, 0:NT], HT), each(hi[:, bass.ds(at, HT)], NT),
                                      ALU.is_equal).then_inc(s_oh, 1)
                    dve.load(regs, wins[0:1, bass.ds(i * 2 + hf, 1), 0:HS])
                    for s in range(HS):
                        k = i * (2 * HS) + (hf * HS + s)
                        w = dve.snap(regs[s], min_val=0, max_val=(NT - 1) * P)
                        dve.wait_ge(s_step, k + 1)
                        dve.wait_ge(s_acc, k + SB)
                        dve.tensor_tensor(acc[:, :, bass.ds(w, P)], acc[:, :, bass.ds(w, P)],
                                          slot(s).rearrange("p (k n) -> p k n", k=KD), ALU.add).then_inc(s_acc, 1)
                        ins = weighted(k + 2 * HS, hf, s)
                    ins.then_inc(s_sel, 1)
                    dve.tensor_copy(idxr[:, hf, 0:HS], step_src[:, bass.ds((i + 1) * (2 * HS) + hf * HS, HS)]).then_inc(s_idx, 1)
            dve.wait_ge(s_hist, 2 * TURNS + 2)
            v(dve.tensor_copy(cnt[:, :], bank[7][:, 0:NT]))
            dve.tensor_tensor(vcol[:, :], cnt[:, NT - 1:NT], above[:, LAST:LAST + 1], ALU.mult).then_inc(s_cnt, 1)
            dve.memset(totx[:, 0:1], 0.0)
            dve.wait_ge(s_pre, 1)
            v.mark(dve.tensor_copy(cnt[:, NT - 1:NT], vcol[:, :]))
            v.mark(dve.tensor_copy(runp[:, 1:2], bank[6][:, 128:129]))
            v(dve.tensor_copy(tots[:, :], bank[6][:, 64:64 + NT]))
            v(dve.tensor_tensor_scan(totx[:, 1:NT + 1], ones[:, 0:NT], tots[:, :], 0.0, ALU.mult, ALU.add))
            v(dve.tensor_tensor(basef[:, :], bank[6][:, 0:NT], totx[:, 0:NT], ALU.add))
            dve.tensor_copy(run4[:, GT - 1, GT - 1, :], basef[:, :]).then_inc(s_t0, 1)
            v(dve.tensor_tensor(runp[:, 1:2], runp[:, 1:2], totx[:, NT - 1:NT], ALU.add))
            v(dve.tensor_scalar(runp[:, 1:2], runp[:, 1:2], float(P - 1), 1.0 / P, ALU.add, ALU.mult))
            v(dve.tensor_scalar(runi[:, :], runp[:, 1:2], 0.5 / P - 0.5, 1.0, ALU.add, ALU.max))
            v(dve.tensor_copy(runp[:, 0:1], runi[:, :]))
            v.mark(dve.tensor_scalar(runp[:, 3:4], runp[:, 0:1], -1.0, float(RUN), ALU.mult, ALU.add))
            v(dve.reciprocal(runp[:, 1:2], runp[:, 0:1]))
            v(dve.tensor_scalar(runp[:, 2:3], runp[:, 1:2], 0.5, -0.5, ALU.mult, ALU.add))

            def partition_of(out, pos):
                return dve.tensor_scalar(out, pos, runp[:, 1:2], runp[:, 2:3], ALU.mult, ALU.add)

            def place(out, pos, part):
                return dve.scalar_tensor_tensor(out, part, runp[:, 3:4], pos, ALU.mult, ALU.add)

            def onehots(G, hf, gi):
                g0 = gi * GT
                dve.tensor_tensor(ol[:, hf, g0:g0 + GT, :], every(iob[:, :], GT), each(lo[:, bass.ds(G * GT, GT)], P), ALU.is_equal)
                dve.tensor_tensor(oh[:, hf, g0:g0 + GT, :], every(iob[:, 0:NT], GT), each(hi[:, bass.ds(G * GT, GT)], NT),
                                  ALU.is_equal).then_inc(s_ol, 1)

            for g in range(HT // GT - 1):
                onehots(g, 0, g)
            def gnn_stats(b, w=512):
                dve.wait_ge(s_bc, b + 2)
                for m in range(KD):
                    ins = dve.bn_stats(stb[:, m, bass.ds(b, 1), :].rearrange("p a s -> p (a s)"), gnn[:, m, bass.ds(b * 512, w)])
                ins.then_inc(s_bn, 1)

            NG = HT // GT

            def products(G, hf, gi):
                g0 = gi * GT
                dve.wait_ge(s_g, G + 3)
                dve.tensor_tensor(gm[:, :, :], bank[4][:, 0:GT * NT].rearrange("p (a b) -> p a b", a=GT),
                                  oh[:, hf, g0:g0 + GT, :], ALU.mult).then_inc(s_gm, 1)

            def sums(G, i, hf, gi, meanwhile=None):
                g0 = gi * GT
                dve.wait_ge(s_gm, G + 1)
                v.mark(dve.tensor_reduce(posf[:, :], gm[:, :, :], AX.X, ALU.add))
                if gi == 0 and not (isinstance(i, int) and i == 0):
                    dve.wait_ge(s_scat[hf], i * (16 * HT))
                dve.tensor_copy(payr[:, hf, g0:g0 + GT, :], pay[:, bass.ds(i * CH + (hf * HT + g0), GT), :])
                if meanwhile:
                    meanwhile()
                v.wait()
                v(partition_of(posq[:, :], posf[:, :]))
                place(posr[:, hf, g0:g0 + GT], posf[:, :], posq[:, :]).then_inc(s_pos, 1)

            def rank(i, hf, gi):
                G = i * (2 * NG) + (hf * NG + gi)
                ph, pg = hf if gi else 1 - hf, (gi - 1) % NG
                first = isinstance(i, int) and G == 0
                if not first:
                    products(G, ph, pg)
                dve.wait_ge(s_eq, G + 1)
                dve.tensor_tensor(ub[:, :, :], bank[2][:, :].rearrange("p (a b) -> p a b", a=GT), every(above[:, :], GT),
                                  ALU.mult).then_inc(s_u, 1)

                def ahead():
                    onehots(G + (NG - 1), hf if gi == 0 else 1 - hf, (gi - 1) % NG)

                if first:
                    ahead()
                else:
                    sums(G, i - 1 if hf == gi == 0 else i, ph, pg, ahead)

            def node(n, hf, gi):
                if gi == 0:
                    dve.wait_ge(s_px, n + 3)
                    v(dve.bn_stats(stn[:, :], bank[5][:, 0:D]))
                    dve.sem_inc(s_begun_v, 1)
                    dve.bn_aggr(mvn[:, :], stn[:, :]).then_inc(s_mvn, 1)
                if gi == 1:
                    dve.wait_ge(s_sdn, n + 1)
                    v(dve.reciprocal(rsn[:, :], sdn[:, :]))
                    dve.wait_ge(s_x2, n + 1)
                    dve.tensor_scalar(x3[:, hf, :], bank[5][:, 0:D], mvn[:, 0:1], rsn[:, :], ALU.subtract, ALU.mult).then_inc(s_x3, 1)

            def turn(i, extra):
                for hf in range(2):
                    for gi in range(NG):
                        n = i * 2 + (hf - 2 * N0)
                        rank(i, hf, gi)
                        if extra == "nodes" or (extra == "last" and hf == 0):
                            node(n, hf, gi)
                        if extra == "gnn" and gi % 2:
                            gnn_stats(i * 4 + (2 * hf + gi // 2))
                        if extra == "bn" and hf == 0 and gi == 1:
                            gnn_stats(CB - 1, N - (CB - 1) * 512)
                            dve.wait_ge(s_bn, CB)
                            for m in range(KD):
                                ins = dve.bn_aggr(mvb[:, m, :], stb[:, m, :, :])
                            ins.then_inc(s_sdb, 1)
                        if extra == "bn" and hf == 1 and gi == 1:
                            dve.wait_ge(s_sdb, 2)
                            v(dve.reciprocal(sdb[:, :], sdb[:, :]))
                            v(dve.tensor_tensor(scb[:, :], sdb[:, :], gam[:, :], ALU.mult))
                            v(dve.tensor_tensor(bib[:, :], mvb[:, :, 0], scb[:, :], ALU.mult))
                            dve.tensor_tensor(bib[:, :], bet[:, :], bib[:, :], ALU.subtract).then_inc(s_bnr, 1)

            RG = 2 * 2 * NG
            turn(0, "gnn")
            with v.loop(1, CT, RG) as i:
                turn(i, "gnn")
            turn(CT, "bn")
            turn(CT + 1, "tanh")
            turn(N0, "nodes")
            with v.loop(N0 + 1, N1, RG + 4) as i:
                turn(i, "nodes")
            turn(N1, "last")
            v(dve.tensor_scalar(t49[:, 0, :], cnt[:, :], 0.0, None, ALU.is_equal))
            v(partition_of(q49[:, :], basef[:, :]))
            v(place(t49[:, 1, :], basef[:, :], q49[:, :]))
            v(dve.tensor_scalar(t49[:, 2, :], iof[:, 0:NT], float(P), pidf[:, 0:1], ALU.mult, ALU.add))
            v(dve.scalar_tensor_tensor(t49[:, 2, :], t49[:, 2, :], float(E2), t49[:, 1, :], ALU.add, ALU.subtract))
            v(dve.tensor_tensor(t49[:, 2, :], t49[:, 2, :], t49[:, 0, :], ALU.mult))
            v(dve.tensor_tensor(sidx[:, :], t49[:, 1, :], t49[:, 2, :], ALU.add))
            v(dve.scalar_tensor_tensor(t49[:, 3, :], basef[:, :], -1.0, cnt[:, :], ALU.add, ALU.add))
            v(partition_of(q49[:, :], t49[:, 3, :]))
            v(place(t49[:, 1, :], t49[:, 3, :], q49[:, :]))
            v(dve.tensor_scalar(t49[:, 2, :], t49[:, 1, :], -1.0, float(SINK), ALU.mult, ALU.add))
            v(dve.tensor_tensor(t49[:, 2, :], t49[:, 2, :], t49[:, 0, :], ALU.mult))
            dve.tensor_tensor(eidx[:, :], t49[:, 1, :], t49[:, 2, :], ALU.add).then_inc(s_seidx, 1)
            with v.loop(N1 + 1, RT, RG) as i:
                turn(i, "")
            products(RT * 2 * NG, 1, NG - 1)
            sums(RT * 2 * NG, RT - 1, 1, NG - 1)

            dve.wait_ge(s_icol, 1)
            dve.wait_ge(s_olt, RT * 2 * NG + 1)
            v(dve.tensor_scalar(hold, icol, runp[:, 0:1], None, ALU.is_ge))
            dve.wait_ge(s_srt, 16)
            v(dve.tensor_copy(key0[:, :], pay[:, 0, 0:1]))
            v(dve.tensor_tensor_scan(pay[:, 0:RUN, 0], hold, pay[:, 0:RUN, 0], 0.0, ALU.mult, ALU.add))
            dve.tensor_copy(lastk[:, :], pay[:, RUN - 1, 0:1]).then_inc(s_lastk, 1)
            dve.tensor_copy(key0u[:, :], key0[:, :]).then_inc(s_k0, 1)
            v(dve.tensor_scalar(hold, hold, -BIG, None, ALU.mult))
            for hf in range(2):
                dve.tensor_copy(gidx[:, hf, :], pay[:, hf * HT:(hf + 1) * HT, 1]).then_inc(s_gidx, 1)
            dve.wait_ge(s_lastd, 32)
            v.mark(dve.tensor_tensor(keep[:, 1:RUN], pay[:, 1:RUN, 0], pay[:, 0:RUN - 1, 0], ALU.is_equal))
            v(dve.tensor_tensor(keep[:, 0:1], key0[:, :], keyp[:, :], ALU.is_equal))
            v.mark(dve.tensor_scalar(neg[:, :], keep[:, :], -1.0, BIG, ALU.add, ALU.mult))
            v(dve.tensor_scalar(same[:, :], pay[:, 0:RUN, 0], key0[:, :], None, ALU.is_equal))
            v(dve.tensor_reduce(nfirst[:, :], same[:, :], AX.X, ALU.add))
            v(dve.tensor_tensor(nfirst[:, :], nfirst[:, :], runp[:, 0:1], ALU.min))
            v(dve.tensor_scalar(cf[:, 0:1], pidf[:, 0:1], float(RUN), -1.0, ALU.mult, ALU.add))
            dve.tensor_tensor(fidx[:, :], cf[:, 0:1], nfirst[:, :], ALU.add).then_inc(s_fidx, 1)
            dve.wait_ge(s_arow, 16)
            dve.wait_ge(s_adr, 16)
            for h in range(H):
                v.mark(dve.tensor_tensor_scan(adst[:, h, :], keep[:, :], adraw[:, :, h], arow[:, HE + H + h:HE + H + h + 1],
                                              ALU.mult, ALU.add))
            v.wait()
            v.mark(dve.tensor_tensor(adst, adst, every(hold, H), ALU.add))
            v.mark(dve.memset(last[:, 0:H], -BIG))
            v(dve.memset(last[:, H:W], 0.0))

            gathered = dve.value_load(runi[0:1, 0:1], min_val=1, max_val=RUN)

            def chunk(i, j):
                t = i * 2 + j
                for hf in range(2):
                    if hf:
                        with dve.If(gathered > t * CH + hf * HT):
                            dve.wait_ge(s_grow[hf], (t + 1) * (16 * HT))
                            dve.sem_inc(s_begun_v, 1)
                    else:
                        dve.wait_ge(s_grow[hf], (t + 1) * (16 * HT))
                    v(dve.tensor_copy(hc[:, :, hf * HT:(hf + 1) * HT], grow[:, hf, :, :].rearrange("p t w -> p w t")))
                    dve.tensor_copy(gidx[:, hf, :], pay[:, bass.ds((t + 1) * CH + hf * HT, HT), 1]).then_inc(s_gidx, 1)
                tc = bass.ds(t * CH, CH)
                v(dve.tensor_tensor(sc[:, :, :], hc[:, HE:HE + H, :], adst[:, :, tc], ALU.add))
                v(dve.scalar_tensor_tensor(sc[:, :, :], sc[:, :, :], 0.2, sc[:, :, :], ALU.mult, ALU.max))
                v(dve.tensor_copy(mb[:, :, 0], last[:, 0:H]))
                for h in range(H):
                    v.mark(dve.tensor_tensor_scan(mb[:, h, 1:CH + 1], neg[:, tc], sc[:, h, :], last[:, h:h + 1], ALU.add, ALU.max))
                v.wait()
                v(dve.tensor_tensor(sc2[:, :, :], mb[:, :, 0:CH], every(neg[:, tc], H), ALU.add))
                v.mark(dve.tensor_tensor(sc2[:, :, :], sc2[:, :, :], mb[:, :, 1:CH + 1], ALU.subtract))
                v(dve.tensor_tensor(sc[:, :, :], sc[:, :, :], mb[:, :, 1:CH + 1], ALU.subtract))
                dve.sem_inc(s_sc, 1)
                dve.wait_ge(s_ww, t + 1)
                dve.wait_ge(s_lcd[j], (i + 1) * 16)
                v(dve.tensor_tensor(nm[:, :, :].rearrange("p (h e) t -> p h e t", h=H),
                                    hc[:, 0:HE, :].rearrange("p (h e) t -> p h e t", h=H),
                                    ww[:, :, :].unsqueeze(2).to_broadcast([P, H, NE, CH]), ALU.mult))
                for h in range(H):
                    v.mark(dve.tensor_tensor_scan(lc[:, j, :, H + h], rr[:, h, :], ww[:, h, :], last[:, H + h:H + h + 1],
                                                  ALU.mult, ALU.add))
                for f in range(HE):
                    v.mark(dve.tensor_tensor_scan(lc[:, j, :, 2 * H + f], rr[:, f // NE, :], nm[:, f, :],
                                                  last[:, 2 * H + f:2 * H + f + 1], ALU.mult, ALU.add))
                v(dve.tensor_copy(lc[:, j, :, 0:H], mb[:, :, 1:CH + 1].rearrange("p h t -> p t h")))
                v.mark(dve.tensor_copy(last[:, :], lc[:, j, CH - 1, :]))
                dve.wait_ge(s_v, v.value())
                dve.sem_inc(s_lc, 1)

            def chunk_or_none(i, j):
                t, before_n = i * 2 + j, v.n
                with dve.If(gathered > t * CH):
                    chunk(i, j)
                with dve.Else():
                    dve.sem_inc(s_v, v.n - before_n)
                    dve.sem_inc(s_gidx, 2)
                    dve.sem_inc(s_sc, 1)
                    dve.sem_inc(s_lc, 1)

            per = 2 * (2 + 1 + 1 + 1 + H + 1 + 1 + 1 + 1 + H + HE + 1 + 1)
            with v.loop(0, TURNS // 2, per) as i:
                chunk_or_none(i, 0)
                chunk_or_none(i, 1)

            v.mark(dve.tensor_copy(cin[:, 0, 0:H], last[:, 0:H]))
            v.mark(dve.tensor_copy(cin[:, 0, H:LF].rearrange("p (h e) -> p h e", h=H), each(last[:, 0:H], NE)))
            v.mark(dve.tensor_copy(cin[:, 1, :], last[:, H:W]))
            v(dve.tensor_scalar(cf[:, 2:3], nfirst[:, :], runp[:, 0:1], None, ALU.is_equal))
            v(dve.tensor_tensor(cf[:, 2:3], cf[:, 2:3], keep[:, 0:1], ALU.mult))
            v(dve.tensor_scalar(cf[:, 2:3], cf[:, 2:3], -1.0, BIG, ALU.add, ALU.mult))
            v.mark(dve.tensor_copy(cin[:, 2, :], cf[:, 2:3].to_broadcast([P, LF])))
            dve.tensor_copy(cin[:, 3, :], neg[:, 0:1].to_broadcast([P, LF])).then_inc(s_cin, 1)
            dve.wait_ge(s_ctr, 1)
            v.mark(dve.tensor_copy(crow[:, 0:4, 0:P], bank[0][0:LF, :].rearrange("p (a b) -> p a b", a=4)))
            v.mark(dve.memset(crow[:, 6, 0:1], -BIG))
            v(dve.memset(crow[:, 7, 0:1], 0.0))
            v(dve.tensor_tensor_scan(crow[:, 6, 1:P + 1], crow[:, 2, 0:P], crow[:, 0, 0:P], -BIG, ALU.add, ALU.max))
            v(dve.tensor_tensor(crow[:, 4, 0:P], crow[:, 6, 0:P], crow[:, 2, 0:P], ALU.add))
            v.mark(dve.tensor_tensor(crow[:, 4, 0:P], crow[:, 4, 0:P], crow[:, 6, 1:P + 1], ALU.subtract))
            v(dve.tensor_tensor(crow[:, 5, 0:P], crow[:, 0, 0:P], crow[:, 6, 1:P + 1], ALU.subtract))
            dve.sem_inc(s_ce, 1)
            dve.wait_ge(s_cx, 1)
            v(dve.tensor_tensor(crow[:, 1, 0:P], crow[:, 1, 0:P], crow[:, 5, 0:P], ALU.mult))
            v(dve.tensor_tensor_scan(crow[:, 7, 1:P + 1], crow[:, 4, 0:P], crow[:, 1, 0:P], 0.0, ALU.mult, ALU.add))
            dve.tensor_tensor(crow[:, 0, 0:P], crow[:, 6, 0:P], crow[:, 3, 0:P], ALU.add).then_inc(s_cb, 1)
            dve.wait_ge(s_cbt, 1)
            v(dve.tensor_copy(cout[:, :, :], bank[1][:, 0:2 * LF].rearrange("p (a b) -> p a b", a=2)))
            dve.wait_ge(s_frow, 16)
            v.mark(dve.tensor_copy(fx[:, 1, 0:H], frow[:, 0:H]))
            v(dve.tensor_copy(fx[:, 1, H:LF].rearrange("p (h e) -> p h e", h=H), each(frow[:, 0:H], NE)))
            v(dve.tensor_tensor(fx[:, 0, :], fx[:, 1, :], cout[:, 0, :], ALU.max))
            v.mark(dve.tensor_tensor(fx[:, 1, :], fx[:, 1, :], fx[:, 0, :], ALU.subtract))
            v(dve.tensor_tensor(fx[:, 2, :], cout[:, 0, :], fx[:, 0, :], ALU.subtract))
            dve.sem_inc(s_fe, 1)
            dve.wait_ge(s_fx, 1)
            v.mark(dve.tensor_tensor(fx[:, 1, :], fx[:, 1, :], frow[:, H:W], ALU.mult))
            v(dve.tensor_tensor(fx[:, 2, :], fx[:, 2, :], cout[:, 1, :], ALU.mult))
            v.mark(dve.tensor_tensor(arow[:, H:W], fx[:, 1, :], fx[:, 2, :], ALU.add))
            dve.tensor_copy(arow[:, 0:H], fx[:, 0, 0:H]).then_inc(s_fst, 1)

            def h3(ap):
                return ap.rearrange("p (n h) -> p n h", h=H)

            def he(ap):
                return ap.rearrange("p (n f) -> p n f", f=HE)

            def bc(ap):
                return each(ap, NE)

            v(dve.tensor_tensor(h3(f4[0]), tab[:, :, HE:HE + H], tab[:, :, HE + H:W], ALU.add))
            v(dve.scalar_tensor_tensor(f4[0], f4[0], 0.2, f4[0], ALU.mult, ALU.max))
            dve.wait_ge(s_esum, 16 * NT)
            v(dve.tensor_tensor(h3(f4[1]), esum[:, :, 0:H], h3(f4[0]), ALU.max))
            v.mark(dve.tensor_tensor(h3(f4[2]), esum[:, :, 0:H], h3(f4[1]), ALU.subtract))
            v(dve.tensor_tensor(f4[3], f4[0], f4[1], ALU.subtract))
            dve.sem_inc(s_ma, 1)
            dve.wait_ge(s_mx, 1)
            v(dve.tensor_tensor(h3(f4[4]), esum[:, :, H:2 * H], h3(f4[2]), ALU.mult))
            v(dve.tensor_tensor(f4[4], f4[4], f4[3], ALU.add))
            v(dve.tensor_scalar(f4[4], f4[4], 1e-16, None, ALU.add))
            v(dve.reciprocal(f4[4], f4[4]))
            v.mark(dve.tensor_copy(he(fin[0]), esum[:, :, 2 * H:W]))
            v(dve.tensor_copy(he(fin[1]), tab[:, :, 0:HE]))

            def g3(ap):
                return ap.rearrange("p (g e) -> p g e", e=NE)

            v.mark(dve.tensor_tensor(g3(fin[0]), g3(fin[0]), bc(f4[2]), ALU.mult))
            v(dve.tensor_tensor(g3(fin[1]), g3(fin[1]), bc(f4[3]), ALU.mult))
            v(dve.tensor_tensor(fin[0], fin[0], fin[1], ALU.add))
            v(dve.tensor_tensor(g3(fin[0]), g3(fin[0]), bc(f4[4]), ALU.mult))
            v(dve.tensor_tensor(he(fin[0]), he(fin[0]), every(gatp[:, 0, :], NT), ALU.add))
            v(dve.tensor_reduce(t49[:, 1, :], he(fin[0]), AX.X, ALU.add))
            v(dve.tensor_scalar(t49[:, 1, :], t49[:, 1, :], 1.0 / HE, None, ALU.mult))
            v(dve.tensor_tensor(he(fin[0]), he(fin[0]), each(t49[:, 1, :], HE), ALU.subtract))
            v(dve.tensor_tensor(fin[1], fin[0], fin[0], ALU.mult))
            v(dve.tensor_reduce(t49[:, 0, :], he(fin[1]), AX.X, ALU.add))
            v(dve.tensor_scalar(t49[:, 0, :], t49[:, 0, :], 1.0 / HE, None, ALU.mult))
            dve.sem_inc(s_sqv, 1)
            dve.wait_ge(s_sqa, 1)
            v(dve.reciprocal(t49[:, 0, :], t49[:, 0, :]))
            v(dve.tensor_tensor(he(fin[0]), he(fin[0]), each(t49[:, 0, :], HE), ALU.mult))
            v(dve.tensor_tensor(he(fin[0]), he(fin[0]), every(gatp[:, 1, :], NT), ALU.mult))
            v(dve.tensor_tensor(he(fin[0]), he(fin[0]), every(gatp[:, 2, :], NT), ALU.add))
            v(dve.tensor_reduce(f4[0], fin[0].rearrange("p (n h e) -> p n e h", h=H, e=NE), AX.X, ALU.add))
            v(dve.tensor_scalar(f4[0], f4[0], 1.0 / H, None, ALU.mult))
            sco = f4[0].rearrange("p (n e) -> p n e", e=NE)
            rk = f4[1].rearrange("p (n e) -> p n e", e=NE)
            v(dve.memset(f4[1], 0.0))
            for a in range(NE):
                for b in range(a + 1, NE):
                    v(dve.tensor_tensor(t49[:, 2, :], sco[:, :, b], sco[:, :, a], ALU.is_gt))
                    v.mark(dve.tensor_tensor(rk[:, :, a], rk[:, :, a], t49[:, 2, :], ALU.add))
                    v(dve.tensor_scalar(t49[:, 3, :], t49[:, 2, :], -1.0, 1.0, ALU.mult, ALU.add))
                    v(dve.tensor_tensor(rk[:, :, b], rk[:, :, b], t49[:, 3, :], ALU.add))
            v(dve.tensor_reduce(t49[:, 2, :], sco, AX.X, ALU.max))
            v(dve.tensor_tensor(f4[2].rearrange("p (n e) -> p n e", e=NE), sco, each(t49[:, 2, :], NE), ALU.subtract))
            dve.sem_inc(s_ma, 1)
            dve.wait_ge(s_mx, 2)
            v(dve.tensor_scalar(f4[1], f4[1], 1.5, None, ALU.is_lt))
            v(dve.tensor_tensor(f4[1], f4[1], f4[2], ALU.mult))
            v(dve.tensor_reduce(t49[:, 2, :], rk, AX.X, ALU.add))
            v(dve.reciprocal(t49[:, 2, :], t49[:, 2, :]))
            v(dve.tensor_tensor(rk, rk, each(t49[:, 2, :], NE), ALU.mult))
            for n0 in range(0, NT, 2):
                pair = range(n0, min(n0 + 2, NT))
                for e in range(NE):
                    for n in pair:
                        b, m = n % YR, (P if n < NT - 1 else LAST)
                        if e == 0:
                            dve.wait_ge(s_yl[b], 32 * (n // YR + 1))
                        ins = dve.scalar_tensor_tensor(ring(b)[0:m, NE, :], ring(b)[0:m, e, :], rk[0:m, n, e:e + 1],
                                                       ring(b)[0:m, NE, :], ALU.mult, ALU.add)
                        if e == NE - 1:
                            ins.then_inc(s_cmb, 1)
                        else:
                            v.mark(ins)
                    if e < NE - 1:
                        v.wait()

        @block.tensor
        def _(pe):
            pe.wait_ge(s_bef, 1)
            pe.wait_ge(s_cstv, 1)
            for k in range(ROWB):
                for c in range(ROWB):
                    ins = pe.matmul(bank[0][:, k:k + 1], before[:, c, k * P:(k + 1) * P], onesb[:, :], start=c == 0, stop=c == ROWB - 1)
            ins.then_inc(s_ik, 1)
            pe.wait_ge(s_dl, 1)
            pe.wait_ge(s_cst, 2)
            for q in range(3):
                for c in range(ROWB):
                    ins = pe.transpose(bank[1 + 2 * q + c // 4][:, (c % 4) * P:(c % 4 + 1) * P], strow[:, c, q, :], ident[:, :])
                ins.then_inc(s_tr, 1)
            pe.wait_ge(s_zero, 1)
            pe.matmul(bank[7][:, 0:NT], zero[:, 0:P], zero[:, 0:NT], start=True, stop=False, skip_group_check=True)
            with pe.Fori(0, TURNS) as i:
                for hf in range(2):
                    pe.wait_ge(s_oh, i * 2 + (hf + 1))
                    for t in range(HT):
                        ins = pe.matmul(bank[7][:, 0:NT], ol[:, hf, t, :], oh[:, hf, t, :], start=False, stop=False, skip_group_check=True)
                    ins.then_inc(s_hist, 1)
                    pe.wait_ge(s_row[hf], (i + 1) * (16 * HS))
                    pe.wait_ge(s_sel, i * 2 + (hf + 1))
                    for s in range(HS):
                        pe.wait_ge(s_acc, i * (2 * HS) + (hf * HS + s + 1))
                        for m in range(KD):
                            ins = pe.matmul(slot(s)[:, m * P:(m + 1) * P], rows[:, hf, s, m * P:(m + 1) * P],
                                            onehot[:, hf, s, :], start=True, stop=True)
                        ins.then_inc(s_step, 1)
            pe.wait_ge(s_cnt, 1)
            pe.wait_ge(s_acc, 2 * HS * TURNS + SB)
            pe.matmul(bank[6][:, 0:NT], above[:, :], cnt[:, :], start=True, stop=True)
            pe.matmul(bank[6][:, 64:64 + NT], ones[:, :], cnt[:, :], start=True, stop=True)
            pe.matmul(bank[6][:, 128:129], ones[:, :], vcol[:, :], start=True, stop=True).then_inc(s_pre, 1)
            def gnn_block(b, w=512):
                pe.wait_ge(s_bc, b + 1)
                for m in range(KD):
                    for k in range(KD):
                        ins = pe.matmul(bank[5 + m][:, 0:w], ham[:, k, m * P:(m + 1) * P], acc[:, k, bass.ds(b * 512, w)],
                                        start=k == 0, stop=k == KD - 1)
                ins.then_inc(s_bo, 1)

            NG = HT // GT

            def transposes(hf, gi, par):
                for t in range(GT):
                    ins = pe.transpose(bank[par][:, :].bitcast(bf16)[:, t * P:(t + 1) * P], ol[:, hf, gi * GT + t, :], identb[:, :])
                ins.then_inc(s_trp, 1)

            def rank(i, hf, gi):
                G = i * (2 * NG) + (hf * NG + gi)
                g0 = gi * GT
                prev = run4[:, (gi - 1) % GT, GT - 1, :]
                pe.wait_ge(s_t, G + 1)
                pe.matmul(bank[3][:, 0:GT * NT], ident[:, :], every(prev, GT), start=True, stop=False, skip_group_check=True)
                for t in range(GT):
                    ins = pe.matmul(bank[3][:, t * NT:GT * NT], ol[:, hf, g0 + t, :], every(oh[:, hf, g0 + t, :], GT - t),
                                    start=False, stop=t == GT - 1, skip_group_check=True)
                ins.then_inc(s_r, 1)
                pe.wait_ge(s_ol, G + 2)
                transposes(hf if gi < NG - 1 else 1 - hf, (gi + 1) % NG, (gi + 1) % 2)
                if not (isinstance(i, int) and G == 0):
                    places(G, hf if gi else 1 - hf, (gi - 1) % NG)
                pe.wait_ge(s_olt, G + 1)
                for t in range(GT):
                    ins = pe.matmul(bank[2][:, t * P:(t + 1) * P], oltb[:, gi % 2, t, :], oltb[:, gi % 2, t, :], start=True, stop=True)
                ins.then_inc(s_eq, 1)

            def places(G, hf, gi):
                g0 = gi * GT
                prev = run4[:, (gi - 1) % GT, GT - 1, :]
                pe.wait_ge(s_u, G + 1)
                pe.wait_ge(s_gm, G)
                for t in range(GT):
                    tb = prev if t == 0 else run4[:, gi, t - 1, :]
                    pe.matmul(bank[4][:, t * NT:(t + 1) * NT], olt[:, gi % 2, t, :], tb, start=True, stop=False, skip_group_check=True)
                    ins = pe.matmul(bank[4][:, t * NT:(t + 1) * NT], ub[:, t, :], oh[:, hf, g0 + t, :], start=False, stop=True,
                                    skip_group_check=True)
                ins.then_inc(s_g, 1)

            def node_rows(n):
                pe.wait_ge(s_x3c, n + 1)
                for k in range(KD):
                    ins = pe.matmul(bank[7][:, 0:W], xt[:, k, :], wg[:, k, :], start=k == 0, stop=k == KD - 1)
                ins.then_inc(s_tabp, 1)

            def node(n, hf, gi, turn):
                if gi == 0:
                    pe.wait_ge(s_xin[hf], (turn + 1) * 16)
                    pe.wait_ge(s_tt, n + 1)
                    pe.wait_ge(s_x3, n + 1)
                    pe.matmul(bank[5][:, 0:D], ident[:, :], xin[:, hf, :], start=True, stop=False, skip_group_check=True)
                    for m in range(KD):
                        ins = pe.matmul(bank[5][:, m * P:(m + 1) * P], tt[:, m, :], ident[:, :], start=False,
                                        stop=m == KD - 1, skip_group_check=True)
                    ins.then_inc(s_px, 1)
                    if not (isinstance(n, int) and n == 0):
                        node_rows(n - 1)
                if gi == 3:
                    pe.wait_ge(s_x3, n + 2)
                    for m in range(KD):
                        ins = pe.transpose(bank[6][:, m * P:(m + 1) * P], x3[:, hf, m * P:(m + 1) * P], ident[:, :])
                    ins.then_inc(s_x3t, 1)

            pe.wait_ge(s_t0, 1)
            pe.wait_ge(s_ol, 1)
            transposes(0, 0, 0)
            def turn(i, extra):
                for hf in range(2):
                    for gi in range(NG):
                        if extra == "gnn" and gi % 2:
                            gnn_block(i * 4 + (2 * hf + gi // 2))
                        if extra == "bn" and hf == 0 and gi == 1:
                            gnn_block(CB - 1, NP - (CB - 1) * 512)
                        if extra == "nodes":
                            node(i * 2 + (hf - 2 * N0), hf, gi, i - N0)
                        if extra == "last" and hf == 0:
                            node(NT - 1, hf, gi, i - N0)
                        if extra == "last" and hf == 1 and gi == 0:
                            pe.wait_ge(s_tab, NT - 1)
                            node_rows(NT - 1)
                        rank(i, hf, gi)

            turn(0, "gnn")
            with pe.Fori(1, CT) as i:
                turn(i, "gnn")
            turn(CT, "bn")
            turn(CT + 1, "tanh")
            turn(N0, "nodes")
            with pe.Fori(N0 + 1, N1) as i:
                turn(i, "nodes")
            turn(N1, "last")
            with pe.Fori(N1 + 1, RT) as i:
                turn(i, "")
            pe.wait_ge(s_t, RT * 2 * NG + 1)
            places(RT * 2 * NG, 1, NG - 1)

            pe.wait_ge(s_wexp, 16 * (2 * NE + 1))
            pe.wait_ge(s_olt, RT * 2 * NG + 1)
            pe.wait_ge(s_gm, RT * 2 * NG + 1)
            pe.wait_ge(s_x3c, NT)
            def up(i, e, m, T):
                pe.wait_ge(s_hh, i * (NE * MF) + (e * MF + m + 1))
                for k in range(KD):
                    ins = pe.matmul(bank[m][:, 0:T], w1s[:, e, k, m * P:(m + 1) * P], x3T[:, k, bass.ds(i * TB, T)],
                                    start=k == 0, stop=k == KD - 1)
                ins.then_inc(s_up, 1)

            def down(i, e, halves=2):
                pe.wait_ge(s_hh, i * (NE * MF) + ((e + 2) * MF))
                for a in range(halves):
                    pe.wait_ge(s_yo, i * (2 * NE) + (halves * e + a + 3 - halves))
                    for k in range(MF):
                        pe.matmul(bank[4 + a][:, 0:D], hh[:, k, a * P:(a + 1) * P], w2s[:, e, k, :], start=k == 0, stop=False)
                    ins = pe.matmul(bank[4 + a][:, 0:D], ones[0:1, 0:P], b2s[0:1, e, :], start=False, stop=True)
                    ins.then_inc(s_dn, 1)

            def experts(i, halves=2):
                T = halves * P
                for e in range(NE):
                    up(i, e, 0, T)
                    up(i, e, 1, T)
                    if e:
                        down(i, e - 1, halves)
                    elif not (isinstance(i, int) and i == 0):
                        down(i - 1, NE - 1)
                    up(i, e, 2, T)
                    up(i, e, 3, T)

            experts(0)
            with pe.Fori(1, FT) as i:
                experts(i)
            experts(FT, 1)
            down(FT, NE - 1, 1)
            pe.wait_ge(s_cin, 1)
            for q in range(4):
                ins = pe.transpose(bank[0][0:LF, q * P:(q + 1) * P], cin[:, q, :], ident[:, :])
            ins.then_inc(s_ctr, 1)
            pe.wait_ge(s_cb, 1)
            pe.transpose(bank[1][:, 0:LF], crow[:, 0, 0:P], ident[0:LF, 0:LF])
            pe.transpose(bank[1][:, LF:2 * LF], crow[:, 7, 0:P], ident[0:LF, 0:LF]).then_inc(s_cbt, 1)


_INS = ["x", "src", "dst", "edge_weight", "L0_gnn_weight", "L0_gnn_gamma", "L0_gnn_beta", "L0_ffn_W_gat",
        "L0_ffn_att_src", "L0_ffn_att_dst", "L0_ffn_b_gat", "L0_ffn_ln_gamma", "L0_ffn_ln_beta", "L0_ffn_W1",
        "L0_ffn_b1", "L0_ffn_W2", "L0_ffn_b2", "L0_ffn_edge_index"]


def kernel(**inputs):
    import numpy as _np
    import concourse.bacc as _bacc
    from concourse import mybir as _mybir
    from concourse.bass_utils import run_bass_kernel_spmd as _run

    nc = _bacc.Bacc("TRN2", target_bir_lowering=False, num_devices=1)
    arrays, args = {}, []
    for name in _INS:
        a = _np.ascontiguousarray(inputs[name])
        arrays[f"in_{name}_dram"] = a
        args.append(nc.dram_tensor(f"in_{name}_dram", a.shape, _mybir.dt.from_np(a.dtype), kind="ExternalInput").ap())
    shape = inputs["x"].shape
    args.append(nc.dram_tensor("out_0_dram", shape, _mybir.dt.float32, kind="ExternalOutput").ap())
    gnn_moe(nc, *args)
    r = _run(nc, [arrays], core_ids=[0])
    return r.results[0]["out_0_dram"]
```

```python
import concourse.bass as bass
import concourse.mybir as mybir
from contextlib import ExitStack, contextmanager

P = 128
IDX = [[0, 1, 2, 3, 4, 5, 6, 7], [1, 0, 3, 2, 5, 4, 7, 6], [2, 3, 0, 1, 6, 7, 4, 5], [3, 2, 1, 0, 7, 6, 5, 4],
       [4, 5, 6, 7, 0, 1, 2, 3], [5, 4, 7, 6, 1, 0, 3, 2], [6, 7, 4, 5, 2, 3, 0, 1], [7, 6, 5, 4, 3, 2, 1, 0]]
SIGN = [[1, 1, 1, 1, 1, 1, 1, 1], [1, -1, 1, -1, 1, -1, -1, 1], [1, -1, -1, 1, 1, 1, -1, -1],
        [1, 1, -1, -1, 1, -1, 1, -1], [1, -1, -1, -1, -1, 1, 1, 1], [1, 1, -1, 1, -1, -1, -1, 1],
        [1, 1, 1, -1, -1, 1, -1, -1], [1, -1, 1, 1, -1, -1, 1, -1]]
BIG = 1e30
EPS = 1e-5


class Chain:

    def __init__(self, eng, sem):
        self.eng, self.sem, self.base, self.n, self.turn = eng, sem, 0, 0, None

    def value(self):
        return self.base + self.n if self.turn is None else self.turn + (self.base + self.n)

    def __call__(self, ins):
        self.mark(ins)
        self.wait()

    def mark(self, ins):
        ins.then_inc(self.sem, 1)
        self.n += 1

    def wait(self):
        self.eng.wait_ge(self.sem, self.value())

    @contextmanager
    def loop(self, first, end, per):
        self.base, self.n = self.base + self.n - first * per, 0
        with self.eng.Fori(first, end) as i:
            self.turn = i * per
            yield i
            assert self.n == per, (self.n, per)
        self.base, self.n, self.turn = self.base + end * per, 0, None


def gnn_moe(nc, x, src, dst, edge_weight, gnn_w, gnn_gamma, gnn_beta, w_gat, att_src, att_dst, b_gat,
            ln_gamma, ln_beta, w1, b1, w2, b2, edge_index, out):
    f32, bf16, i32, u32 = mybir.dt.float32, mybir.dt.bfloat16, mybir.dt.int32, mybir.dt.uint32
    ALU, ACT, AX = mybir.AluOpType, mybir.ActivationFunctionType, mybir.AxisListType

    N, D = x.shape
    NT = -(-N // P)
    NP = NT * P
    LAST = N - (NT - 1) * P
    E1 = src.shape[0]
    FULL = E1 // P
    REST = E1 - FULL * P
    ROWB = -(-(FULL + 1 + NT + 1) // P)
    STEPS = FULL + 1 + NT
    HS = 13
    TURNS = 32
    assert TURNS * 2 * HS >= STEPS and (TURNS + 1) * 2 * HS <= ROWB * P
    WW = 4
    assert (NT - 1) % WW == 0
    E2 = edge_index.shape[1]
    RUN = E2 // P
    GT = 4
    HT = 16
    RT = RUN // (2 * HT)
    assert RT == TURNS and RUN % (2 * HT) == 0
    CH = 2 * HT
    NE, FF = w1.shape[0], w1.shape[2]
    H = w_gat.shape[1] // NE
    HE = H * NE
    KD = D // P
    MF = FF // P
    TB = 2 * P
    FT = NP // TB
    assert FT * TB + P == NP and FT < TURNS and FT % 2 == 0
    LOADS = 7
    LN = NT // LOADS
    CT = 3
    LAG = 2
    N0 = CT + 2
    N1 = N0 + (NT - 1) // 2
    W = HE + 2 * H
    LF = H + HE
    SINK = E2

    def dram(name, shape, dt=f32):
        return nc.dram_tensor(name, shape, dt).ap()

    x1_d = dram("x1_d", [NP, D])
    rows_d = dram("rows_d", [ROWB * P, 3 * P])
    win_d = dram("win_d", [ROWB * P], i32)
    node_d = dram("node_d", [NP, W])
    x2_d = dram("x2_d", [NP, D])
    sorted_d = dram("sorted_d", [E2, 2])
    adst_d = dram("adst_d", [E2 + NP, H])
    sums_d = dram("sums_d", [E2 + 1, W])
    y_d = dram("y_d", [NP, NE, D])
    lastkey_d = dram("lastkey_d", [P, 1])

    ctx = ExitStack()
    with ctx:
        def sb(name, shape, dt=f32):
            return ctx.enter_context(nc.sbuf_tensor(name, shape, dt))

        def sem(name):
            return ctx.enter_context(nc.semaphore(name))

        regA = sb("regA", [P, NT * D])
        xa = regA[:, :].rearrange("p (n d) -> p n d", n=NT)
        gnn = regA[:, :].rearrange("p (k n) -> p k n", k=KD)
        regB = sb("regB", [P, NT * D])
        acc = regB[:, :].rearrange("p (k n) -> p k n", k=KD)
        x3T = acc
        regC = sb("regC", [P, 2 * HS * (D + P)])
        rows = regC[:, 0:2 * HS * D].rearrange("p (a s d) -> p a s d", a=2, s=HS)
        onehot = regC[:, 2 * HS * D:2 * HS * (D + P)].rearrange("p (a s d) -> p a s d", a=2, s=HS)
        w1s = regC[:, 0:NE * KD * FF].rearrange("p (e k f) -> p e k f", e=NE, k=KD)
        w2s = regC[:, NE * KD * FF:NE * KD * FF + NE * MF * D].rearrange("p (e k f) -> p e k f", e=NE, k=MF)
        iokb = regC[:, 0:ROWB * P].bitcast(i32)
        st1 = regC[:, 2 * ROWB * P:2 * ROWB * P + NT * 6].rearrange("p (n s) -> p n s", n=NT)
        EX = NE * (KD * FF + MF * D)
        EXB = EX + NE * D
        oltb = regC[:, EXB:EXB + GT * P].bitcast(bf16).rearrange("p (a b c) -> p a b c", a=2, b=GT)
        assert EXB + GT * P <= 2 * HS * (D + P)
        b2s = regC[0:1, EX:EX + NE * D].rearrange("p (e d) -> p e d", e=NE)
        RD = 3 * ROWB * P
        erow = regB[:, 0:RD].rearrange("p (c q e) -> p c q e", c=ROWB, q=3)
        eint = regB[:, RD:2 * RD].bitcast(i32).rearrange("p (c q e) -> p c q e", c=ROWB, q=3)
        strow = regB[:, 2 * RD:3 * RD].rearrange("p (c q e) -> p c q e", c=ROWB, q=3)
        before = regB[:, 3 * RD:3 * RD + ROWB * ROWB * P // 2].bitcast(bf16).rearrange("p (c k) -> p c k", c=ROWB)
        adraw = regA[:, 0:H * RUN].rearrange("p (t h) -> p t h", h=H)
        adst = regA[:, H * RUN:2 * H * RUN].rearrange("p (h t) -> p h t", h=H)
        at = 2 * H * RUN
        yo = regA[:, at:at + 2 * NE * D].rearrange("p (a e d) -> p a e d", a=2, e=NE)
        at += 2 * NE * D
        lc = regA[:, at:at + 2 * CH * W].rearrange("p (a t w) -> p a t w", a=2, t=CH)
        at += 2 * CH * W
        hc = regA[:, at:at + W * CH].rearrange("p (w t) -> p w t", w=W)
        assert at + W * CH <= NT * D
        regE = sb("regE", [P, 4 * ROWB * P + 16])
        stcol = regE[:, 0:RD].rearrange("p (q k) -> p q k", q=3)
        step_src = regE[:, RD:RD + ROWB * P].bitcast(u32)
        xin = regE[:, 0:2 * D].rearrange("p (a d) -> p a d", a=2)
        x2o = regE[:, 2 * D:4 * D].rearrange("p (a d) -> p a d", a=2)
        x3 = regE[:, 4 * D:6 * D].rearrange("p (a d) -> p a d", a=2)
        olt = regE[:, 6 * D:6 * D + 2 * GT * P].rearrange("p (a b c) -> p a b c", a=2, b=GT)
        at = 6 * D + 2 * GT * P
        run4 = regE[:, at:at + GT * GT * NT].rearrange("p (a b c) -> p a b c", a=GT, b=GT)
        at += GT * GT * NT
        ub = regE[:, at:at + GT * P // 2].bitcast(bf16).rearrange("p (a b) -> p a b", a=GT)
        assert at + GT * P // 2 <= 4 * ROWB * P + 16
        icol = regE[:, 0:RUN].bitcast(i32)
        hold = regE[:, RUN:2 * RUN]
        crow = regE[0:LF, 2 * RUN:2 * RUN + 8 * (P + 1)].rearrange("p (a b) -> p a b", a=8)
        kint = sb("kint", [P, RUN], i32)
        sint = sb("sint", [P, RUN], i32)
        pay = sb("pay", [P, RUN + CH, 2])
        lo = sb("lo", [P, RUN + HT], bf16)
        hi = sb("hi", [P, RUN + HT], bf16)
        ol = sb("ol", [P, 2, HT, P], bf16)
        ohf = sb("ohf", [P, 2 * HT * NT], bf16)
        oh = ohf[:, :].rearrange("p (a b c) -> p a b c", a=2, b=HT)
        olf = ol[:, :, :, :].rearrange("p a b c -> p (a b c)").bitcast(f32)
        hh = olf[:, 0:MF * TB].rearrange("p (m t) -> p m t", m=MF)
        at = MF * TB
        sc, sc2, ww, rr = [olf[:, at + i * H * CH:at + (i + 1) * H * CH].rearrange("p (h t) -> p h t", h=H) for i in range(4)]
        at += 4 * H * CH
        mb = olf[:, at:at + H * (CH + 1)].rearrange("p (h t) -> p h t", h=H)
        nm = ohf[:, :].bitcast(f32)[:, 0:HE * CH].rearrange("p (f t) -> p f t", f=HE)
        neg = kint[:, :].bitcast(f32)
        keep = sint[:, :].bitcast(f32)
        iot = sb("iot", [P, P], i32)
        iof = sb("iof", [P, P])
        iob = sb("iob", [P, P], bf16)
        pidx = sb("pidx", [P, ROWB], i32)
        pidf = sb("pidf", [P, ROWB])
        ident = sb("ident", [P, P])
        identb = sb("identb", [P, P], bf16)
        above = sb("above", [P, P])
        ones = sb("ones", [P, P])
        onesb = sb("onesb", [P, 1], bf16)
        ZC = 148
        ZR = (E2 + NP) * H // P // ZC
        assert ZC * ZR * P == (E2 + NP) * H
        zero = sb("zero", [P, ZC])
        eps = sb("eps", [P, 1])
        sinkrow = sb("sinkrow", [1, W])
        mv1 = sb("mv1", [P, NT, 2])
        sd1 = sb("sd1", [P, NT])
        rs1 = sb("rs1", [P, NT])
        nb1 = sb("nb1", [P, NT])
        gam = sb("gam", [P, KD])
        bet = sb("bet", [P, KD])
        CB = -(-NP // 512)
        stb = sb("stb", [P, KD, CB, 6])
        mvb = sb("mvb", [P, KD, 2])
        sdb = sb("sdb", [P, KD])
        scb = sb("scb", [P, KD])
        bib = sb("bib", [P, KD])
        lwin = sb("lwin", [P, ROWB], i32)
        lv = sb("lv", [P, ROWB])
        ikf = sb("ikf", [P, ROWB])
        jkf = sb("jkf", [P, ROWB])
        iku = sb("iku", [P, ROWB], u32)
        jki = sb("jki", [P, ROWB], i32)
        wins = sb("wins", [1, 2 * TURNS, 16], i32)
        idxr = sb("idxr", [P, 2, 16], u32)
        cnt = sb("cnt", [P, NT])
        basef = sb("basef", [P, NT])
        tots = sb("tots", [P, NT])
        totx = sb("totx", [P, NT + 1])
        gm = sb("gm", [P, GT, NT])
        posr = sb("posr", [P, 2, HT], u32)
        payr = sb("payr", [P, 2, HT, 2])
        tt = sb("tt", [P, KD, P])
        xt = sb("xt", [P, KD, P])
        ham4 = xt[:, :, :].rearrange("p k c -> p (k c)")
        stn = sb("stn", [P, 6])
        mvn = sb("mvn", [P, 2])
        sdn = sb("sdn", [P, 1])
        rsn = sb("rsn", [P, 1])
        wg = sb("wg", [P, KD, W])
        attb = sb("attb", [P, 2, HE])
        wt = sb("wt", [P, HE])
        tab = sb("tab", [P, NT, W])
        vcol = sb("vcol", [P, 1])
        runp = sb("runp", [P, 4])
        runi = sb("runi", [P, 1], i32)
        posf = sb("posf", [P, GT])
        posq = sb("posq", [P, GT], i32)
        q49 = sb("q49", [P, NT], i32)
        lastk = sb("lastk", [P, 1])
        sidx = sb("sidx", [P, NT], u32)
        eidx = sb("eidx", [P, NT], u32)
        t49 = sb("t49", [P, 4, NT])
        b1s = sb("b1s", [P, NE, MF])
        gatp = sb("gatp", [P, 3, HE])
        key0 = sb("key0", [P, 1])
        keyp = sb("keyp", [P, 1])
        key0u = sb("key0u", [P, 1], u32)
        arow = sb("arow", [P, W])
        grow = sb("grow", [P, 2, HT, W])
        gidx = sb("gidx", [P, 2, HT], u32)
        ham = grow[:, :, :, :].rearrange("p a b c -> p (a b c)")[:, 0:KD * D].rearrange("p (k d) -> p k d", k=KD)
        last = sb("last", [P, W])
        cin = sb("cin", [P, 4, LF])
        cout = sb("cout", [P, 2, LF])
        same = lo[:, 0:RUN]
        nfirst = sb("nfirst", [P, 1])
        fidx = sb("fidx", [P, 1], u32)
        cf = sb("cf", [P, 4])
        frow = sb("frow", [P, W])
        fx = sb("fx", [P, 4, LF])
        disorder = fx[:, 0, 0:1]
        unsorted = fx[:, 1, 0:1].bitcast(i32)
        dcol = cin[:, 0:2, 0:WW]
        esum = pay[:, :, :].rearrange("p t w -> p (t w)")[:, 0:NT * W].rearrange("p (n w) -> p n w", n=NT)

        fin = [regA[:, i * NT * HE:(i + 1) * NT * HE] for i in range(6)]
        f4 = [regA[:, 6 * NT * HE + i * NT * H:6 * NT * HE + (i + 1) * NT * H] for i in range(16)]
        assert 6 * NT * HE + 16 * NT * H <= NT * D
        YB = NT * D // ((NE + 1) * D)
        YR = YB + 2 * HS * (D + P) // ((NE + 1) * D)

        PARTS = ((0, NT // 4 * 2), (NT // 4 * 2, NT))

        def gate(n):
            return f4[1][:, n * NE:(n + 1) * NE]

        diag = regE[:, 0:2 * NE * P].rearrange("p (a e c) -> p a e c", a=2, e=NE)

        def ring(b):
            reg, k = (regB, b) if b < YB else (regC, b - YB)
            return reg[:, k * (NE + 1) * D:(k + 1) * (NE + 1) * D].rearrange("p (e d) -> p e d", e=NE + 1)


        bank = [ctx.enter_context(nc.psum_tensor(f"bank{i}", [P, 512], f32)) for i in range(8)]

        def slot(s):
            return bank[s % 7][:, 0:D]

        SB = HS - 7

        s_fill = sem("s_fill")
        s_x = [sem(f"s_xpart{i}") for i in range(LOADS)]
        s_edge = sem("s_edge")
        s_gat = sem("s_gat")
        s_par = sem("s_par")
        s_cst = sem("s_cst")
        s_cstv = sem("s_cstv")
        s_mv1, s_sd1, s_rs1, s_x1, s_x1d = sem("s_mv1"), sem("s_sd1"), sem("s_rs1"), sem("s_x1"), sem("s_x1d")
        s_rows, s_rowsd, s_bef, s_ik, s_iku, s_strow, s_dl, s_tr, s_win, s_wind = [
            sem(n) for n in ("s_rows", "s_rowsd", "s_bef", "s_ik", "s_iku", "s_strow", "s_dl", "s_tr", "s_win", "s_wind")]
        s_v = sem("s_v")
        s_idx, s_oh, s_hist, s_sel, s_step, s_acc = [sem(n) for n in ("s_idx", "s_oh", "s_hist", "s_sel", "s_step", "s_acc")]
        s_row = [sem("s_row0"), sem("s_row1")]
        s_zero, s_adz = sem("s_zero"), sem("s_adz")
        s_cnt, s_pre, s_t0 = sem("s_cnt"), sem("s_pre"), sem("s_t0")
        s_icol, s_lastk, s_lastd = sem("s_icol"), sem("s_lastk"), sem("s_lastd")
        s_bo, s_bn, s_bc, s_sdb, s_bnr, s_tanh = [sem(n) for n in ("s_bo", "s_bn", "s_bc", "s_sdb", "s_bnr", "s_tanh")]
        s_ol, s_r, s_t, s_trp, s_olt, s_eq, s_u, s_g, s_gm, s_pos = [
            sem(n) for n in ("s_ol", "s_r", "s_t", "s_trp", "s_olt", "s_eq", "s_u", "s_g", "s_gm", "s_pos")]
        s_scat = [sem("s_scat0"), sem("s_scat1")]
        s_xin = [sem("s_xin0"), sem("s_xin1")]
        s_x2d = [sem("s_x2d0"), sem("s_x2d1")]
        s_px, s_mvn, s_sdn, s_x2, s_x3, s_x3t, s_x3c, s_tabp, s_tab = [
            sem(n) for n in ("s_px", "s_mvn", "s_sdn", "s_x2", "s_x3", "s_x3t", "s_x3c", "s_tabp", "s_tab")]
        s_wexp, s_noded, s_seidx, s_ads, s_srt, s_k0, s_arow, s_adr = [
            sem(n) for n in ("s_wexp", "s_noded", "s_seidx", "s_ads", "s_srt", "s_k0", "s_arow", "s_adr")]
        s_gidx = sem("s_gidx")
        s_grow = [sem("s_grow0"), sem("s_grow1")]
        s_sc, s_ww, s_lc = sem("s_sc"), sem("s_ww"), sem("s_lc")
        s_lcd = [sem("s_lcd0"), sem("s_lcd1")]
        s_up, s_hh, s_dn, s_yo = sem("s_up"), sem("s_hh"), sem("s_dn"), sem("s_yo")
        s_yd = [sem("s_yd0"), sem("s_yd1")]
        s_cin, s_ctr, s_ce, s_cx, s_cb, s_cbt, s_fidx, s_frow, s_fe, s_fx, s_fst, s_fixed = [
            sem(n) for n in ("s_cin", "s_ctr", "s_ce", "s_cx", "s_cb", "s_cbt", "s_fidx", "s_frow", "s_fe", "s_fx",
                             "s_fst", "s_fixed")]
        s_esum = [sem("s_esum0"), sem("s_esum1")]
        s_dis, s_uns, s_gnn, s_ham = [sem(n) for n in ("s_dis", "s_uns", "s_gnn", "s_ham")]
        s_uidx, s_urow, s_usel, s_uprod, s_uv = [sem(n) for n in ("s_uidx", "s_urow", "s_usel", "s_uprod", "s_uv")]
        s_tt, s_begun, s_begun_v = [sem(n) for n in ("s_tt", "s_begun", "s_begun_v")]
        s_ma, s_mx, s_sqv, s_sqa = sem("s_ma"), sem("s_mx"), sem("s_sqv"), sem("s_sqa")
        s_yl = [sem(f"s_yl{i}") for i in range(YR)]
        s_cmb, s_cmbp, s_gate, s_diag, s_sum = [sem(n) for n in ("s_cmb", "s_cmbp", "s_gate", "s_diag", "s_sum")]
        OB = 4
        s_out = [sem(f"s_out{i}") for i in range(OB)]

        def each(ap, n):
            return ap.unsqueeze(2).to_broadcast([ap.shape[0], ap.shape[1], n])

        def every(ap, n):
            return ap.unsqueeze(1).to_broadcast([ap.shape[0], n, ap.shape[1]])

        block = ctx.enter_context(nc.Block())

        @block.sync
        def _(sp):
            sp.sem_inc(s_hist, 2)
            sp.sem_inc(s_hh, MF)
            sp.sem_inc(s_yo, 2)
            sp.sem_inc(s_acc, SB)
            sp.sem_inc(s_g, 3)
            sp.sem_inc(s_t, 1)
            sp.sem_inc(s_u, 1)
            sp.sem_inc(s_gm, 1)
            sp.sem_inc(s_px, 2)
            sp.sem_inc(s_x3, 1)
            sp.sem_inc(s_bc, 1)
            for s in s_x2d + s_lcd + s_yd:
                sp.sem_inc(s, 16)
            sp.wait_ge(s_fill, 1)
            with nc.allow_non_contiguous_dma(reason="short parameter vectors"):
                for q, a in ((0, src), (1, dst)):
                    fb = (ROWB - 1) * P
                    sp.dma_start(eint[:, 0:ROWB - 1, q, :], a[0:fb * P].rearrange("(c p e) -> p c e", p=P, e=P)).then_inc(s_edge, 16)
                    sp.dma_start(eint[0:FULL - fb, ROWB - 1, q, :], a[fb * P:FULL * P].rearrange("(p e) -> p e", e=P)).then_inc(s_edge, 16)
                    sp.dma_start(eint[FULL - fb:FULL - fb + 1, ROWB - 1, q, 0:REST], a[FULL * P:E1].rearrange("(a e) -> a e", a=1)).then_inc(s_edge, 16)
                E1N = E1 - 1 - (E1 - 1) // P * P
                FN = (E1 - 1) // P
                sp.dma_start(eint[:, 0:ROWB - 1, 2, :], dst[1:1 + fb * P].rearrange("(c p e) -> p c e", p=P, e=P)).then_inc(s_edge, 16)
                sp.dma_start(eint[0:FN - fb, ROWB - 1, 2, :], dst[1 + fb * P:1 + FN * P].rearrange("(p e) -> p e", e=P)).then_inc(s_edge, 16)
                sp.dma_start(eint[FN - fb:FN - fb + 1, ROWB - 1, 2, 0:E1N], dst[1 + FN * P:E1].rearrange("(a e) -> a e", a=1)).then_inc(s_edge, 16)
                sp.dma_start(erow[:, 0:ROWB - 1, 2, :], edge_weight[0:fb * P].rearrange("(c p e) -> p c e", p=P, e=P)).then_inc(s_edge, 16)
                sp.dma_start(erow[0:FULL - fb, ROWB - 1, 2, :], edge_weight[fb * P:FULL * P].rearrange("(p e) -> p e", e=P)).then_inc(s_edge, 16)
                sp.dma_start(erow[FULL - fb:FULL - fb + 1, ROWB - 1, 2, 0:REST], edge_weight[FULL * P:E1].rearrange("(a e) -> a e", a=1)).then_inc(s_edge, 16)
                for c in range(LOADS):
                    n0, n1 = c * LN, min((c + 1) * LN, NT - 1)
                    sp.dma_start(xa[:, n0:n1, :], x[n0 * P:n1 * P, :].rearrange("(n p) d -> p n d", p=P)).then_inc(s_x[c], 16)
                sp.dma_start(xa[0:LAST, NT - 1, :], x[(NT - 1) * P:N, :]).then_inc(s_x[LOADS - 1], 16)
                sp.dma_start(kint[:, :], edge_index[1, :].rearrange("(p t) -> p t", p=P)).then_inc(s_gat, 16)
                sp.dma_start(sint[:, :], edge_index[0, :].rearrange("(p t) -> p t", p=P)).then_inc(s_gat, 16)
                for g in range(4):
                    sp.dma_start(ham4[32 * g:32 * g + 32, :], gnn_w[:, :]).then_inc(s_par, 16)
                sp.dma_start(gam[:, :], gnn_gamma.rearrange("(m p) -> p m", p=P)).then_inc(s_par, 16)
                sp.dma_start(bet[:, :], gnn_beta.rearrange("(m p) -> p m", p=P)).then_inc(s_par, 16)
                sp.dma_start(wg[:, :, 0:HE], w_gat.rearrange("(k p) f -> p k f", p=P)).then_inc(s_par, 16)
                for q, a in ((0, att_src), (1, att_dst)):
                    sp.dma_start(attb[:, q, :], a.rearrange("h e -> (h e)").partition_broadcast(P)).then_inc(s_par, 16)
                for q, a in ((0, b_gat), (1, ln_gamma), (2, ln_beta)):
                    sp.dma_start(gatp[:, q, :], a.partition_broadcast(P)).then_inc(s_par, 16)
                for e in range(NE):
                    sp.dma_start(b1s[:, e, :], b1[e, :].rearrange("(m p) -> p m", p=P)).then_inc(s_par, 16)
            sp.wait_ge(s_rows, 1)
            sp.dma_start(rows_d.rearrange("(c p) w -> p c w", p=P), erow[:, :, :, :].rearrange("p c q e -> p c (q e)")).then_inc(s_rowsd, 16)
            for c in range(LOADS):
                sp.wait_ge(s_x1, c + 1)
                sp.dma_start(x1_d[c * LN * P:(c + 1) * LN * P, :].rearrange("(n p) d -> p n d", p=P),
                             xa[:, c * LN:(c + 1) * LN, :]).then_inc(s_x1d, 16)
            sp.wait_ge(s_win, 1)
            with nc.allow_non_contiguous_dma(reason="896 window numbers"):
                sp.dma_start(win_d.rearrange("(c p) -> p c", p=P), jki[:, :]).then_inc(s_wind, 16)
            sp.wait_ge(s_wind, 16)
            sp.dma_start(wins[:, :, 0:HS], win_d[0:2 * TURNS * HS].rearrange("(o a s) -> o a s", o=1, s=HS)).then_inc(s_wind, 16)

            sp.wait_ge(s_zero, 2)
            sp.dma_start(adst_d.rearrange("(p q t) h -> p q (t h)", p=P, q=ZR), every(zero[:, :], ZR)).then_inc(s_adz, 16)
            sp.dma_start(sorted_d.rearrange("(p q t) w -> p q (t w)", p=P, q=HT), every(zero[:, 0:P], HT)).then_inc(s_adz, 16)
            sp.dma_start(sums_d[SINK:SINK + 1, :], sinkrow[:, :]).then_inc(s_adz, 16)

            sp.wait_ge(s_gnn, 1)
            for e in range(NE):
                sp.dma_start(w1s[:, e, :, :], w1[e].rearrange("(k p) f -> p k f", p=P)).then_inc(s_wexp, 16)
                sp.dma_start(w2s[:, e, :, :], w2[e].rearrange("(k p) f -> p k f", p=P)).then_inc(s_wexp, 16)

            sp.dma_start(b2s, b2.rearrange("(a e) d -> a e d", a=1)).then_inc(s_wexp, 16)

            def load_x(n, hf, rows_n=P):
                sp.wait_ge(s_px, n + 1)
                sp.dma_start(xin[0:rows_n, hf, :], x[bass.ds(n * P, rows_n), :]).then_inc(s_xin[hf], 16)

            def store_x2(n, hf):
                sp.wait_ge(s_x2, n + 1)
                sp.dma_start(x2_d[bass.ds(n * P, P), :], x2o[:, hf, :]).then_inc(s_x2d[hf], 16)

            with sp.Fori(0, (NT - 1) // 2) as i:
                load_x(i * 2, 0)
                load_x(i * 2 + 1, 1)
                store_x2(i * 2, 0)
                store_x2(i * 2 + 1, 1)
            load_x(NT - 1, 0, LAST)
            store_x2(NT - 1, 0)
            sp.wait_ge(s_tab, NT)
            sp.dma_start(node_d.rearrange("(n p) w -> p n w", p=P), tab[:, :, :]).then_inc(s_noded, 16)
            for hf in range(2):
                sp.wait_ge(s_scat[hf], 16 * HT * RT)
            sp.dma_start(pay[:, 0:RUN, :], sorted_d.rearrange("(p t) w -> p t w", p=P)).then_inc(s_srt, 16)
            with nc.allow_non_contiguous_dma(reason="one key of each partition"):
                sp.wait_ge(s_lastk, 1)
                sp.dma_start(lastkey_d, lastk[:, :]).then_inc(s_lastd, 16)
                sp.wait_ge(s_lastd, 16)
                sp.dma_start(keyp[1:P, :], lastkey_d[0:P - 1, :]).then_inc(s_lastd, 16)
            def store_y(t):
                for a in range(2):
                    sp.wait_ge(s_yo, t * (2 * NE) + (2 * NE + 1 + a))
                    sp.dma_start(y_d[bass.ds(t * TB + a * P, P), :, :], yo[:, a, :, :]).then_inc(s_yd[a], 16)

            for t in range(LAG):
                store_y(t)
            sp.wait_ge(s_ads, 16 * NT)
            sp.dma_start(adraw, adst_d[0:E2, :].rearrange("(p t) h -> p t h", p=P)).then_inc(s_adr, 16)

            def store_sums(t, hf):
                sp.wait_ge(s_lc, t + 1)
                sp.dma_start(sums_d[0:E2, :].rearrange("(p t) w -> p t w", p=P)[:, bass.ds(t * CH, CH), :],
                             lc[:, hf, :, :]).then_inc(s_lcd[hf], 16)

            AHEAD = 4
            for t in range(LAG, AHEAD):
                store_y(t)
                store_sums(t - LAG, (t - LAG) % 2)
            with sp.Fori(AHEAD // 2, FT // 2) as i:
                for hf in range(2):
                    store_y(i * 2 + hf)
                    store_sums(i * 2 + (hf - LAG), (hf - LAG) % 2)
            sp.wait_ge(s_yo, (2 * FT + 1) * NE + 2)
            sp.dma_start(y_d[FT * TB:FT * TB + P, :, :], yo[:, 0, :, :]).then_inc(s_yd[0], 16)
            for t in range(FT - LAG, TURNS):
                store_sums(t, t % 2)
            sp.wait_ge(s_yd[0], 16 * (FT + 2))
            sp.wait_ge(s_yd[1], 16 * (FT + 1))
            sp.wait_ge(s_x2d[0], 16 * (NT // 2 + 2))
            sp.wait_ge(s_x2d[1], 16 * (NT // 2 + 1))
            sp.wait_ge(s_fixed, 16)
            def store_out(k):
                m = P if k < NT - 1 else LAST
                sp.wait_ge(s_cmbp if k % 2 else s_cmb, k // 2 + 1)
                sp.dma_start(out[k * P:k * P + m, :], ring(k % YR)[0:m, NE, :]).then_inc(s_out[k % OB], 16)

            LEAD = 4
            stored = 0
            for n in range(NT):
                b, m = n % YR, (P if n < NT - 1 else LAST)
                if n >= YR:
                    while stored < n - YR + LEAD:
                        store_out(stored)
                        stored += 1
                    sp.wait_ge(s_out[(n - YR) % OB], 16 * ((n - YR) // OB + 1))
                sp.dma_start(ring(b)[0:m, 0:NE, :], y_d[n * P:n * P + m, :, :]).then_inc(s_yl[b], 16)
                sp.dma_start(ring(b)[0:m, NE, :], x2_d[n * P:n * P + m, :]).then_inc(s_yl[b], 16)
            for k in range(stored, NT):
                store_out(k)
            for b in range(OB):
                sp.wait_ge(s_out[b], 16 * len(range(b, NT, OB)))

        @block.gpsimd
        def _(pool):
            pool.iota(iot[:, :], pattern=[[1, P]], base=0, channel_multiplier=0)
            pool.iota(iokb[:, :], pattern=[[1, ROWB * P]], base=0, channel_multiplier=0)
            pool.iota(pidx[:, :], pattern=[[P, ROWB]], base=0, channel_multiplier=1)
            pool.memset(ident[:, :], 0.0)
            pool.memset(above[:, :], 1.0)
            pool.memset(ones[:, :], 1.0).then_inc(s_cst, 1)
            pool.wait_ge(s_cst, 1)
            pool.affine_select(out=ident[:, :], in_=ident[:, :], compare_op=ALU.not_equal, fill=1.0, base=0,
                               pattern=[[-1, P]], channel_multiplier=1)
            pool.affine_select(out=above[:, :], in_=above[:, :], compare_op=ALU.is_gt, fill=0.0, base=0,
                               pattern=[[1, P]], channel_multiplier=-1).then_inc(s_cst, 1)
            pool.wait_ge(s_iku, 1)
            pool.wait_ge(s_rowsd, 16)
            for c in range(ROWB):
                pool.indirect_dma_start(strow[:, c, :, :].rearrange("p q e -> p (q e)"), None, rows_d,
                                        bass.IndirectOffsetOnAxis(ap=iku[:, c:c + 1], axis=0)).then_inc(s_strow, 16)
            pool.wait_ge(s_x1d, 16 * LOADS)
            with pool.Fori(0, TURNS) as i:
                for hf in range(2):
                    pool.wait_ge(s_idx, i * 2 + (hf + 1))
                    pool.sem_inc(s_begun, 1)
                    for s in range(HS):
                        pool.indirect_dma_start(rows[:, hf, s, :], None, x1_d,
                                                bass.IndirectOffsetOnAxis(ap=idxr[:, hf, s:s + 1], axis=0)
                                                ).then_inc(s_row[hf], 16)
            pool.wait_ge(s_uns, 1)
            uns = pool.value_load(unsorted[0:1, 0:1], min_val=0, max_val=1)
            with pool.If(uns > 0):
                with pool.Fori(0, FULL + 1) as k:
                    pool.wait_ge(s_uidx, k + 1)
                    pool.sem_inc(s_begun, 1)
                    pool.indirect_dma_start(rows[:, 0, 0, :], None, x1_d,
                                            bass.IndirectOffsetOnAxis(ap=idxr[:, 0, 0:1], axis=0)).then_inc(s_urow, 16)
            pool.wait_ge(s_adz, 16 * 3)
            with pool.Fori(0, RT) as i:
                for hf in range(2):
                    for g in range(HT // GT):
                        pool.wait_ge(s_pos, i * (2 * HT // GT) + (hf * (HT // GT) + g + 1))
                        pool.sem_inc(s_begun, 1)
                        for t in range(g * GT, (g + 1) * GT):
                            pool.indirect_dma_start(sorted_d, bass.IndirectOffsetOnAxis(ap=posr[:, hf, t:t + 1], axis=0),
                                                    payr[:, hf, t, :], None, bounds_check=E2 - 1,
                                                    oob_is_err=False).then_inc(s_scat[hf], 16)
            pool.wait_ge(s_tab, NT)
            pool.wait_ge(s_seidx, 1)
            pool.wait_ge(s_x2d[0], 16 * (NT // 2 + 2))
            pool.wait_ge(s_x2d[1], 16 * (NT // 2 + 1))
            pool.iota(icol, pattern=[[1, RUN]], base=0, channel_multiplier=0).then_inc(s_icol, 1)
            for n in range(NT):
                pool.indirect_dma_start(adst_d, bass.IndirectOffsetOnAxis(ap=sidx[:, n:n + 1], axis=0),
                                        tab[:, n, HE + H:W], None).then_inc(s_ads, 16)
            pool.wait_ge(s_k0, 1)
            pool.wait_ge(s_noded, 16)
            pool.indirect_dma_start(arow[:, :], None, node_d, bass.IndirectOffsetOnAxis(ap=key0u[:, :], axis=0)).then_inc(s_arow, 16)
            run = pool.value_load(runi[0:1, 0:1], min_val=1, max_val=RUN)
            with pool.Fori(0, RT) as i:
                for hf in range(2):
                    pool.wait_ge(s_gidx, i * 2 + (hf + 1))
                    pool.sem_inc(s_begun, 1)
                    with pool.If(run > i * CH + hf * HT):
                        for t in range(HT):
                            pool.indirect_dma_start(grow[:, hf, t, :], None, node_d,
                                                    bass.IndirectOffsetOnAxis(ap=gidx[:, hf, t:t + 1], axis=0)
                                                    ).then_inc(s_grow[hf], 16)
            pool.wait_ge(s_fidx, 1)
            for s in s_lcd:
                pool.wait_ge(s, 16 * (TURNS // 2 + 1))
            pool.indirect_dma_start(frow[:, :], None, sums_d, bass.IndirectOffsetOnAxis(ap=fidx[:, :], axis=0)).then_inc(s_frow, 16)
            pool.wait_ge(s_fst, 1)
            pool.indirect_dma_start(sums_d, bass.IndirectOffsetOnAxis(ap=fidx[:, :], axis=0), arow[:, :], None).then_inc(s_fixed, 16)
            pool.wait_ge(s_fixed, 16)
            for q, (n0, n1) in enumerate(PARTS):
                for n in range(n0, n1):
                    pool.indirect_dma_start(esum[:, n, :], None, sums_d, bass.IndirectOffsetOnAxis(ap=eidx[:, n:n + 1], axis=0)
                                            ).then_inc(s_esum[q], 16)

        @block.scalar
        def _(act):
            act.wait_ge(s_cstv, 1)
            for c in range(LOADS + 1):
                if c < LOADS:
                    part = slice(c * LN, (c + 1) * LN)
                    act.wait_ge(s_mv1, c + 1)
                    act.activation(sd1[:, part], mv1[:, part, 1], ACT.Sqrt, bias=eps[:, :], scale=1.0).then_inc(s_sd1, 1)
                if c:
                    act.wait_ge(s_rs1, c)
                    for n in range((c - 1) * LN, c * LN):
                        ins = act.activation(xa[:, n, :], xa[:, n, :], ACT.Identity, bias=nb1[:, n:n + 1], scale=rs1[:, n:n + 1])
                    ins.then_inc(s_x1, 1)
            act.wait_ge(s_par, 16 * 16)
            S8 = D // 8
            for q in range(8):
                r = slice(32 * (q % 4), 32 * (q % 4) + 32)
                for p in range(8):
                    j = IDX[p][q]
                    act.activation(ham[r, q // 4, p * S8:(p + 1) * S8], ham4[r, j * S8:(j + 1) * S8], ACT.Copy,
                                   scale=float(SIGN[p][q])).then_inc(s_ham, 1)

            def olt_copy(g, par):
                act.wait_ge(s_trp, g + 1)
                act.wait_ge(s_g, g + 2)
                one = bank[par][:, :].bitcast(bf16)[:, 0:GT * P]
                act.activation(oltb[:, par, :, :].rearrange("p a b -> p (a b)"), one, ACT.Copy)
                act.activation(olt[:, par, :, :].rearrange("p a b -> p (a b)"), one, ACT.Copy).then_inc(s_olt, 1)

            def rank(G, gi):
                act.wait_ge(s_r, G + 1)
                act.wait_ge(s_g, G + 1)
                act.activation(run4[:, gi, :, :].rearrange("p a b -> p (a b)"), bank[3][:, 0:GT * NT], ACT.Copy).then_inc(s_t, 1)
                olt_copy(G + 1, (gi + 1) % 2)

            def next_tanh(n):
                act.activation(tt[:, :, :], gnn[:, :, bass.ds(n * P, P)], ACT.Copy).then_inc(s_tt, 1)

            def node(n, hf, gi, turn, ahead=True):
                if gi == 0 and not (isinstance(n, int) and n == 0):
                    act.wait_ge(s_tabp, n)
                    act.activation(tab[:, bass.ds(n - 1, 1), :].rearrange("p a w -> p (a w)"), bank[7][:, 0:W], ACT.Copy).then_inc(s_tab, 1)
                if gi == 1:
                    act.wait_ge(s_mvn, n + 1)
                    act.activation(sdn[:, :], mvn[:, 1:2], ACT.Sqrt, bias=eps[:, :], scale=1.0).then_inc(s_sdn, 1)
                    act.wait_ge(s_x2d[hf], (turn + 1) * 16)
                    act.activation(x2o[:, hf, :], bank[5][:, 0:D], ACT.Copy).then_inc(s_x2, 1)
                    if ahead:
                        next_tanh(n + 1)
                if gi == 3:
                    act.wait_ge(s_x3t, n + 1)
                    act.activation(xt[:, :, :], bank[6][:, 0:D].rearrange("p (k n) -> p k n", k=KD), ACT.Copy)
                    act.activation(x3T[:, :, bass.ds(n * P, P)], bank[6][:, 0:D].rearrange("p (k n) -> p k n", k=KD),
                                   ACT.Copy).then_inc(s_x3c, 1)

            def gnn_block(b, w=512):
                act.wait_ge(s_bo, b + 1)
                for m in range(KD):
                    ins = act.activation(gnn[:, m, bass.ds(b * 512, w)], bank[5 + m][:, 0:w], ACT.Copy)
                ins.then_inc(s_bc, 1)

            def turn(i, extra):
                for hf in range(2):
                    for gi in range(NG):
                        rank(i * (2 * NG) + (hf * NG + gi), gi)
                        if extra == "gnn" and gi % 2:
                            gnn_block(i * 4 + (2 * hf + gi // 2))
                        if extra == "bn" and hf == 0 and gi == 1:
                            gnn_block(CB - 1, NP - (CB - 1) * 512)
                        if extra == "bn" and hf == 1 and gi == 0:
                            act.wait_ge(s_sdb, 1)
                            act.activation(sdb[:, :], mvb[:, :, 1], ACT.Sqrt, bias=eps[:, :], scale=1.0).then_inc(s_sdb, 1)
                        if extra == "tanh":
                            k = hf * NG + gi
                            act.wait_ge(s_bnr, 1)
                            for m in range(KD):
                                part = gnn[:, m, k * (NP // 8):(k + 1) * (NP // 8)]
                                act.activation(part, part, ACT.Tanh, bias=bib[:, m:m + 1], scale=scb[:, m:m + 1]).then_inc(s_tanh, 1)
                        if extra == "nodes":
                            node(i * 2 + (hf - 2 * N0), hf, gi, i - N0)
                        if extra == "last" and hf == 0:
                            node(NT - 1, hf, gi, i - N0, ahead=False)
                        if extra == "last" and hf == 1 and gi == 0:
                            node(NT, hf, gi, i - N0)

            NG = HT // GT
            olt_copy(0, 0)
            turn(0, "gnn")
            with act.Fori(1, CT) as i:
                turn(i, "gnn")
            turn(CT, "bn")
            turn(CT + 1, "tanh")
            act.wait_ge(s_tanh, 8 * KD)
            next_tanh(0)
            turn(N0, "nodes")
            with act.Fori(N0 + 1, N1) as i:
                turn(i, "nodes")
            turn(N1, "last")
            with act.Fori(N1 + 1, RT) as i:
                turn(i, "")

            def gelu(i, e, m, T):
                act.wait_ge(s_up, i * (NE * MF) + (e * MF + m + 1))
                act.activation(hh[:, m, 0:T], bank[m][:, 0:T], ACT.Gelu, bias=b1s[:, e, m:m + 1], scale=1.0).then_inc(s_hh, 1)

            def outputs(i, e, halves=2):
                for a in range(halves):
                    act.wait_ge(s_dn, i * (2 * NE) + (halves * e + a + 1))
                    if e == 0:
                        act.wait_ge(s_yd[a], (i + 1) * 16)
                    act.activation(yo[:, a, e, :], bank[4 + a][:, 0:D], ACT.Copy).then_inc(s_yo, 1)

            def experts(i, halves=2):
                T = halves * P
                for e in range(NE):
                    first = isinstance(i, int) and i == 0 and e == 0
                    if not first:
                        act.wait_ge(s_dn, i * (2 * NE) + halves * e)
                    gelu(i, e, 0, T)
                    gelu(i, e, 1, T)
                    if e:
                        outputs(i, e - 1, halves)
                    elif not first:
                        outputs(i - 1, NE - 1)
                    gelu(i, e, 2, T)
                    gelu(i, e, 3, T)

            def exponentials(i):
                act.wait_ge(s_sc, i + 1)
                act.activation(rr[:, :, :], sc2[:, :, :], ACT.Exp)
                act.activation(ww[:, :, :], sc[:, :, :], ACT.Exp).then_inc(s_ww, 1)

            for i in range(LAG):
                experts(i)
            with act.Fori(LAG, FT) as i:
                experts(i)
                exponentials(i - LAG)
            experts(FT, 1)
            outputs(FT, NE - 1, 1)
            for i in range(FT - LAG, TURNS):
                act.wait_ge(s_ww, i)
                exponentials(i)

            act.wait_ge(s_ce, 1)
            act.activation(crow[:, 4, 0:P], crow[:, 4, 0:P], ACT.Exp)
            act.activation(crow[:, 5, 0:P], crow[:, 5, 0:P], ACT.Exp).then_inc(s_cx, 1)
            act.wait_ge(s_fe, 1)
            act.activation(fx[:, 1:3, :], fx[:, 1:3, :], ACT.Exp).then_inc(s_fx, 1)
            def diagonals(n):
                j = n // 2
                if j >= 2:
                    act.wait_ge(s_sum, j - 1)
                for e in range(NE):
                    ins = act.activation(diag[:, j % 2, e, :], ident[:, :], ACT.Copy, scale=gate(n)[:, e:e + 1])
                ins.then_inc(s_diag, 1)

            def sum_copy(n):
                act.wait_ge(s_sum, n // 2 + 1)
                act.activation(ring(n % YR)[:, NE, :], bank[2 + n // 2 % 2][:, 0:D], ACT.Copy).then_inc(s_cmbp, 1)

            for q, (n0, n1) in enumerate(PARTS):
                hs = slice(n0 * H, n1 * H)
                act.wait_ge(s_ma, 2 * q + 1)
                act.activation(f4[2][:, hs], f4[2][:, hs], ACT.Exp)
                act.activation(f4[3][:, hs], f4[3][:, hs], ACT.Exp).then_inc(s_mx, 1)
                act.wait_ge(s_sqv, q + 1)
                act.activation(t49[:, 0, n0:n1], t49[:, 0, n0:n1], ACT.Sqrt, bias=eps[:, :], scale=1.0).then_inc(s_sqa, 1)
                act.wait_ge(s_ma, 2 * q + 2)
                act.activation(f4[2][:, hs], f4[2][:, hs], ACT.Exp).then_inc(s_mx, 1)
                act.wait_ge(s_gate, q + 1)
                odd = range(n0 + 1, n1, 2)
                for n in odd:
                    diagonals(n)
                    if n > odd[0]:
                        sum_copy(n - 2)
                sum_copy(odd[-1])

        @block.vector
        def _(dve):
            v = Chain(dve, s_v)
            fb = ROWB - 1
            dve.memset(xa[:, NT - 1, :], 0.0)
            dve.memset(eint[:, fb, 0, :], 0)
            dve.memset(eint[:, fb, 1, :], N - 1)
            dve.memset(eint[:, fb, 2, :], 2**30)
            dve.memset(erow[:, fb, 2, :], 0.0).then_inc(s_fill, 1)
            dve.memset(zero[:, :], 0.0).then_inc(s_zero, 1)
            dve.memset(eps[:, :], EPS)
            dve.memset(onesb[:, :], 1.0).then_inc(s_cstv, 1)
            dve.memset(lo[:, RUN:RUN + HT], 0.0)
            dve.memset(hi[:, RUN:RUN + HT], 0.0)
            dve.memset(keyp[0:1, :], -1.0)
            dve.memset(pay[:, RUN:RUN + CH, :], 0.0)
            dve.memset(sinkrow[:, H:W], 0.0)
            dve.memset(sinkrow[:, 0:H], -BIG).then_inc(s_zero, 1)
            dve.wait_ge(s_cst, 2)
            dve.tensor_copy(iof[:, :], iot[:, :])
            dve.tensor_copy(iob[:, :], iot[:, :])
            dve.tensor_copy(pidf[:, :], pidx[:, :])
            v(dve.tensor_copy(identb[:, :], ident[:, :]))
            dve.wait_ge(s_edge, 16 * 12)
            v.mark(dve.tensor_scalar(erow[:, :, 0, :], eint[:, :, 0, :], float(N - 1), 0.0, ALU.min, ALU.max))
            dve.tensor_copy(erow[:, :, 1, :], eint[:, :, 1, :]).then_inc(s_rows, 1)
            v(dve.tensor_single_scalar(lwin[:, :], eint[:, :, 1, P - 1], 7, ALU.arith_shift_right))
            v(dve.tensor_scalar(lv[:, :], lwin[:, :], 0.0, float(NT - 1), ALU.max, ALU.min))
            v(dve.scalar_tensor_tensor(lv[:, :], lv[:, :], 1.0, pidf[:, :], ALU.add, ALU.add))
            for c in range(ROWB):
                ins = dve.tensor_scalar(before[:, c, :], iokb[:, :], lv[:, c:c + 1], None, ALU.is_ge)
            ins.then_inc(s_bef, 1)
            v(dve.tensor_tensor(strow[:, :, 0, :], eint[:, :, 1, :], eint[:, :, 2, :], ALU.is_gt))
            dve.tensor_reduce(disorder[:, :], strow[:, :, 0, :], AX.XY, ALU.max).then_inc(s_dis, 1)
            def stats(c):
                dve.wait_ge(s_x[c], 16 if c < LOADS - 1 else 32)
                for n in range(c * LN, (c + 1) * LN):
                    ins = dve.bn_stats(st1[:, n, :], xa[:, n, :])
                v(ins)
                for n in range(c * LN, (c + 1) * LN):
                    ins = dve.bn_aggr(mv1[:, n, :], st1[:, n, :])
                ins.then_inc(s_mv1, 1)

            def norms(c):
                part = slice(c * LN, (c + 1) * LN)
                dve.wait_ge(s_sd1, c + 1)
                v(dve.reciprocal(rs1[:, part], sd1[:, part]))
                dve.scalar_tensor_tensor(nb1[:, part], mv1[:, part, 0], -1.0, rs1[:, part], ALU.mult, ALU.mult).then_inc(s_rs1, 1)

            WALK = 3
            for c in range(WALK):
                stats(c)
                if c:
                    norms(c - 1)
            dve.wait_ge(s_ik, 1)
            v(dve.tensor_scalar(disorder[:, :], bank[0][:, ROWB:ROWB + 1], 1.0, None, ALU.min))
            dve.tensor_copy(unsorted[:, :], disorder[:, :]).then_inc(s_uns, 1)
            v(dve.tensor_tensor(ikf[:, :], pidf[:, :], bank[0][:, 0:ROWB], ALU.subtract))
            v(dve.scalar_tensor_tensor(ikf[:, :], ikf[:, :], disorder[:, :], bank[0][:, 0:ROWB], ALU.mult, ALU.add))
            dve.tensor_copy(iku[:, :], ikf[:, :]).then_inc(s_iku, 1)
            v(dve.tensor_tensor(jkf[:, :], pidf[:, :], ikf[:, :], ALU.subtract))
            v(dve.tensor_scalar(jkf[:, :], jkf[:, :], float(NT - 1), float(P), ALU.min, ALU.mult))
            dve.tensor_copy(jki[:, :], jkf[:, :]).then_inc(s_win, 1)
            for c in range(WALK, LOADS):
                stats(c)
                norms(c - 1)
            norms(LOADS - 1)
            dve.wait_ge(s_rowsd, 16)
            v.mark(dve.memset(regB[:, 0:2 * RD], 0.0))
            v.mark(dve.memset(regB[:, 3 * RD:], 0.0))
            v.mark(dve.memset(grow[:, :, :, :].rearrange("p a b c -> p (a b c)")[:, KD * D:], 0.0))
            dve.wait_ge(s_strow, 16 * ROWB)
            for c in range(ROWB):
                ins = dve.tensor_scalar(strow[:, c, 1, :], strow[:, c, 1, :], jkf[:, c:c + 1], None, ALU.subtract)
            ins.then_inc(s_dl, 1)
            for q in range(3):
                dve.wait_ge(s_tr, q + 1)
                v.mark(dve.tensor_copy(stcol[:, q, 0:4 * P], bank[1 + 2 * q][:, :]))
                v.mark(dve.tensor_copy(stcol[:, q, 4 * P:ROWB * P], bank[2 + 2 * q][:, 0:(ROWB - 4) * P]))
            v.wait()
            v(dve.tensor_copy(step_src, stcol[:, 0, :]))
            def weighted(k, hf, s):
                return dve.tensor_scalar(onehot[:, hf, s, :], iof[:, :], stcol[:, 1, bass.ds(k, 1)],
                                         stcol[:, 2, bass.ds(k, 1)], ALU.is_equal, ALU.mult)

            for hf in range(2):
                dve.tensor_copy(idxr[:, hf, 0:HS], step_src[:, hf * HS:(hf + 1) * HS]).then_inc(s_idx, 1)
            v.mark(dve.memset(regB[:, 2 * RD:3 * RD], 0.0))
            for hf in range(2):
                for s in range(HS):
                    ins = weighted(hf * HS + s, hf, s)
                ins.then_inc(s_sel, 1)
            dve.wait_ge(s_gat, 32)
            v.mark(dve.tensor_scalar(pay[:, 0:RUN, 1], sint[:, :], float(N - 1), 0.0, ALU.min, ALU.max))
            v(dve.tensor_scalar(pay[:, 0:RUN, 0], kint[:, :], 0.0, 2.0**33, ALU.is_lt, ALU.mult))
            v(dve.tensor_tensor(pay[:, 0:RUN, 0], pay[:, 0:RUN, 0], kint[:, :], ALU.add))
            v(dve.tensor_scalar(pay[:, 0:RUN, 0], pay[:, 0:RUN, 0], float(N), None, ALU.min))
            v(dve.tensor_copy(kint[:, :], pay[:, 0:RUN, 0]))
            v(dve.tensor_single_scalar(sint[:, :], kint[:, :], P - 1, ALU.bitwise_and))
            v(dve.tensor_copy(lo[:, 0:RUN], sint[:, :]))
            v(dve.tensor_single_scalar(sint[:, :], kint[:, :], 7, ALU.arith_shift_right))
            v(dve.tensor_copy(hi[:, 0:RUN], sint[:, :]))
            dve.wait_ge(s_par, 16 * 16)
            for k in range(KD):
                for q in range(2):
                    v(dve.tensor_tensor(wt[:, :], wg[:, k, 0:HE], attb[:, q, :], ALU.mult))
                    v(dve.tensor_reduce(wg[:, k, HE + q * H:HE + (q + 1) * H], wt[:, :].rearrange("p (h e) -> p h e", h=H),
                                        AX.X, ALU.add))
            regs = [dve.alloc_register(f"win{s}") for s in range(HS)]
            dve.wait_ge(s_wind, 32)
            with dve.Fori(0, TURNS) as i:
                for hf in range(2):
                    dve.load(regs, wins[0:1, bass.ds(i * 2 + hf, 1), 0:HS])
                    for s in range(HS):
                        k = i * (2 * HS) + (hf * HS + s)
                        w = dve.snap(regs[s], min_val=0, max_val=(NT - 1) * P)
                        dve.wait_ge(s_step, k + 1)
                        dve.wait_ge(s_acc, k + SB)
                        dve.tensor_tensor(acc[:, :, bass.ds(w, P)], acc[:, :, bass.ds(w, P)],
                                          slot(s).rearrange("p (k n) -> p k n", k=KD), ALU.add).then_inc(s_acc, 1)
                        ins = weighted(k + 2 * HS, hf, s)
                    ins.then_inc(s_sel, 1)
                    dve.tensor_copy(idxr[:, hf, 0:HS], step_src[:, bass.ds((i + 1) * (2 * HS) + hf * HS, HS)]).then_inc(s_idx, 1)
                    dve.wait_ge(s_hist, i * 2 + (hf + 1))
                    at = i * CH + hf * HT
                    dve.tensor_tensor(ol[:, hf, :, :], every(iob[:, :], HT), each(lo[:, bass.ds(at, HT)], P), ALU.is_equal)
                    dve.tensor_tensor(oh[:, hf, :, :], every(iob[:, 0:NT], HT), each(hi[:, bass.ds(at, HT)], NT),
                                      ALU.is_equal).then_inc(s_oh, 1)
            dve.wait_ge(s_sel, 2 * TURNS + 2)
            dve.wait_ge(s_acc, 2 * HS * TURNS + SB)
            uns = dve.value_load(unsorted[0:1, 0:1], min_val=0, max_val=1)
            with dve.If(uns > 0):
                u = Chain(dve, s_uv)
                wide = onehot[:, 0, 0:WW, :]
                dve.wait_ge(s_idx, 2 * TURNS + 2)
                u(dve.tensor_scalar(dcol[:, 0, :], iof[:, 0:WW], float(-P), float(-P), ALU.mult, ALU.add))
                with u.loop(0, FULL + 1, 1 + (NT - 1) // WW * 5) as k:
                    dve.tensor_copy(idxr[:, 0, 0:1], step_src[:, bass.ds(k, 1)]).then_inc(s_uidx, 1)
                    u(dve.tensor_scalar(dcol[:, 1, :], dcol[:, 0, :], stcol[:, 1, bass.ds(k, 1)], None, ALU.add))
                    for g in range((NT - 1) // WW):
                        u(dve.tensor_tensor(wide, every(iof[:, :], WW), each(dcol[:, 1, :], P), ALU.is_equal))
                        u.mark(dve.tensor_scalar(dcol[:, 1, :], dcol[:, 1, :], float(-WW * P), None, ALU.add))
                        u(dve.tensor_scalar(wide, wide, stcol[:, 2, bass.ds(k, 1)], None, ALU.mult))
                        dve.sem_inc(s_usel, 1)
                        dve.wait_ge(s_uprod, k * ((NT - 1) // WW) + (g + 1))
                        for m in range(KD):
                            c0 = (1 + g * WW) * P
                            u.mark(dve.tensor_tensor(acc[:, m, c0:c0 + WW * P], acc[:, m, c0:c0 + WW * P], bank[m][:, :], ALU.add))
                        u.wait()
                    dve.sem_inc(s_begun_v, 1)
            dve.sem_inc(s_gnn, 1)
            dve.wait_ge(s_hist, 2 * TURNS + 2)
            v(dve.tensor_copy(cnt[:, :], bank[7][:, 0:NT]))
            dve.tensor_tensor(vcol[:, :], cnt[:, NT - 1:NT], above[:, LAST:LAST + 1], ALU.mult).then_inc(s_cnt, 1)
            dve.memset(totx[:, 0:1], 0.0)
            dve.wait_ge(s_pre, 1)
            v.mark(dve.tensor_copy(cnt[:, NT - 1:NT], vcol[:, :]))
            v.mark(dve.tensor_copy(runp[:, 1:2], bank[6][:, 128:129]))
            v(dve.tensor_copy(tots[:, :], bank[6][:, 64:64 + NT]))
            v(dve.tensor_tensor_scan(totx[:, 1:NT + 1], ones[:, 0:NT], tots[:, :], 0.0, ALU.mult, ALU.add))
            v(dve.tensor_tensor(basef[:, :], bank[6][:, 0:NT], totx[:, 0:NT], ALU.add))
            dve.tensor_copy(run4[:, GT - 1, GT - 1, :], basef[:, :]).then_inc(s_t0, 1)
            v(dve.tensor_tensor(runp[:, 1:2], runp[:, 1:2], totx[:, NT - 1:NT], ALU.add))
            v(dve.tensor_scalar(runp[:, 1:2], runp[:, 1:2], float(P - 1), 1.0 / P, ALU.add, ALU.mult))
            v(dve.tensor_scalar(runi[:, :], runp[:, 1:2], 0.5 / P - 0.5, 1.0, ALU.add, ALU.max))
            v(dve.tensor_copy(runp[:, 0:1], runi[:, :]))
            v.mark(dve.tensor_scalar(runp[:, 3:4], runp[:, 0:1], -1.0, float(RUN), ALU.mult, ALU.add))
            v(dve.reciprocal(runp[:, 1:2], runp[:, 0:1]))
            v(dve.tensor_scalar(runp[:, 2:3], runp[:, 1:2], 0.5, -0.5, ALU.mult, ALU.add))

            def partition_of(out, pos):
                return dve.tensor_scalar(out, pos, runp[:, 1:2], runp[:, 2:3], ALU.mult, ALU.add)

            def place(out, pos, part):
                return dve.scalar_tensor_tensor(out, part, runp[:, 3:4], pos, ALU.mult, ALU.add)

            def onehots(G, hf, gi):
                g0 = gi * GT
                dve.tensor_tensor(ol[:, hf, g0:g0 + GT, :], every(iob[:, :], GT), each(lo[:, bass.ds(G * GT, GT)], P), ALU.is_equal)
                dve.tensor_tensor(oh[:, hf, g0:g0 + GT, :], every(iob[:, 0:NT], GT), each(hi[:, bass.ds(G * GT, GT)], NT),
                                  ALU.is_equal).then_inc(s_ol, 1)

            for g in range(HT // GT - 1):
                onehots(g, 0, g)
            def gnn_stats(b, w=512):
                dve.wait_ge(s_bc, b + 2)
                for m in range(KD):
                    ins = dve.bn_stats(stb[:, m, bass.ds(b, 1), :].rearrange("p a s -> p (a s)"), gnn[:, m, bass.ds(b * 512, w)])
                ins.then_inc(s_bn, 1)

            NG = HT // GT

            def products(G, hf, gi):
                g0 = gi * GT
                dve.wait_ge(s_g, G + 3)
                dve.tensor_tensor(gm[:, :, :], bank[4][:, 0:GT * NT].rearrange("p (a b) -> p a b", a=GT),
                                  oh[:, hf, g0:g0 + GT, :], ALU.mult).then_inc(s_gm, 1)

            def sums(G, i, hf, gi, meanwhile=None):
                g0 = gi * GT
                dve.wait_ge(s_gm, G + 1)
                v.mark(dve.tensor_reduce(posf[:, :], gm[:, :, :], AX.X, ALU.add))
                if gi == 0 and not (isinstance(i, int) and i == 0):
                    dve.wait_ge(s_scat[hf], i * (16 * HT))
                dve.tensor_copy(payr[:, hf, g0:g0 + GT, :], pay[:, bass.ds(i * CH + (hf * HT + g0), GT), :])
                if meanwhile:
                    meanwhile()
                v.wait()
                v(partition_of(posq[:, :], posf[:, :]))
                place(posr[:, hf, g0:g0 + GT], posf[:, :], posq[:, :]).then_inc(s_pos, 1)

            def rank(i, hf, gi):
                G = i * (2 * NG) + (hf * NG + gi)
                ph, pg = hf if gi else 1 - hf, (gi - 1) % NG
                first = isinstance(i, int) and G == 0
                if not first:
                    products(G, ph, pg)
                dve.wait_ge(s_eq, G + 1)
                dve.tensor_tensor(ub[:, :, :], bank[2][:, :].rearrange("p (a b) -> p a b", a=GT), every(above[:, :], GT),
                                  ALU.mult).then_inc(s_u, 1)

                def ahead():
                    onehots(G + (NG - 1), hf if gi == 0 else 1 - hf, (gi - 1) % NG)

                if first:
                    ahead()
                else:
                    sums(G, i - 1 if hf == gi == 0 else i, ph, pg, ahead)

            def node(n, hf, gi):
                if gi == 0:
                    dve.wait_ge(s_px, n + 3)
                    v(dve.bn_stats(stn[:, :], bank[5][:, 0:D]))
                    dve.sem_inc(s_begun_v, 1)
                    dve.bn_aggr(mvn[:, :], stn[:, :]).then_inc(s_mvn, 1)
                if gi == 1:
                    dve.wait_ge(s_sdn, n + 1)
                    v(dve.reciprocal(rsn[:, :], sdn[:, :]))
                    dve.wait_ge(s_x2, n + 1)
                    dve.tensor_scalar(x3[:, hf, :], bank[5][:, 0:D], mvn[:, 0:1], rsn[:, :], ALU.subtract, ALU.mult).then_inc(s_x3, 1)

            def turn(i, extra):
                for hf in range(2):
                    for gi in range(NG):
                        n = i * 2 + (hf - 2 * N0)
                        rank(i, hf, gi)
                        if extra == "nodes" or (extra == "last" and hf == 0):
                            node(n, hf, gi)
                        if extra == "gnn" and gi % 2:
                            gnn_stats(i * 4 + (2 * hf + gi // 2))
                        if extra == "bn" and hf == 0 and gi == 1:
                            gnn_stats(CB - 1, N - (CB - 1) * 512)
                            dve.wait_ge(s_bn, CB)
                            for m in range(KD):
                                ins = dve.bn_aggr(mvb[:, m, :], stb[:, m, :, :])
                            ins.then_inc(s_sdb, 1)
                        if extra == "bn" and hf == 1 and gi == 1:
                            dve.wait_ge(s_sdb, 2)
                            v(dve.reciprocal(sdb[:, :], sdb[:, :]))
                            v(dve.tensor_tensor(scb[:, :], sdb[:, :], gam[:, :], ALU.mult))
                            v(dve.tensor_tensor(bib[:, :], mvb[:, :, 0], scb[:, :], ALU.mult))
                            dve.tensor_tensor(bib[:, :], bet[:, :], bib[:, :], ALU.subtract).then_inc(s_bnr, 1)

            RG = 2 * 2 * NG
            turn(0, "gnn")
            with v.loop(1, CT, RG) as i:
                turn(i, "gnn")
            turn(CT, "bn")
            turn(CT + 1, "tanh")
            turn(N0, "nodes")
            with v.loop(N0 + 1, N1, RG + 4) as i:
                turn(i, "nodes")
            turn(N1, "last")
            v(dve.tensor_scalar(t49[:, 0, :], cnt[:, :], 0.0, None, ALU.is_equal))
            v(partition_of(q49[:, :], basef[:, :]))
            v(place(t49[:, 1, :], basef[:, :], q49[:, :]))
            v(dve.tensor_scalar(t49[:, 1, :], t49[:, 1, :], float(E2), None, ALU.min))
            v(dve.tensor_scalar(t49[:, 2, :], iof[:, 0:NT], float(P), pidf[:, 0:1], ALU.mult, ALU.add))
            v(dve.scalar_tensor_tensor(t49[:, 2, :], t49[:, 2, :], float(E2), t49[:, 1, :], ALU.add, ALU.subtract))
            v(dve.tensor_tensor(t49[:, 2, :], t49[:, 2, :], t49[:, 0, :], ALU.mult))
            v(dve.tensor_tensor(sidx[:, :], t49[:, 1, :], t49[:, 2, :], ALU.add))
            v(dve.scalar_tensor_tensor(t49[:, 3, :], basef[:, :], -1.0, cnt[:, :], ALU.add, ALU.add))
            v(partition_of(q49[:, :], t49[:, 3, :]))
            v(place(t49[:, 1, :], t49[:, 3, :], q49[:, :]))
            v(dve.tensor_scalar(t49[:, 1, :], t49[:, 1, :], float(E2), None, ALU.min))
            v(dve.tensor_scalar(t49[:, 2, :], t49[:, 1, :], -1.0, float(SINK), ALU.mult, ALU.add))
            v(dve.tensor_tensor(t49[:, 2, :], t49[:, 2, :], t49[:, 0, :], ALU.mult))
            dve.tensor_tensor(eidx[:, :], t49[:, 1, :], t49[:, 2, :], ALU.add).then_inc(s_seidx, 1)
            with v.loop(N1 + 1, RT, RG) as i:
                turn(i, "")
            products(RT * 2 * NG, 1, NG - 1)
            sums(RT * 2 * NG, RT - 1, 1, NG - 1)

            dve.wait_ge(s_icol, 1)
            dve.wait_ge(s_olt, RT * 2 * NG + 1)
            v(dve.tensor_scalar(hold, icol, runp[:, 0:1], None, ALU.is_ge))
            dve.wait_ge(s_srt, 16)
            v(dve.tensor_copy(key0[:, :], pay[:, 0, 0:1]))
            v(dve.tensor_tensor_scan(pay[:, 0:RUN, 0], hold, pay[:, 0:RUN, 0], 0.0, ALU.mult, ALU.add))
            dve.tensor_copy(lastk[:, :], pay[:, RUN - 1, 0:1]).then_inc(s_lastk, 1)
            dve.tensor_copy(key0u[:, :], key0[:, :]).then_inc(s_k0, 1)
            v(dve.tensor_scalar(hold, hold, -BIG, None, ALU.mult))
            for hf in range(2):
                dve.tensor_copy(gidx[:, hf, :], pay[:, hf * HT:(hf + 1) * HT, 1]).then_inc(s_gidx, 1)
            dve.wait_ge(s_lastd, 32)
            v.mark(dve.tensor_tensor(keep[:, 1:RUN], pay[:, 1:RUN, 0], pay[:, 0:RUN - 1, 0], ALU.is_equal))
            v(dve.tensor_tensor(keep[:, 0:1], key0[:, :], keyp[:, :], ALU.is_equal))
            v.mark(dve.tensor_scalar(neg[:, :], keep[:, :], -1.0, BIG, ALU.add, ALU.mult))
            v(dve.tensor_scalar(same[:, :], pay[:, 0:RUN, 0], key0[:, :], None, ALU.is_equal))
            v(dve.tensor_reduce(nfirst[:, :], same[:, :], AX.X, ALU.add))
            v(dve.tensor_tensor(nfirst[:, :], nfirst[:, :], runp[:, 0:1], ALU.min))
            v(dve.tensor_scalar(cf[:, 0:1], pidf[:, 0:1], float(RUN), -1.0, ALU.mult, ALU.add))
            dve.tensor_tensor(fidx[:, :], cf[:, 0:1], nfirst[:, :], ALU.add).then_inc(s_fidx, 1)
            dve.wait_ge(s_arow, 16)
            dve.wait_ge(s_adr, 16)
            for h in range(H):
                v.mark(dve.tensor_tensor_scan(adst[:, h, :], keep[:, :], adraw[:, :, h], arow[:, HE + H + h:HE + H + h + 1],
                                              ALU.mult, ALU.add))
            v.wait()
            v.mark(dve.tensor_tensor(adst, adst, every(hold, H), ALU.add))
            v.mark(dve.memset(last[:, 0:H], -BIG))
            v(dve.memset(last[:, H:W], 0.0))

            gathered = dve.value_load(runi[0:1, 0:1], min_val=1, max_val=RUN)

            def chunk(i, j):
                t = i * 2 + j
                for hf in range(2):
                    if hf:
                        with dve.If(gathered > t * CH + hf * HT):
                            dve.wait_ge(s_grow[hf], (t + 1) * (16 * HT))
                            dve.sem_inc(s_begun_v, 1)
                    else:
                        dve.wait_ge(s_grow[hf], (t + 1) * (16 * HT))
                    v(dve.tensor_copy(hc[:, :, hf * HT:(hf + 1) * HT], grow[:, hf, :, :].rearrange("p t w -> p w t")))
                    dve.tensor_copy(gidx[:, hf, :], pay[:, bass.ds((t + 1) * CH + hf * HT, HT), 1]).then_inc(s_gidx, 1)
                tc = bass.ds(t * CH, CH)
                v(dve.tensor_tensor(sc[:, :, :], hc[:, HE:HE + H, :], adst[:, :, tc], ALU.add))
                v(dve.scalar_tensor_tensor(sc[:, :, :], sc[:, :, :], 0.2, sc[:, :, :], ALU.mult, ALU.max))
                v(dve.tensor_copy(mb[:, :, 0], last[:, 0:H]))
                for h in range(H):
                    v.mark(dve.tensor_tensor_scan(mb[:, h, 1:CH + 1], neg[:, tc], sc[:, h, :], last[:, h:h + 1], ALU.add, ALU.max))
                v.wait()
                v(dve.tensor_tensor(sc2[:, :, :], mb[:, :, 0:CH], every(neg[:, tc], H), ALU.add))
                v.mark(dve.tensor_tensor(sc2[:, :, :], sc2[:, :, :], mb[:, :, 1:CH + 1], ALU.subtract))
                v(dve.tensor_tensor(sc[:, :, :], sc[:, :, :], mb[:, :, 1:CH + 1], ALU.subtract))
                dve.sem_inc(s_sc, 1)
                dve.wait_ge(s_ww, t + 1)
                dve.wait_ge(s_lcd[j], (i + 1) * 16)
                v(dve.tensor_tensor(nm[:, :, :].rearrange("p (h e) t -> p h e t", h=H),
                                    hc[:, 0:HE, :].rearrange("p (h e) t -> p h e t", h=H),
                                    ww[:, :, :].unsqueeze(2).to_broadcast([P, H, NE, CH]), ALU.mult))
                for h in range(H):
                    v.mark(dve.tensor_tensor_scan(lc[:, j, :, H + h], rr[:, h, :], ww[:, h, :], last[:, H + h:H + h + 1],
                                                  ALU.mult, ALU.add))
                for f in range(HE):
                    v.mark(dve.tensor_tensor_scan(lc[:, j, :, 2 * H + f], rr[:, f // NE, :], nm[:, f, :],
                                                  last[:, 2 * H + f:2 * H + f + 1], ALU.mult, ALU.add))
                v(dve.tensor_copy(lc[:, j, :, 0:H], mb[:, :, 1:CH + 1].rearrange("p h t -> p t h")))
                v.mark(dve.tensor_copy(last[:, :], lc[:, j, CH - 1, :]))
                dve.wait_ge(s_v, v.value())
                dve.sem_inc(s_lc, 1)

            def chunk_or_none(i, j):
                t, before_n = i * 2 + j, v.n
                with dve.If(gathered > t * CH):
                    chunk(i, j)
                with dve.Else():
                    dve.sem_inc(s_v, v.n - before_n)
                    dve.sem_inc(s_gidx, 2)
                    dve.sem_inc(s_sc, 1)
                    dve.sem_inc(s_lc, 1)

            per = 2 * (2 + 1 + 1 + 1 + H + 1 + 1 + 1 + 1 + H + HE + 1 + 1)
            with v.loop(0, TURNS // 2, per) as i:
                chunk_or_none(i, 0)
                chunk_or_none(i, 1)

            v.mark(dve.tensor_copy(cin[:, 0, 0:H], last[:, 0:H]))
            v.mark(dve.tensor_copy(cin[:, 0, H:LF].rearrange("p (h e) -> p h e", h=H), each(last[:, 0:H], NE)))
            v.mark(dve.tensor_copy(cin[:, 1, :], last[:, H:W]))
            v(dve.tensor_scalar(cf[:, 2:3], nfirst[:, :], runp[:, 0:1], None, ALU.is_equal))
            v(dve.tensor_tensor(cf[:, 2:3], cf[:, 2:3], keep[:, 0:1], ALU.mult))
            v(dve.tensor_scalar(cf[:, 2:3], cf[:, 2:3], -1.0, BIG, ALU.add, ALU.mult))
            v.mark(dve.tensor_copy(cin[:, 2, :], cf[:, 2:3].to_broadcast([P, LF])))
            dve.tensor_copy(cin[:, 3, :], neg[:, 0:1].to_broadcast([P, LF])).then_inc(s_cin, 1)
            dve.wait_ge(s_ctr, 1)
            v.mark(dve.tensor_copy(crow[:, 0:4, 0:P], bank[0][0:LF, :].rearrange("p (a b) -> p a b", a=4)))
            v.mark(dve.memset(crow[:, 6, 0:1], -BIG))
            v(dve.memset(crow[:, 7, 0:1], 0.0))
            v(dve.tensor_tensor_scan(crow[:, 6, 1:P + 1], crow[:, 2, 0:P], crow[:, 0, 0:P], -BIG, ALU.add, ALU.max))
            v(dve.tensor_tensor(crow[:, 4, 0:P], crow[:, 6, 0:P], crow[:, 2, 0:P], ALU.add))
            v.mark(dve.tensor_tensor(crow[:, 4, 0:P], crow[:, 4, 0:P], crow[:, 6, 1:P + 1], ALU.subtract))
            v(dve.tensor_tensor(crow[:, 5, 0:P], crow[:, 0, 0:P], crow[:, 6, 1:P + 1], ALU.subtract))
            dve.sem_inc(s_ce, 1)
            dve.wait_ge(s_cx, 1)
            v(dve.tensor_tensor(crow[:, 1, 0:P], crow[:, 1, 0:P], crow[:, 5, 0:P], ALU.mult))
            v(dve.tensor_tensor_scan(crow[:, 7, 1:P + 1], crow[:, 4, 0:P], crow[:, 1, 0:P], 0.0, ALU.mult, ALU.add))
            dve.tensor_tensor(crow[:, 0, 0:P], crow[:, 6, 0:P], crow[:, 3, 0:P], ALU.add).then_inc(s_cb, 1)
            dve.wait_ge(s_cbt, 1)
            v(dve.tensor_copy(cout[:, :, :], bank[1][:, 0:2 * LF].rearrange("p (a b) -> p a b", a=2)))
            dve.wait_ge(s_frow, 16)
            v.mark(dve.tensor_copy(fx[:, 1, 0:H], frow[:, 0:H]))
            v(dve.tensor_copy(fx[:, 1, H:LF].rearrange("p (h e) -> p h e", h=H), each(frow[:, 0:H], NE)))
            v(dve.tensor_tensor(fx[:, 0, :], fx[:, 1, :], cout[:, 0, :], ALU.max))
            v.mark(dve.tensor_tensor(fx[:, 1, :], fx[:, 1, :], fx[:, 0, :], ALU.subtract))
            v(dve.tensor_tensor(fx[:, 2, :], cout[:, 0, :], fx[:, 0, :], ALU.subtract))
            dve.sem_inc(s_fe, 1)
            dve.wait_ge(s_fx, 1)
            v.mark(dve.tensor_tensor(fx[:, 1, :], fx[:, 1, :], frow[:, H:W], ALU.mult))
            v(dve.tensor_tensor(fx[:, 2, :], fx[:, 2, :], cout[:, 1, :], ALU.mult))
            v.mark(dve.tensor_tensor(arow[:, H:W], fx[:, 1, :], fx[:, 2, :], ALU.add))
            dve.tensor_copy(arow[:, 0:H], fx[:, 0, 0:H]).then_inc(s_fst, 1)

            def h3(ap):
                return ap.rearrange("p (n h) -> p n h", h=H)

            def he(ap):
                return ap.rearrange("p (n f) -> p n f", f=HE)

            def bc(ap):
                return each(ap, NE)

            def g3(ap):
                return ap.rearrange("p (g e) -> p g e", e=NE)

            def score(q, n0, n1):
                C = n1 - n0
                f = [ap[:, n0 * H:n1 * H] for ap in f4[0:5]]
                fa, fb = [ap[:, n0 * HE:n1 * HE] for ap in fin[0:2]]
                tb, es = tab[:, n0:n1, :], esum[:, n0:n1, :]
                t = [t49[:, i, n0:n1] for i in range(4)]
                v(dve.tensor_tensor(h3(f[0]), tb[:, :, HE:HE + H], tb[:, :, HE + H:W], ALU.add))
                v(dve.scalar_tensor_tensor(f[0], f[0], 0.2, f[0], ALU.mult, ALU.max))
                dve.wait_ge(s_esum[q], 16 * C)
                v(dve.tensor_tensor(h3(f[1]), es[:, :, 0:H], h3(f[0]), ALU.max))
                v.mark(dve.tensor_tensor(h3(f[2]), es[:, :, 0:H], h3(f[1]), ALU.subtract))
                v(dve.tensor_tensor(f[3], f[0], f[1], ALU.subtract))
                dve.sem_inc(s_ma, 1)
                dve.wait_ge(s_mx, 2 * q + 1)
                v(dve.tensor_tensor(h3(f[4]), es[:, :, H:2 * H], h3(f[2]), ALU.mult))
                v(dve.tensor_tensor(f[4], f[4], f[3], ALU.add))
                v(dve.tensor_scalar(f[4], f[4], 1e-16, None, ALU.add))
                v.mark(dve.reciprocal(f[4], f[4]))
                v.mark(dve.tensor_copy(he(fa), es[:, :, 2 * H:W]))
                v(dve.tensor_copy(he(fb), tb[:, :, 0:HE]))
                v.mark(dve.tensor_tensor(g3(fa), g3(fa), bc(f[2]), ALU.mult))
                v(dve.tensor_tensor(g3(fb), g3(fb), bc(f[3]), ALU.mult))
                v(dve.tensor_tensor(fa, fa, fb, ALU.add))
                v(dve.tensor_tensor(g3(fa), g3(fa), bc(f[4]), ALU.mult))
                v(dve.tensor_tensor(he(fa), he(fa), every(gatp[:, 0, :], C), ALU.add))
                v(dve.tensor_reduce(t[1], he(fa), AX.X, ALU.add))
                v(dve.tensor_scalar(t[1], t[1], 1.0 / HE, None, ALU.mult))
                v(dve.tensor_tensor(he(fa), he(fa), each(t[1], HE), ALU.subtract))
                v(dve.tensor_tensor(fb, fa, fa, ALU.mult))
                v(dve.tensor_reduce(t[0], he(fb), AX.X, ALU.add))
                v(dve.tensor_scalar(t[0], t[0], 1.0 / HE, None, ALU.mult))
                dve.sem_inc(s_sqv, 1)
                dve.wait_ge(s_sqa, q + 1)
                v(dve.reciprocal(t[0], t[0]))
                v(dve.tensor_tensor(he(fa), he(fa), each(t[0], HE), ALU.mult))
                v(dve.tensor_tensor(he(fa), he(fa), every(gatp[:, 1, :], C), ALU.mult))
                v(dve.tensor_tensor(he(fa), he(fa), every(gatp[:, 2, :], C), ALU.add))
                v(dve.tensor_reduce(f[0], fa.rearrange("p (n h e) -> p n e h", h=H, e=NE), AX.X, ALU.add))
                v(dve.tensor_scalar(f[0], f[0], 1.0 / H, None, ALU.mult))
                sco = f[0].rearrange("p (n e) -> p n e", e=NE)
                rk = f[1].rearrange("p (n e) -> p n e", e=NE)
                v(dve.memset(f[1], 0.0))
                for a in range(NE):
                    for b in range(a + 1, NE):
                        v(dve.tensor_tensor(t[2], sco[:, :, b], sco[:, :, a], ALU.is_gt))
                        v.mark(dve.tensor_tensor(rk[:, :, a], rk[:, :, a], t[2], ALU.add))
                        v(dve.tensor_scalar(t[3], t[2], -1.0, 1.0, ALU.mult, ALU.add))
                        v(dve.tensor_tensor(rk[:, :, b], rk[:, :, b], t[3], ALU.add))
                v(dve.tensor_reduce(t[2], sco, AX.X, ALU.max))
                v(dve.tensor_tensor(f[2].rearrange("p (n e) -> p n e", e=NE), sco, each(t[2], NE), ALU.subtract))
                dve.sem_inc(s_ma, 1)
                dve.wait_ge(s_mx, 2 * q + 2)
                v(dve.tensor_scalar(f[1], f[1], 1.5, None, ALU.is_lt))
                v(dve.tensor_tensor(f[1], f[1], f[2], ALU.mult))
                v(dve.tensor_reduce(t[2], rk, AX.X, ALU.add))
                v(dve.reciprocal(t[2], t[2]))
                v(dve.tensor_tensor(rk, rk, each(t[2], NE), ALU.mult))
                dve.sem_inc(s_gate, 1)

            def combine(n0, n1):
                for a in range(n0, n1, 4):
                    pair = range(a, min(a + 4, n1), 2)
                    for e in range(NE):
                        for n in pair:
                            b, m = n % YR, (P if n < NT - 1 else LAST)
                            if e == 0:
                                dve.wait_ge(s_yl[b], 32 * (n // YR + 1))
                            ins = dve.scalar_tensor_tensor(ring(b)[0:m, NE, :], ring(b)[0:m, e, :], gate(n)[0:m, e:e + 1],
                                                           ring(b)[0:m, NE, :], ALU.mult, ALU.add)
                            if e == NE - 1:
                                ins.then_inc(s_cmb, 1)
                            else:
                                v.mark(ins)
                        if e < NE - 1:
                            v.wait()

            for q, (n0, n1) in enumerate(PARTS):
                score(q, n0, n1)
                combine(n0, n1)

        @block.tensor
        def _(pe):
            pe.wait_ge(s_bef, 1)
            pe.wait_ge(s_cstv, 1)
            for k in range(ROWB):
                for c in range(ROWB):
                    pe.matmul(bank[0][:, k:k + 1], before[:, c, k * P:(k + 1) * P], onesb[:, :], start=c == 0, stop=c == ROWB - 1)
            pe.wait_ge(s_dis, 1)
            pe.wait_ge(s_cst, 1)
            pe.matmul(bank[0][:, ROWB:ROWB + 1], ones[:, :], disorder[:, :], start=True, stop=True).then_inc(s_ik, 1)
            pe.wait_ge(s_dl, 1)
            pe.wait_ge(s_cst, 2)
            for q in range(3):
                for c in range(ROWB):
                    ins = pe.transpose(bank[1 + 2 * q + c // 4][:, (c % 4) * P:(c % 4 + 1) * P], strow[:, c, q, :], ident[:, :])
                ins.then_inc(s_tr, 1)
            pe.wait_ge(s_zero, 1)
            pe.matmul(bank[7][:, 0:NT], zero[:, 0:P], zero[:, 0:NT], start=True, stop=False, skip_group_check=True)
            with pe.Fori(0, TURNS) as i:
                for hf in range(2):
                    pe.wait_ge(s_row[hf], (i + 1) * (16 * HS))
                    pe.wait_ge(s_sel, i * 2 + (hf + 1))
                    for s in range(HS):
                        pe.wait_ge(s_acc, i * (2 * HS) + (hf * HS + s + 1))
                        for m in range(KD):
                            ins = pe.matmul(slot(s)[:, m * P:(m + 1) * P], rows[:, hf, s, m * P:(m + 1) * P],
                                            onehot[:, hf, s, :], start=True, stop=True)
                        ins.then_inc(s_step, 1)
                    pe.wait_ge(s_oh, i * 2 + (hf + 1))
                    for t in range(HT):
                        ins = pe.matmul(bank[7][:, 0:NT], ol[:, hf, t, :], oh[:, hf, t, :], start=False, stop=False, skip_group_check=True)
                    ins.then_inc(s_hist, 1)
            uns = pe.value_load(unsorted[0:1, 0:1], min_val=0, max_val=1)
            with pe.If(uns > 0):
                with pe.Fori(0, FULL + 1) as k:
                    pe.wait_ge(s_urow, (k + 1) * 16)
                    for g in range((NT - 1) // WW):
                        pe.wait_ge(s_usel, k * ((NT - 1) // WW) + (g + 1))
                        for m in range(KD):
                            ins = pe.matmul(bank[m][:, :], rows[:, 0, 0, m * P:(m + 1) * P],
                                            onehot[:, 0, 0:WW, :].rearrange("p a b -> p (a b)"), start=True, stop=True)
                        ins.then_inc(s_uprod, 1)
            pe.wait_ge(s_cnt, 1)
            pe.wait_ge(s_acc, 2 * HS * TURNS + SB)
            pe.matmul(bank[6][:, 0:NT], above[:, :], cnt[:, :], start=True, stop=True)
            pe.matmul(bank[6][:, 64:64 + NT], ones[:, :], cnt[:, :], start=True, stop=True)
            pe.matmul(bank[6][:, 128:129], ones[:, :], vcol[:, :], start=True, stop=True).then_inc(s_pre, 1)
            def gnn_block(b, w=512):
                pe.wait_ge(s_bc, b + 1)
                for m in range(KD):
                    for k in range(KD):
                        ins = pe.matmul(bank[5 + m][:, 0:w], ham[:, k, m * P:(m + 1) * P], acc[:, k, bass.ds(b * 512, w)],
                                        start=k == 0, stop=k == KD - 1)
                ins.then_inc(s_bo, 1)

            NG = HT // GT

            def transposes(hf, gi, par):
                for t in range(GT):
                    ins = pe.transpose(bank[par][:, :].bitcast(bf16)[:, t * P:(t + 1) * P], ol[:, hf, gi * GT + t, :], identb[:, :])
                ins.then_inc(s_trp, 1)

            def rank(i, hf, gi):
                G = i * (2 * NG) + (hf * NG + gi)
                g0 = gi * GT
                prev = run4[:, (gi - 1) % GT, GT - 1, :]
                pe.wait_ge(s_t, G + 1)
                pe.matmul(bank[3][:, 0:GT * NT], ident[:, :], every(prev, GT), start=True, stop=False, skip_group_check=True)
                for t in range(GT):
                    ins = pe.matmul(bank[3][:, t * NT:GT * NT], ol[:, hf, g0 + t, :], every(oh[:, hf, g0 + t, :], GT - t),
                                    start=False, stop=t == GT - 1, skip_group_check=True)
                ins.then_inc(s_r, 1)
                pe.wait_ge(s_ol, G + 2)
                transposes(hf if gi < NG - 1 else 1 - hf, (gi + 1) % NG, (gi + 1) % 2)
                if not (isinstance(i, int) and G == 0):
                    places(G, hf if gi else 1 - hf, (gi - 1) % NG)
                pe.wait_ge(s_olt, G + 1)
                for t in range(GT):
                    ins = pe.matmul(bank[2][:, t * P:(t + 1) * P], oltb[:, gi % 2, t, :], oltb[:, gi % 2, t, :], start=True, stop=True)
                ins.then_inc(s_eq, 1)

            def places(G, hf, gi):
                g0 = gi * GT
                prev = run4[:, (gi - 1) % GT, GT - 1, :]
                pe.wait_ge(s_u, G + 1)
                pe.wait_ge(s_gm, G)
                for t in range(GT):
                    tb = prev if t == 0 else run4[:, gi, t - 1, :]
                    pe.matmul(bank[4][:, t * NT:(t + 1) * NT], olt[:, gi % 2, t, :], tb, start=True, stop=False, skip_group_check=True)
                    ins = pe.matmul(bank[4][:, t * NT:(t + 1) * NT], ub[:, t, :], oh[:, hf, g0 + t, :], start=False, stop=True,
                                    skip_group_check=True)
                ins.then_inc(s_g, 1)

            def node_rows(n):
                pe.wait_ge(s_x3c, n + 1)
                for k in range(KD):
                    ins = pe.matmul(bank[7][:, 0:W], xt[:, k, :], wg[:, k, :], start=k == 0, stop=k == KD - 1)
                ins.then_inc(s_tabp, 1)

            def node(n, hf, gi, turn):
                if gi == 0:
                    pe.wait_ge(s_xin[hf], (turn + 1) * 16)
                    pe.wait_ge(s_tt, n + 1)
                    pe.wait_ge(s_x3, n + 1)
                    pe.matmul(bank[5][:, 0:D], ident[:, :], xin[:, hf, :], start=True, stop=False, skip_group_check=True)
                    for m in range(KD):
                        ins = pe.matmul(bank[5][:, m * P:(m + 1) * P], tt[:, m, :], ident[:, :], start=False,
                                        stop=m == KD - 1, skip_group_check=True)
                    ins.then_inc(s_px, 1)
                    if not (isinstance(n, int) and n == 0):
                        node_rows(n - 1)
                if gi == 3:
                    pe.wait_ge(s_x3, n + 2)
                    for m in range(KD):
                        ins = pe.transpose(bank[6][:, m * P:(m + 1) * P], x3[:, hf, m * P:(m + 1) * P], ident[:, :])
                    ins.then_inc(s_x3t, 1)

            pe.wait_ge(s_t0, 1)
            pe.wait_ge(s_ol, 1)
            transposes(0, 0, 0)
            def turn(i, extra):
                for hf in range(2):
                    for gi in range(NG):
                        if extra == "nodes":
                            node(i * 2 + (hf - 2 * N0), hf, gi, i - N0)
                        if extra == "last" and hf == 0:
                            node(NT - 1, hf, gi, i - N0)
                        if extra == "last" and hf == 1 and gi == 0:
                            pe.wait_ge(s_tab, NT - 1)
                            node_rows(NT - 1)
                        rank(i, hf, gi)
                        if extra == "gnn" and gi % 2:
                            gnn_block(i * 4 + (2 * hf + gi // 2))
                        if extra == "bn" and hf == 0 and gi == 1:
                            gnn_block(CB - 1, NP - (CB - 1) * 512)

            turn(0, "gnn")
            with pe.Fori(1, CT) as i:
                turn(i, "gnn")
            turn(CT, "bn")
            turn(CT + 1, "tanh")
            turn(N0, "nodes")
            with pe.Fori(N0 + 1, N1) as i:
                turn(i, "nodes")
            turn(N1, "last")
            with pe.Fori(N1 + 1, RT) as i:
                turn(i, "")
            pe.wait_ge(s_t, RT * 2 * NG + 1)
            places(RT * 2 * NG, 1, NG - 1)

            pe.wait_ge(s_wexp, 16 * (2 * NE + 1))
            pe.wait_ge(s_olt, RT * 2 * NG + 1)
            pe.wait_ge(s_gm, RT * 2 * NG + 1)
            pe.wait_ge(s_x3c, NT)
            def up(i, e, m, T):
                pe.wait_ge(s_hh, i * (NE * MF) + (e * MF + m + 1))
                for k in range(KD):
                    ins = pe.matmul(bank[m][:, 0:T], w1s[:, e, k, m * P:(m + 1) * P], x3T[:, k, bass.ds(i * TB, T)],
                                    start=k == 0, stop=k == KD - 1)
                ins.then_inc(s_up, 1)

            def down(i, e, halves=2):
                pe.wait_ge(s_hh, i * (NE * MF) + ((e + 2) * MF))
                for a in range(halves):
                    pe.wait_ge(s_yo, i * (2 * NE) + (halves * e + a + 3 - halves))
                    for k in range(MF):
                        pe.matmul(bank[4 + a][:, 0:D], hh[:, k, a * P:(a + 1) * P], w2s[:, e, k, :], start=k == 0, stop=False)
                    ins = pe.matmul(bank[4 + a][:, 0:D], ones[0:1, 0:P], b2s[0:1, e, :], start=False, stop=True)
                    ins.then_inc(s_dn, 1)

            def experts(i, halves=2):
                T = halves * P
                for e in range(NE):
                    up(i, e, 0, T)
                    up(i, e, 1, T)
                    if e:
                        down(i, e - 1, halves)
                    elif not (isinstance(i, int) and i == 0):
                        down(i - 1, NE - 1)
                    up(i, e, 2, T)
                    up(i, e, 3, T)

            experts(0)
            with pe.Fori(1, FT) as i:
                experts(i)
            experts(FT, 1)
            down(FT, NE - 1, 1)
            pe.wait_ge(s_cin, 1)
            for q in range(4):
                ins = pe.transpose(bank[0][0:LF, q * P:(q + 1) * P], cin[:, q, :], ident[:, :])
            ins.then_inc(s_ctr, 1)
            pe.wait_ge(s_cb, 1)
            pe.transpose(bank[1][:, 0:LF], crow[:, 0, 0:P], ident[0:LF, 0:LF])
            pe.transpose(bank[1][:, LF:2 * LF], crow[:, 7, 0:P], ident[0:LF, 0:LF]).then_inc(s_cbt, 1)
            for n in range(1, NT, 2):
                j, b = n // 2, n % YR
                pe.wait_ge(s_diag, j + 1)
                pe.wait_ge(s_yl[b], 32 * (n // YR + 1))
                if j >= 2:
                    pe.wait_ge(s_cmbp, j - 1)
                pe.matmul(bank[2 + j % 2][:, 0:D], ident[:, :], ring(b)[:, NE, :], start=True, stop=False)
                for e in range(NE):
                    ins = pe.matmul(bank[2 + j % 2][:, 0:D], diag[:, j % 2, e, :], ring(b)[:, e, :], start=False, stop=e == NE - 1)
                ins.then_inc(s_sum, 1)


_INS = ["x", "src", "dst", "edge_weight", "L0_gnn_weight", "L0_gnn_gamma", "L0_gnn_beta", "L0_ffn_W_gat",
        "L0_ffn_att_src", "L0_ffn_att_dst", "L0_ffn_b_gat", "L0_ffn_ln_gamma", "L0_ffn_ln_beta", "L0_ffn_W1",
        "L0_ffn_b1", "L0_ffn_W2", "L0_ffn_b2", "L0_ffn_edge_index"]


def kernel(**inputs):
    import numpy as _np
    import concourse.bacc as _bacc
    from concourse import mybir as _mybir
    from concourse.bass_utils import run_bass_kernel_spmd as _run

    nc = _bacc.Bacc("TRN2", target_bir_lowering=False, num_devices=1)
    arrays, args = {}, []
    for name in _INS:
        a = _np.ascontiguousarray(inputs[name])
        arrays[f"in_{name}_dram"] = a
        args.append(nc.dram_tensor(f"in_{name}_dram", a.shape, _mybir.dt.from_np(a.dtype), kind="ExternalInput").ap())
    shape = inputs["x"].shape
    args.append(nc.dram_tensor("out_0_dram", shape, _mybir.dt.float32, kind="ExternalOutput").ap())
    gnn_moe(nc, *args)
    r = _run(nc, [arrays], core_ids=[0])
    return r.results[0]["out_0_dram"]
```
